# Optimizing a Trainium2 kernel written in Bass

```python
import numpy as np
import jax
import jax.numpy as jnp

def _softmax(x, axis=-1):
    return jax.nn.softmax(x, axis=axis)

def _gelu(x):
    return jax.nn.gelu(x, approximate=True)

def _silu(x):
    return jax.nn.silu(x)

def _sigmoid(x):
    return jax.nn.sigmoid(x)

def _layernorm(x, axis=-1, eps=1e-05):
    m = jnp.mean(x, axis=axis, keepdims=True)
    v = jnp.var(x, axis=axis, keepdims=True)
    return (x - m) / jnp.sqrt(v + eps)

def _scatter_add(tgt, idx, src, axis=0):
    return tgt.at[idx].add(src)

def _segment_sum(src, seg, n):
    return jax.ops.segment_sum(src, seg, n)
kernel_name = 'mk_perceiver_d1_seqx_r2_c810ee'

def setup_inputs(seed: int=0):
    np.random.seed(seed)
    _w = jnp.asarray

    def _rec_inputs():
        import jax
        import jax.numpy as jnp
        _rk = jax.random.key(seed)
        x = 7.22e-05 + 1 * jax.random.normal(jax.random.fold_in(_rk, 1), (32, 64, 512), jnp.float32)
        _lenS = 64 - jax.random.randint(jax.random.fold_in(_rk, 7), (32,), 0, max(1, 64 // 4) + 1, jnp.int32)
        _lenS2 = 1601 - jax.random.randint(jax.random.fold_in(_rk, 8), (32,), 0, max(1, 1601 // 4) + 1, jnp.int32)
        _ctx_1024P = jax.random.normal(jax.random.fold_in(_rk, 11), (32, 16, 512), jnp.float32)
        _ctx_1024c = jax.random.dirichlet(jax.random.fold_in(_rk, 511), 0.3 * jnp.ones((16,), jnp.float32), (32, 1601))
        _ctx_1024t = jnp.einsum('bsk,bkd->bsd', _ctx_1024c, _ctx_1024P)
        _ctx_1024t = _ctx_1024t * jax.lax.rsqrt(jnp.mean(jnp.square(_ctx_1024t)) + 1e-12) * 0.953939
        ctx_1024 = -0.000514642 + 1.00011 * (_ctx_1024t + 0.3 * jax.random.normal(jax.random.fold_in(_rk, 611), (32, 1601, 512), jnp.float32))
        return (x, ctx_1024)
    x, ctx_1024 = _rec_inputs()

    def _L0_xattn_setup():
        import jax, jax.numpy as jnp
        import numpy as np
        B, L_ENC, L_DEC, D = (16, 256, 128, 512)
        key = jax.random.key(seed)
        k1, k2, k3, k4, k5, k6 = jax.random.split(key, 6)
        encoder_hc = jax.random.normal(k1, (B, L_ENC, D), dtype=jnp.float32)
        decoder_hq = jax.random.normal(k2, (B, L_DEC, D), dtype=jnp.float32)
        w_sim = jax.random.normal(k3, (3 * D,), dtype=jnp.float32) * 0.02
        b_sim = jax.random.normal(k4, (1,), dtype=jnp.float32) * 0.02
        W_qv = jax.random.normal(k5, (4 * D, D), dtype=jnp.float32) * 0.02
        b_qv = jax.random.normal(k6, (D,), dtype=jnp.float32) * 0.02
        return {'encoder_hc': encoder_hc, 'decoder_hq': decoder_hq, 'w_sim': w_sim, 'b_sim': b_sim, 'W_qv': W_qv, 'b_qv': b_qv}
    _L0_xattn_all = _L0_xattn_setup()
    _L0_xattn_in = {k: v for k, v in _L0_xattn_all.items() if k in ('w_sim', 'b_sim', 'W_qv', 'b_qv')}
    del _L0_xattn_all

    def _L0_attn_setup():
        import jax, jax.numpy as jnp
        import numpy as np
        B, L, D = (8, 2048, 512)
        EPS = 1e-05
        key = jax.random.key(seed)
        ks = jax.random.split(key, 8)
        s = 0.02
        return {'x': jax.random.normal(ks[0], (B, L, D), dtype=jnp.float32), 'decay': jnp.full((D,), 0.9, dtype=jnp.float32), 'Wr': jax.random.normal(ks[1], (D, D), dtype=jnp.float32) * s, 'br': jnp.zeros((D,), dtype=jnp.float32), 'Wg': jax.random.normal(ks[2], (D, D), dtype=jnp.float32) * s, 'bg': jnp.zeros((D,), dtype=jnp.float32), 'Wo': jax.random.normal(ks[3], (D, D), dtype=jnp.float32) * s, 'bo': jnp.zeros((D,), dtype=jnp.float32), 'ln_w': jnp.ones((D,), dtype=jnp.float32), 'ln_b': jnp.zeros((D,), dtype=jnp.float32)}
    _L0_attn_all = _L0_attn_setup()
    _L0_attn_in = {k: v for k, v in _L0_attn_all.items() if k in ('decay', 'Wr', 'br', 'Wg', 'bg', 'Wo', 'bo', 'ln_w', 'ln_b')}
    del _L0_attn_all

    def _L0_ffn_setup():
        import jax, jax.numpy as jnp
        import numpy as np
        EPS = 1e-09
        key = jax.random.key(seed)
        k1, k2, k3, k4 = jax.random.split(key, 4)
        B, T, H, D, E = (2, 1024, 512, 512, 8)
        x = jax.random.normal(k1, (B, T, H), dtype=jnp.float32)
        gate_w = jax.random.normal(k2, (E, H), dtype=jnp.float32) * 0.02
        gate_up_proj = jax.random.normal(k3, (E, H, 2 * D), dtype=jnp.float32) * 0.02
        down_proj = jax.random.normal(k4, (E, D, H), dtype=jnp.float32) * 0.02
        return {'x': x, 'gate_w': gate_w, 'gate_up_proj': gate_up_proj, 'down_proj': down_proj}
    _L0_ffn_all = _L0_ffn_setup()
    _L0_ffn_in = {k: v for k, v in _L0_ffn_all.items() if k in ('gate_w', 'gate_up_proj', 'down_proj')}
    del _L0_ffn_all
    return {'x': x, 'ctx_1024': ctx_1024, 'L0_xattn_w_sim': _L0_xattn_in['w_sim'], 'L0_xattn_b_sim': _L0_xattn_in['b_sim'], 'L0_xattn_W_qv': _L0_xattn_in['W_qv'], 'L0_xattn_b_qv': _L0_xattn_in['b_qv'], 'L0_attn_decay': _L0_attn_in['decay'], 'L0_attn_Wr': _L0_attn_in['Wr'], 'L0_attn_br': _L0_attn_in['br'], 'L0_attn_Wg': _L0_attn_in['Wg'], 'L0_attn_bg': _L0_attn_in['bg'], 'L0_attn_Wo': _L0_attn_in['Wo'], 'L0_attn_bo': _L0_attn_in['bo'], 'L0_attn_ln_w': _L0_attn_in['ln_w'], 'L0_attn_ln_b': _L0_attn_in['ln_b'], 'L0_ffn_gate_w': _L0_ffn_in['gate_w'], 'L0_ffn_gate_up_proj': _L0_ffn_in['gate_up_proj'], 'L0_ffn_down_proj': _L0_ffn_in['down_proj']}

def reference(x, ctx_1024, L0_xattn_w_sim, L0_xattn_b_sim, L0_xattn_W_qv, L0_xattn_b_qv, L0_attn_decay, L0_attn_Wr, L0_attn_br, L0_attn_Wg, L0_attn_bg, L0_attn_Wo, L0_attn_bo, L0_attn_ln_w, L0_attn_ln_b, L0_ffn_gate_w, L0_ffn_gate_up_proj, L0_ffn_down_proj):
    import jax
    import jax.numpy as jnp

    def _L0_xattn_ref(encoder_hc, decoder_hq, w_sim, b_sim, W_qv, b_qv):
        import jax, jax.numpy as jnp
        import numpy as np
        B, L_ENC, L_DEC, D = (16, 256, 128, 512)
        d = encoder_hc.shape[-1]
        w1, w2, w3 = (w_sim[:d], w_sim[d:2 * d], w_sim[2 * d:])
        Sim = (encoder_hc @ w1)[:, :, None] + (decoder_hq @ w2)[:, None, :] + jnp.einsum('bid,bjd->bij', encoder_hc * w3, decoder_hq) + b_sim[0]
        A = jax.nn.softmax(Sim, axis=2)
        hq_hat = jnp.einsum('bij,bjd->bid', A, decoder_hq)
        Batt = jax.nn.softmax(jnp.max(Sim, axis=2), axis=1)
        hc_bar = jnp.einsum('bi,bid->bd', Batt, encoder_hc)[:, None, :]
        hc_hat = jnp.broadcast_to(hc_bar, encoder_hc.shape)
        feats = jnp.concatenate([encoder_hc, hq_hat, encoder_hc * hq_hat, encoder_hc * hc_hat], axis=-1)
        hcq = feats @ W_qv + b_qv
        return hcq

    def _L0_attn_ref(x, decay, Wr, br, Wg, bg, Wo, bo, ln_w, ln_b):
        import jax, jax.numpy as jnp
        import numpy as np
        B, L, D = (8, 2048, 512)
        EPS = 1e-05
        b, l, d = x.shape
        decay_factor = jax.nn.sigmoid(decay)
        one_minus = 1.0 - decay_factor
        z = jax.nn.sigmoid(jnp.einsum('bld,ed->ble', x, Wg) + bg)
        x_t_first = jnp.moveaxis(x, 1, 0)
        z_t_first = jnp.moveaxis(z, 1, 0)

        def step(h, inp):
            x_t, z_t = inp
            pred_x = h @ Wr.T + br
            error = x_t - pred_x
            h_new = decay_factor * h + one_minus * (z_t * error)
            return (h_new, h_new)
        h0 = jnp.zeros((b, d), dtype=x.dtype)
        _, ys = jax.lax.scan(step, h0, (x_t_first, z_t_first))
        y = jnp.moveaxis(ys, 0, 1)
        mean = jnp.mean(y, axis=-1, keepdims=True)
        var = jnp.mean(jnp.square(y - mean), axis=-1, keepdims=True)
        y = (y - mean) * jax.lax.rsqrt(var + EPS) * ln_w + ln_b
        return jnp.einsum('bld,ed->ble', y, Wo) + bo

    def _L0_ffn_ref(x, gate_w, gate_up_proj, down_proj):
        import jax, jax.numpy as jnp
        import numpy as np
        EPS = 1e-09
        B, T, H = x.shape
        E = gate_w.shape[0]
        top_k = 2
        hidden = x.reshape(-1, H)
        router_logits = hidden @ gate_w.T
        routing_weights = jax.nn.softmax(router_logits.astype(jnp.float32), axis=-1)
        topk_weights, topk_indices = jax.lax.top_k(routing_weights, top_k)
        topk_weights = topk_weights / (jnp.sum(topk_weights, axis=-1, keepdims=True) + EPS)
        N = hidden.shape[0]
        routed = jnp.zeros((N, E), dtype=router_logits.dtype)
        rows = jnp.arange(N)[:, None]
        routed = routed.at[rows, topk_indices].set(topk_weights.astype(router_logits.dtype))
        routed = routed / (jnp.sum(routed, axis=-1, keepdims=True) + EPS)
        routed = routed.astype(hidden.dtype)
        gate_up = jnp.einsum('th,ehq->teq', hidden, gate_up_proj)
        gate, up = jnp.split(gate_up, 2, axis=-1)
        expert_outputs = jnp.einsum('teq,eqh->teh', jax.nn.silu(gate) * up, down_proj)
        out = jnp.sum(expert_outputs * routed[:, :, None], axis=1)
        return out.reshape(B, T, H)
    x = x + _L0_xattn_ref(_layernorm(x, axis=-1), ctx_1024, L0_xattn_w_sim, L0_xattn_b_sim, L0_xattn_W_qv, L0_xattn_b_qv)
    x = x + _L0_attn_ref(_layernorm(x, axis=-1), L0_attn_decay, L0_attn_Wr, L0_attn_br, L0_attn_Wg, L0_attn_bg, L0_attn_Wo, L0_attn_bo, L0_attn_ln_w, L0_attn_ln_b)
    x = x + _L0_ffn_ref(_layernorm(x, axis=-1), L0_ffn_gate_w, L0_ffn_gate_up_proj, L0_ffn_down_proj)
    return x

_drawn_inputs = setup_inputs


def setup_inputs(seed=0):
    import zlib

    import numpy as np

    out = dict(_drawn_inputs(seed))
    spreads = {'L0_attn_decay': (0.8999999761581421, 0.2),
     'L0_attn_br': (0.0, 0.1),
     'L0_attn_bg': (0.0, 0.437),
     'L0_attn_bo': (0.0, 0.1),
     'L0_attn_ln_w': (1.0, 0.2),
     'L0_attn_ln_b': (0.0, 0.1)}
    factors = {}
    for name, (base, spread) in spreads.items():
        noise = np.random.default_rng([zlib.crc32(name.encode()), seed]).standard_normal(out[name].shape)
        drawn = base * np.exp(spread * noise) if base else spread * noise
        out[name] = jnp.asarray(drawn.astype(out[name].dtype))
    for name, factor in factors.items():
        out[name] = (out[name] * factor).astype(out[name].dtype)
    return out
```

```python
from contextlib import ExitStack

import concourse.bass as bass
from concourse import mybir

F32 = mybir.dt.float32
I32 = mybir.dt.int32
U32 = mybir.dt.uint32
ALU = mybir.AluOpType
ACT = mybir.ActivationFunctionType
AX = mybir.AxisListType

P = 128
LN_EPS = 1e-5


class Shapes:

    def __init__(self, x, ctx, gate_w):
        self.B, self.L, self.D = x.shape
        self.J = ctx.shape[1]
        self.E = gate_w.shape[0]
        self.N = self.B * self.L
        self.C = self.D // P
        self.PAIRS = self.N // P
        self.JT = -(-self.J // P)
        self.JMAIN = (self.JT - 1) * P
        self.JTAIL = self.J - self.JMAIN
        assert P == 2 * self.L and self.D == 4 * P and self.B == 32 and self.JT == 13


def bcast_row(vec):
    return vec.rearrange("(o d) -> o d", o=1).to_broadcast([P, vec.shape[0]])


BLOCKS = [(0, 3, 0, 0), (3, 3, 1, 0), (6, 3, 2, 0), (9, 2, 3, 0), (11, 2, 3, 256)]
NBLK = len(BLOCKS)
BANK_TILES = [(0, 3), (3, 3), (6, 3), (9, 4)]
AT_TILES = [(0, 4), (4, 3), (7, 3), (10, 3)]


def turn_order(front, back):
    bank = ([], [])
    for j, (_, n, _, _) in enumerate(BLOCKS):
        for u in range(2 * n if front else 0):
            bank[u % 2].append(f"ctx{j}.{u}")
    if front:
        bank[0].insert(1, "hc")
    if back:
        bank[1].insert(1 if front else 0, "trow")
        bank[0].append("hqh")
        bank[1].append("brow")
    for q in range(len(AT_TILES) if front else 0):
        bank[q % 2].append(f"probs{q}")
    return bank


FIRST_TURNS = turn_order(True, False)
FULL_TURNS = turn_order(True, True)
LAST_TURNS = turn_order(False, True)


def turn(bank, name, p, step):
    if step == "first":
        return FIRST_TURNS[bank].index(name)
    order = LAST_TURNS if step == "last" else FULL_TURNS
    return len(FIRST_TURNS[bank]) + p * len(FULL_TURNS[bank]) + order[bank].index(name)


def before(p):
    return p - 1, "first" if isinstance(p, int) and p == 0 else "full"


def later(p, n):
    return not isinstance(p, int) or p >= n


def cross_attention(nc, sh, ident, x, ctx, w_sim, b_sim, W_qv, b_qv, x1):
    D, C, JT, JMAIN, JTAIL, PAIRS = sh.D, sh.C, sh.JT, sh.JMAIN, sh.JTAIL, sh.PAIRS
    BW = 3 * P

    with ExitStack() as stack:
        def sb(name, shape, dt=F32):
            return stack.enter_context(nc.sbuf_tensor(name, shape, dt))

        def sem(name):
            return stack.enter_context(nc.semaphore(name))

        ctx_sb = [[sb(f"ctx_sb{s}{b}", [P, JT, D]) for b in range(2)] for s in range(2)]
        ctxT = [sb(f"ctxT{s}", [P, 2, C, BW]) for s in range(2)]
        wqv = sb("wqv", [P, 4 * C, D])
        x_sb = sb("x_sb", [P, D])
        xb = [sb(f"xb{s}", [P, D]) for s in range(2)]
        hc = sb("hc", [P, D])
        hcT = [sb(f"hcT{s}", [P, C, P]) for s in range(2)]
        qT = sb("qT", [P, C, P])
        probs = sb("probs", [P, JT * P])
        probsT = sb("probsT", [P, JT, P])
        hqh = sb("hqh", [P, D])
        hqhT = sb("hqhT", [P, C, P])
        f2 = sb("f2", [P, C, P])
        f3 = sb("f3", [P, C, P])
        w1_b = sb("w1_b", [P, D])
        bqv_b = sb("bqv_b", [P, D])
        s1_prod = sb("s1_prod", [P, D])
        w2T = sb("w2T", [P, C])
        w3T = sb("w3T", [P, C])
        bsim_b = sb("bsim_b", [P, 1])
        stats = sb("stats", [P, 6])
        mv = sb("mv", [P, 2])
        ve = sb("ve", [P, 1])
        nmean = sb("nmean", [P, 1])
        rstd = sb("rstd", [P, 1])
        mhalf = sb("mhalf", [P, 1])
        s1 = sb("s1", [P, 1])
        mx4 = sb("mx4", [P, 4])
        mx = sb("mx", [P, 1])
        nmx = sb("nmx", [P, 1])
        z4 = sb("z4", [P, 4])
        zsum = sb("zsum", [P, 1])
        rz = sb("rz", [P, 1])
        tcol = sb("tcol", [P, 1])
        nrm = sb("nrm", [1, 2])
        rsub = sb("rsub", [1, P])
        erow = sb("erow", [1, P])
        rsum = sb("rsum", [1, 2])
        rinv = sb("rinv", [1, 2])
        brow = sb("brow", [1, P])
        ones1 = sb("ones1", [1, P])
        hcb = sb("hcb", [P, C, 2])

        S = stack.enter_context(nc.psum_tensor("S", [P, 4, 512], F32))
        T = [stack.enter_context(nc.psum_tensor(f"T{s}", [P, 512], F32)) for s in range(2)]
        O = stack.enter_context(nc.psum_tensor("O", [P, 512], F32))
        Y = stack.enter_context(nc.psum_tensor("Y", [P, 512], F32))

        const_in = sem("const_in")
        wqv_in = sem("wqv_in")
        x_in = sem("x_in")
        ctx_in = [[sem(f"ctx_in{s}_{j}") for j in range(NBLK)] for s in range(2)]
        x1_out = sem("x1_out")
        consts = sem("consts")
        stat_done = sem("stat_done")
        ln_ready = sem("ln_ready")
        rstd_ready = sem("rstd_ready")
        hc_ready = sem("hc_ready")
        xb_ready = sem("xb_ready")
        q_ready = sem("q_ready")
        s1_ready = sem("s1_ready")
        t_full = [sem(f"t_full{s}") for s in range(2)]
        t_free = [sem(f"t_free{s}") for s in range(2)]
        qk_done = sem("qk_done")
        mx_done = sem("mx_done")
        nmx_ready = sem("nmx_ready")
        tcol_ready = sem("tcol_ready")
        exp_done = sem("exp_done")
        z_done = sem("z_done")
        rz_ready = sem("rz_ready")
        nrm_done = sem("nrm_done")
        erow_ready = sem("erow_ready")
        bsm_done = sem("bsm_done")
        brow_ready = sem("brow_ready")
        hcb_done = sem("hcb_done")
        f2_ready = sem("f2_ready")
        f3_ready = sem("f3_ready")
        av_done = sem("av_done")
        hqh_ready = sem("hqh_ready")
        y_done = sem("y_done")
        x1_ready = sem("x1_ready")

        def tile_rows(t):
            return P if t < JT - 1 else JTAIL

        def bank_cols(k):
            t0, n = BANK_TILES[k]
            return sum(tile_rows(t) for t in range(t0, t0 + n))

        def block_dmas(j):
            t0, n, _, _ = BLOCKS[j]
            return 2 * (2 if t0 + n == JT else 1)

        def block_cols(j):
            t0, n, _, _ = BLOCKS[j]
            return sum(tile_rows(t) for t in range(t0, t0 + n))

        def steps(eng, body):
            body(-1, 0, "first")
            body(0, 0, "full")
            with eng.Fori(0, (PAIRS - 2) // 2) as i:
                body(2 * i + 1, 1, "full")
                body(2 * i + 2, 0, "full")
            body(PAIRS - 1, 1, "last")

        block = stack.enter_context(nc.Block())

        @block.sync
        def _(sp):
            def load_x(row):
                sp.dma_start(x_sb[:], x[row]).then_inc(x_in, 16)

            def load_ctx(s, pair):
                for j, (t0, n, _, _) in enumerate(BLOCKS):
                    for b in range(2):
                        src = ctx[pair, b]
                        full = min(n, JT - 1 - t0)
                        sp.dma_start(ctx_sb[s][b][:, t0:t0 + full, :],
                                     src[0:JMAIN, :].rearrange("(p t) d -> p t d", t=JT - 1)[:, t0:t0 + full, :]
                                     ).then_inc(ctx_in[s][j], 16)
                        if full < n:
                            sp.dma_start(ctx_sb[s][b][0:JTAIL, JT - 1, :], src[JMAIN:sh.J, :]).then_inc(ctx_in[s][j], 16)

            load_x(0)
            sp.dma_start(w1_b[:], bcast_row(w_sim[0:D])).then_inc(const_in, 16)
            with nc.allow_non_contiguous_dma(reason="two small weight vectors, a column for each chunk"):
                sp.dma_start(w2T[:], w_sim[D:2 * D].rearrange("(c p) -> p c", p=P)).then_inc(const_in, 16)
                sp.dma_start(w3T[:], w_sim[2 * D:3 * D].rearrange("(c p) -> p c", p=P)).then_inc(const_in, 16)
            sp.dma_start(bsim_b[:], bcast_row(b_sim)).then_inc(const_in, 16)
            sp.dma_start(bqv_b[:], bcast_row(b_qv)).then_inc(const_in, 16)
            load_ctx(0, 0)
            sp.wait_ge(hc_ready, 1)
            sp.wait_ge(xb_ready, 1)
            load_x(1)
            sp.dma_start(wqv[:], W_qv.rearrange("(k p) e -> p k e", p=P)).then_inc(wqv_in, 16)
            load_ctx(1, 1)

            def step(p, s, load, store):
                nxt = p + 2
                if load:
                    rows = nxt if isinstance(nxt, int) else sp.snap(nxt)
                if store:
                    prev = p - 1 if isinstance(p, int) else sp.snap(p - 1)
                    sp.wait_ge(x1_ready, p)
                    sp.dma_start(x1[prev], xb[1 - s][:]).then_inc(x1_out, 16)
                if load:
                    sp.wait_ge(hc_ready, p + 2)
                    sp.wait_ge(xb_ready, p + 2)
                    load_x(rows)
                    sp.wait_ge(av_done, p + 1)
                    load_ctx(s, rows)

            step(0, 0, True, False)
            with sp.Fori(0, (PAIRS - 4) // 2) as i:
                step(2 * i + 1, 1, True, True)
                step(2 * i + 2, 0, True, True)
            step(PAIRS - 3, 1, True, True)
            step(PAIRS - 2, 0, False, True)
            step(PAIRS - 1, 1, False, True)
            step(PAIRS, 0, False, True)
            sp.wait_ge(x1_out, 16 * PAIRS)

        @block.gpsimd
        def _(pool):
            pool.memset(mhalf[:], -0.5).then_inc(consts, 1)
            pool.memset(ones1[:], 1.0).then_inc(consts, 1)
            pool.wait_ge(consts, 2)
            pool.wait_ge(const_in, 80)

            def body(p, s, step):
                if step != "last":
                    f = p + 1
                    pool.wait_ge(ln_ready, 2 * f + 2)
                    pool.tensor_tensor(rstd[:], ve[:], mhalf[:], ALU.pow).then_inc(rstd_ready, 1)
                    if not (isinstance(f, int) and f < 2):
                        pool.wait_ge(x1_out, 16 * (f - 1))
                    pool.tensor_tensor(xb[1 - s if step != "first" else 0][:], x_sb[:], bqv_b[:], ALU.add).then_inc(xb_ready, 1)
                if step != "first":
                    pool.wait_ge(t_free[0], turn(0, "hqh", p, step) + 1)
                    pool.wait_ge(y_done, p)
                    pool.tensor_tensor(f2[:], hcT[s][:], hqhT[:], ALU.mult).then_inc(f2_ready, 1)

            steps(pool, body)

        @block.tensor
        def _(pe):
            def fill(bank, name, p, step):
                pe.wait_ge(t_free[bank], turn(bank, name, p, step))

            def turn_ctx(j, u, p, fs, loads, step):
                t0, n, _, _ = BLOCKS[j]
                t, b, bank = t0 + u // 2, u % 2, u % 2
                rows = tile_rows(t)
                if u == 0:
                    pe.wait_ge(ctx_in[fs][j], block_dmas(j) * 16 * loads)
                fill(bank, f"ctx{j}.{u}", p, step)
                for c in range(C):
                    last = pe.transpose(T[bank][:, c * P:c * P + rows], ctx_sb[fs][b][0:rows, t, c * P:(c + 1) * P],
                                        ident[0:rows, 0:rows])
                last.then_inc(t_full[bank], 1)

            def turn_tile(bank, name, src, p, step):
                fill(bank, name, p, step)
                for c in range(C):
                    last = pe.transpose(T[bank][:, c * P:(c + 1) * P], src[:, c * P:(c + 1) * P], ident[:])
                last.then_inc(t_full[bank], 1)

            def turn_probs(q, p, step):
                t0, n = AT_TILES[q]
                if q == 0:
                    pe.wait_ge(exp_done, 4 * (p + 2))
                fill(q % 2, f"probs{q}", p, step)
                for i in range(n):
                    rows = tile_rows(t0 + i)
                    last = pe.transpose(T[q % 2][0:rows, i * P:(i + 1) * P],
                                        probs[:, (t0 + i) * P:(t0 + i) * P + rows], ident[:])
                last.then_inc(t_full[q % 2], 1)

            def scores(j, p, f, fs, loads, step):
                t0, n, k, col = BLOCKS[j]
                w = block_cols(j)
                buf = ctxT[(j + fs) % 2]
                for bank in range(2):
                    pe.wait_ge(t_free[bank], turn(bank, f"ctx{j}.{2 * n - 2 + bank}", p, step) + 1)
                if j == 0:
                    pe.wait_ge(q_ready, C * (f + 1))
                    pe.wait_ge(exp_done, 4 * f)
                for c in range(C):
                    if j + 1 < NBLK and c < BLOCKS[j + 1][1]:
                        turn_ctx(j + 1, 2 * c, p, fs, loads, step)
                        turn_ctx(j + 1, 2 * c + 1, p, fs, loads, step)
                    for b in range(2):
                        last = pe.matmul(S[64 * b:64 * b + 64, k, col:col + w], qT[:, c, 64 * b:64 * b + 64],
                                         buf[:, b, c, 0:w], start=(c == 0), stop=(c == C - 1))
                last.then_inc(qk_done, 1)

            def body(p, s, step, loads):
                front, back = step != "last", step != "first"
                f, fs = p + 1, (1 - s) if back else 0
                if back:
                    for bank in range(2):
                        pe.wait_ge(t_free[bank], turn(bank, f"probs{2 + bank}", *before(p)) + 1)
                    pe.wait_ge(hqh_ready, p)
                for t in range(JT):
                    if t == 1:
                        if front:
                            pe.wait_ge(hc_ready, f + 1)
                            turn_tile(0, "hc", hc, p, step)
                        if back:
                            pe.wait_ge(tcol_ready, p + 1)
                            fill(1, "trow", p, step)
                            pe.transpose(T[1][0:1, 0:P], tcol[:], ident[:]).then_inc(t_full[1], 1)
                    elif front and t in (0, 2, 3):
                        u = 2 * max(t - 1, 0)
                        turn_ctx(0, u, p, fs, loads, step)
                        turn_ctx(0, u + 1, p, fs, loads, step)
                    for b in range(2 if back else 0):
                        rows = tile_rows(t)
                        last = pe.matmul(O[64 * b:64 * b + 64, :], probsT[0:rows, t, 64 * b:64 * b + 64],
                                         ctx_sb[s][b][0:rows, t, :], start=(t == 0), stop=(t == JT - 1))
                if back:
                    last.then_inc(av_done, 1)
                if front:
                    for j in range(NBLK - 1):
                        scores(j, p, f, fs, loads, step)
                if back:
                    pe.wait_ge(hqh_ready, p + 1)
                    turn_tile(0, "hqh", hqh, p, step)
                    fill(1, "brow", p, step)
                    pe.wait_ge(brow_ready, p + 1)
                    pe.matmul(T[1][:, 0:P], ones1[:], brow[:], start=True, stop=True).then_inc(t_full[1], 1)
                if front:
                    scores(NBLK - 1, p, f, fs, loads, step)
                if back:
                    pe.wait_ge(wqv_in, 16)
                    pe.wait_ge(x1_ready, p)
                    for k, feat in enumerate((hcT[s], hqhT, f2, f3)):
                        if k == 1:
                            pe.wait_ge(t_free[0], turn(0, "hqh", p, step) + 1)
                        if k == 2:
                            pe.wait_ge(f2_ready, p + 1)
                        if k == 3:
                            pe.wait_ge(f3_ready, p + 1)
                        for c in range(C):
                            if front and c % 2 == 0 and k >= 2:
                                turn_probs(2 * (k - 2) + c // 2, p, step)
                            last = pe.matmul(Y[:], feat[:, c, :], wqv[:, k * C + c, :],
                                             start=(k == 0 and c == 0), stop=(k == 3 and c == C - 1))
                    last.then_inc(y_done, 1)
                elif front:
                    for q in range(len(AT_TILES)):
                        turn_probs(q, p, step)

            body(-1, 0, "first", 1)
            body(0, 0, "full", 1)
            with pe.Fori(0, (PAIRS - 2) // 2) as i:
                body(2 * i + 1, 1, "full", i + 2)
                body(2 * i + 2, 0, "full", i + 2)
            body(PAIRS - 1, 1, "last", None)

        def drain_ctx(eng, copy, bank, j, p, fs, step, only=None):
            t0, n, _, _ = BLOCKS[j]
            buf = ctxT[(j + fs) % 2]
            if not (step == "first" and j < 2):
                eng.wait_ge(qk_done, NBLK * (p + 1) + j - 1)
            for u in range(bank, 2 * n, 2) if only is None else only:
                t = t0 + u // 2
                rows, i = tile_rows(t), u // 2
                eng.wait_ge(t_full[bank], turn(bank, f"ctx{j}.{u}", p, step) + 1)
                copy(buf[:, bank, :, i * P:i * P + rows],
                     T[bank][:].rearrange("p (c j) -> p c j", c=C)[:, :, 0:rows]).then_inc(t_free[bank], 1)

        def drain_probs(eng, copy, bank, p, step):
            eng.wait_ge(av_done, p + 1)
            for q in range(bank, len(AT_TILES), 2):
                t0, n = AT_TILES[q]
                eng.wait_ge(t_full[bank], turn(bank, f"probs{q}", p, step) + 1)
                full = n if t0 + n < JT else n - 1
                last = copy(probsT[:, t0:t0 + full, :], T[bank][:, 0:full * P].rearrange("p (t i) -> p t i", i=P))
                if full < n:
                    last = copy(probsT[0:JTAIL, JT - 1, :], T[bank][0:JTAIL, full * P:n * P])
                last.then_inc(t_free[bank], 1)

        @block.scalar
        def _(act):
            copy = nc.scalar.copy

            def body(p, s, step):
                front, back = step != "last", step != "first"
                f, fs = p + 1, (1 - s) if back else 0
                if front:
                    drain_ctx(act, copy, 0, 0, p, fs, step, only=(0,))
                    act.wait_ge(t_full[0], turn(0, "hc", p, step) + 1)
                    if later(f, 2):
                        act.wait_ge(y_done, f - 1)
                    act.copy(hcT[fs][:], T[0][:].rearrange("p (c i) -> p c i", c=C)).then_inc(t_free[0], 1)
                    drain_ctx(act, copy, 0, 0, p, fs, step, only=(2, 4))
                if back:
                    act.wait_ge(t_free[1], turn(1, "trow", p, step) + 1)
                    act.wait_ge(brow_ready, p)
                    act.activation(erow[:], rsub[:], ACT.Exp).then_inc(erow_ready, 1)
                if front:
                    drain_ctx(act, copy, 0, 1, p, fs, step)
                if back:
                    act.wait_ge(av_done, p + 1)
                    act.wait_ge(rz_ready, p + 1)
                    if later(p, 1):
                        act.wait_ge(t_free[0], turn(0, "hqh", *before(p)) + 1)
                    act.activation(hqh[:], O[:], ACT.Copy, scale=rz[:, 0:1]).then_inc(hqh_ready, 1)
                if front:
                    for j in range(2, NBLK):
                        drain_ctx(act, copy, 0, j, p, fs, step)
                if back:
                    act.wait_ge(t_full[0], turn(0, "hqh", p, step) + 1)
                    act.wait_ge(y_done, p)
                    act.copy(hqhT[:], T[0][:].rearrange("p (c i) -> p c i", c=C)).then_inc(t_free[0], 1)
                if front:
                    act.wait_ge(nmx_ready, f + 1)
                    if back:
                        for bank in range(2):
                            act.wait_ge(t_free[bank], turn(bank, f"probs{2 + bank}", *before(p)) + 1)
                        act.wait_ge(rz_ready, f)
                    for k, (t0, _) in enumerate(BANK_TILES):
                        w = bank_cols(k)
                        act.activation(probs[:, t0 * P:t0 * P + w], S[:, k, 0:w], ACT.Exp, bias=nmx[:, 0:1],
                                       accum_out=z4[:, k:k + 1]).then_inc(exp_done, 1)
                    drain_probs(act, copy, 0, p, step)

            steps(act, body)

        @block.vector
        def _(dve):
            copy = nc.vector.tensor_copy
            dve.wait_ge(const_in, 80)

            def norm_stats(f):
                dve.wait_ge(x_in, 16 * f + 16)
                dve.wait_ge(hc_ready, f)
                dve.bn_stats(stats[:], x_sb[:])
                dve.drain()
                dve.bn_aggr(mv[:], stats[:]).then_inc(stat_done, 1)
                dve.wait_ge(stat_done, f + 1)
                dve.tensor_scalar(ve[:], mv[:, 1:2], LN_EPS, None, ALU.add).then_inc(ln_ready, 1)
                dve.tensor_scalar(nmean[:], mv[:, 0:1], -1.0, None, ALU.mult).then_inc(ln_ready, 1)

            def add_x(p, s):
                dve.wait_ge(y_done, p + 1)
                dve.tensor_tensor(xb[s][:], Y[:], xb[s][:], ALU.add).then_inc(x1_ready, 1)

            def body(p, s, step):
                front, back = step != "last", step != "first"
                f, fs = p + 1, (1 - s) if back else 0
                if front:
                    norm_stats(f)
                if back and later(p, 1):
                    add_x(p - 1, 1 - s)
                if front:
                    dve.wait_ge(rstd_ready, f + 1)
                    if back:
                        dve.wait_ge(t_free[0], turn(0, "hc", *before(p)) + 1)
                        dve.wait_ge(s1_ready, f)
                    dve.tensor_scalar(hc[:], x_sb[:], nmean[:, 0:1], rstd[:, 0:1], ALU.add, ALU.mult).then_inc(hc_ready, 1)
                    drain_ctx(dve, copy, 1, 0, p, fs, step, only=(1,))
                if back:
                    row = T[1][0:1, 0:P].rearrange("o (b i) -> o b i", b=2)
                    dve.wait_ge(t_full[1], turn(1, "trow", p, step) + 1)
                    dve.tensor_reduce(nrm[:], row, axis=AX.X, op=ALU.max, negate=True).then_inc(nrm_done, 1)
                    dve.wait_ge(nrm_done, p + 1)
                    dve.wait_ge(erow_ready, p)
                    dve.tensor_tensor(rsub[:].rearrange("o (b i) -> o b i", b=2), row,
                                      nrm[:, :, None].to_broadcast([1, 2, 64]), ALU.add).then_inc(t_free[1], 1)
                if front:
                    drain_ctx(dve, copy, 1, 0, p, fs, step, only=(3, 5))
                    dve.wait_ge(hc_ready, f + 1)
                    dve.wait_ge(tcol_ready, f)
                    dve.tensor_tensor_reduce(out=s1_prod[:], in0=hc[:], in1=w1_b[:], scale=1.0, scalar=0.0,
                                             op0=ALU.mult, op1=ALU.add, accum_out=s1[:]).then_inc(s1_ready, 1)
                    dve.wait_ge(t_free[0], turn(0, "hc", p, step) + 1)
                    dve.wait_ge(qk_done, NBLK * f)
                    for c in range(C):
                        dve.tensor_scalar(qT[:, c, :], hcT[fs][:, c, :], w3T[:, c:c + 1], w2T[:, c:c + 1],
                                          ALU.mult, ALU.add).then_inc(q_ready, 1)
                if back:
                    dve.wait_ge(erow_ready, p + 1)
                    e3 = erow[:].rearrange("o (b i) -> o b i", b=2)
                    dve.tensor_reduce(rsum[:], e3, axis=AX.X, op=ALU.add).then_inc(bsm_done, 1)
                    dve.wait_ge(bsm_done, 2 * p + 1)
                    dve.reciprocal(rinv[:], rsum[:]).then_inc(bsm_done, 1)
                    dve.wait_ge(bsm_done, 2 * p + 2)
                    if later(p, 1):
                        dve.wait_ge(t_free[1], turn(1, "brow", *before(p)) + 1)
                    dve.tensor_tensor(brow[:].rearrange("o (b i) -> o b i", b=2), e3,
                                      rinv[:, :, None].to_broadcast([1, 2, 64]), ALU.mult).then_inc(brow_ready, 1)
                if front:
                    drain_ctx(dve, copy, 1, 1, p, fs, step)
                    for j in range(2, NBLK):
                        drain_ctx(dve, copy, 1, j, p, fs, step)
                        bank_max(j - 2, f)
                if back:
                    dve.wait_ge(t_full[1], turn(1, "brow", p, step) + 1)
                    dve.wait_ge(y_done, p)
                    dve.tensor_tensor(f3[:], hcT[s][:], T[1][:, None, 0:P].to_broadcast([P, C, P]),
                                      ALU.mult).then_inc(t_free[1], 1)
                    dve.wait_ge(t_free[1], turn(1, "brow", p, step) + 1)
                    dve.tensor_reduce(hcb[:], f3[:].rearrange("p c (b i) -> p c b i", b=2), axis=AX.X,
                                      op=ALU.add).then_inc(hcb_done, 1)
                    dve.wait_ge(hcb_done, p + 1)
                    dve.tensor_tensor(f3[:].rearrange("p c (b i) -> p c b i", b=2),
                                      hcT[s][:].rearrange("p c (b i) -> p c b i", b=2),
                                      hcb[:, :, :, None].to_broadcast([P, C, 2, 64]), ALU.mult).then_inc(f3_ready, 1)
                if front:
                    bank_max(3, f)
                    dve.wait_ge(mx_done, 5 * f + 4)
                    dve.tensor_reduce(mx[:], mx4[:], axis=AX.X, op=ALU.max).then_inc(mx_done, 1)
                    dve.wait_ge(mx_done, 5 * f + 5)
                    dve.tensor_scalar(nmx[:], mx[:], -1.0, None, ALU.mult).then_inc(nmx_ready, 1)
                    dve.wait_ge(s1_ready, f + 1)
                    dve.tensor_scalar(tcol[:], mx[:], s1[:, 0:1], bsim_b[:, 0:1], ALU.add, ALU.add).then_inc(tcol_ready, 1)
                    dve.wait_ge(exp_done, 4 * f + 4)
                    dve.tensor_reduce(zsum[:], z4[:], axis=AX.X, op=ALU.add).then_inc(z_done, 1)
                    dve.wait_ge(z_done, f + 1)
                    dve.wait_ge(hqh_ready, f)
                    dve.reciprocal(rz[:], zsum[:]).then_inc(rz_ready, 1)
                    drain_probs(dve, copy, 1, p, step)

            def bank_max(k, f):
                dve.wait_ge(qk_done, NBLK * f + (k + 1 if k < 3 else NBLK))
                dve.tensor_reduce(mx4[:, k:k + 1], S[:, k, 0:bank_cols(k)], axis=AX.X, op=ALU.max).then_inc(mx_done, 1)

            steps(dve, body)
            add_x(PAIRS - 1, 1)


def make_identity(nc, ident):
    with nc.semaphore("ident_zero") as ident_zero, nc.Block() as block:
        @block.gpsimd
        def _(pool):
            pool.memset(ident[:], 0.0).then_inc(ident_zero, 1)
            pool.wait_ge(ident_zero, 1)
            pool.affine_select(out=ident[:], in_=ident[:], compare_op=ALU.not_equal, fill=1.0, base=0,
                               pattern=[[-1, P]], channel_multiplier=1).then_inc(ident_zero, 1)


def recurrence_gates(nc, sh, ident, x1, Wg, bg, br, decay, u_d, c_d):
    D, C, N = sh.D, sh.C, sh.N
    TILES = N // P
    with ExitStack() as stack:
        def sb(name, shape, dt=F32):
            return stack.enter_context(nc.sbuf_tensor(name, shape, dt))

        def sem(name):
            return stack.enter_context(nc.semaphore(name))

        wg_rows = sb("wg_rows", [P, C, D])
        wgT = sb("wgT", [P, C, D])
        bg_b = sb("bg_b", [P, D])
        br_b = sb("br_b", [P, D])
        om_b = sb("om_b", [P, D])
        dec_b = sb("dec_b", [P, D])
        xt = [sb(f"g_xt{s}", [P, D]) for s in range(2)]
        xn = [sb(f"g_xn{s}", [P, D]) for s in range(2)]
        xnT = [sb(f"g_xnT{s}", [P, C, P]) for s in range(2)]
        zt = sb("zt", [P, D])
        z = sb("z", [P, D])
        xm = sb("xm", [P, D])
        u = [sb(f"g_u{s}", [P, D]) for s in range(2)]
        cc = [sb(f"g_c{s}", [P, D]) for s in range(2)]
        stats = sb("g_stats", [P, 6])
        mv = sb("g_mv", [P, 2])
        ve = sb("g_ve", [P, 1])
        nmean = sb("g_nmean", [P, 1])
        rstd = sb("g_rstd", [P, 1])
        mhalf = sb("g_mhalf", [P, 1])
        T = [stack.enter_context(nc.psum_tensor(f"g_T{s}", [P, 512], F32)) for s in range(2)]
        Z = [stack.enter_context(nc.psum_tensor(f"g_Z{s}", [P, 512], F32)) for s in range(2)]

        w_in = sem("g_w_in")
        row_in = sem("g_row_in")
        x_in = [sem(f"g_x_in{s}") for s in range(2)]
        uc_out = [sem(f"g_uc_out{s}") for s in range(2)]
        half_set = sem("g_half_set")
        om_done = sem("g_om_done")
        wT_full = sem("g_wT_full")
        wT_ready = sem("g_wT_ready")
        stat_done = sem("g_stat_done")
        ln_ready = sem("g_ln_ready")
        rstd_ready = sem("g_rstd_ready")
        xn_ready = sem("g_xn_ready")
        xT_full = sem("g_xT_full")
        xnT_ready = sem("g_xnT_ready")
        z_full = sem("g_z_full")
        zt_ready = sem("g_zt_ready")
        z_ready = sem("g_z_ready")
        xm_ready = sem("g_xm_ready")
        u_ready = sem("g_u_ready")
        c_ready = sem("g_c_ready")
        block = stack.enter_context(nc.Block())

        u_rows = u_d.rearrange("(c b) l e -> (b l) c e", c=C)
        c_rows = c_d.rearrange("(c b) l e -> (b l) c e", c=C)

        def steps(eng, body):
            body(0, 0)
            body(1, 1)
            with eng.Fori(1, TILES // 2) as i:
                body(2 * i, 0)
                body(2 * i + 1, 1)

        @block.sync
        def _(sp):
            def load(k, s):
                sp.dma_start(xt[s][:], x1[k]).then_inc(x_in[s], 16)

            sp.dma_start(wg_rows[:], Wg.rearrange("(k p) d -> p k d", p=P)).then_inc(w_in, 16)
            load(0, 0)
            load(1, 1)
            sp.dma_start(dec_b[:], bcast_row(decay)).then_inc(row_in, 16)
            sp.dma_start(bg_b[:], bcast_row(bg)).then_inc(row_in, 16)
            sp.dma_start(br_b[:], bcast_row(br)).then_inc(row_in, 16)

            def store(k, s, base):
                sp.wait_ge(u_ready, k + 1)
                sp.dma_start(u_rows[base], u[s][:].rearrange("p (c e) -> p c e", c=C)).then_inc(uc_out[s], 16)
                sp.wait_ge(c_ready, k + 1)
                sp.dma_start(c_rows[base], cc[s][:].rearrange("p (c e) -> p c e", c=C)).then_inc(uc_out[s], 16)

            def body(k, s, more):
                base = bass.ds(k * P, P) if isinstance(k, int) else bass.ds(sp.snap(k * P), P)
                if more:
                    nxt = k + 2 if isinstance(k, int) else sp.snap(k + 2)
                    sp.wait_ge(xn_ready, k + 1)
                    load(nxt, s)
                store(k, s, base)

            with sp.Fori(0, TILES // 2 - 1) as i:
                body(2 * i, 0, True)
                body(2 * i + 1, 1, True)
            body(TILES - 2, 0, False)
            body(TILES - 1, 1, False)
            for s in range(2):
                sp.wait_ge(uc_out[s], 32 * (TILES // 2))

        @block.gpsimd
        def _(pool):
            pool.memset(mhalf[:], -0.5).then_inc(half_set, 1)
            pool.wait_ge(half_set, 1)
            pool.wait_ge(row_in, 48)

            def body(k, s):
                pool.wait_ge(ln_ready, 2 * k + 2)
                pool.tensor_tensor(rstd[:], ve[:], mhalf[:], ALU.pow).then_inc(rstd_ready, 1)
                pool.wait_ge(xn_ready, k + 1)
                pool.wait_ge(c_ready, k)
                pool.tensor_tensor(xm[:], xn[s][:], br_b[:], ALU.subtract).then_inc(xm_ready, 1)

            steps(pool, body)

        @block.tensor
        def _(pe):
            pe.wait_ge(w_in, 16)
            for k in range(C):
                if k >= 2:
                    pe.wait_ge(wT_ready, k - 1)
                for c in range(C):
                    last = pe.transpose(T[k % 2][:, c * P:(c + 1) * P], wg_rows[:, k, c * P:(c + 1) * P], ident[:])
                last.then_inc(wT_full, 1)
            pe.wait_ge(wT_ready, C)

            def turn(k, s):
                pe.wait_ge(xn_ready, k + 1)
                if later(k, 2):
                    pe.wait_ge(xnT_ready, k - 1)
                for c in range(C):
                    last = pe.transpose(T[s][:, c * P:(c + 1) * P], xn[s][:, c * P:(c + 1) * P], ident[:])
                last.then_inc(xT_full, 1)

            def gates(k, s):
                pe.wait_ge(xnT_ready, k + 1)
                if later(k, 2):
                    pe.wait_ge(zt_ready, k - 1)
                for c in range(C):
                    last = pe.matmul(Z[s][:], xnT[s][:, c, :], wgT[:, c, :], start=(c == 0), stop=(c == C - 1))
                last.then_inc(z_full, 1)

            turn(0, 0)
            turn(1, 1)
            gates(0, 0)
            with pe.Fori(0, TILES // 2 - 1) as i:
                turn(2 * i + 2, 0)
                gates(2 * i + 1, 1)
                turn(2 * i + 3, 1)
                gates(2 * i + 2, 0)
            gates(TILES - 1, 1)

        @block.scalar
        def _(act):
            act.wait_ge(row_in, 48)
            act.activation(om_b[:], dec_b[:], ACT.Sigmoid).then_inc(om_done, 1)
            for k in range(0, C, 2):
                act.wait_ge(wT_full, k + 1)
                act.copy(wgT[:, :, k * P:(k + 1) * P], T[0][:].rearrange("p (c e) -> p c e", c=C)).then_inc(wT_ready, 1)
                act.wait_ge(wT_full, k + 2)
                act.copy(wgT[:, :, (k + 1) * P:(k + 2) * P], T[1][:].rearrange("p (c e) -> p c e", c=C)).then_inc(wT_ready, 1)

            def drain(k, s):
                act.wait_ge(xT_full, k + 1)
                if later(k, 2):
                    act.wait_ge(z_full, k - 1)
                act.copy(xnT[s][:], T[s][:].rearrange("p (c i) -> p c i", c=C)).then_inc(xnT_ready, 1)

            def gate(k, s):
                act.wait_ge(zt_ready, k + 1)
                act.wait_ge(u_ready, k)
                act.activation(z[:], zt[:], ACT.Sigmoid).then_inc(z_ready, 1)

            drain(0, 0)
            drain(1, 1)
            gate(0, 0)
            with act.Fori(0, TILES // 2 - 1) as i:
                drain(2 * i + 2, 0)
                gate(2 * i + 1, 1)
                drain(2 * i + 3, 1)
                gate(2 * i + 2, 0)
            gate(TILES - 1, 1)

        @block.vector
        def _(dve):
            dve.wait_ge(om_done, 1)
            dve.tensor_scalar(om_b[:], om_b[:], -1.0, 1.0, ALU.mult, ALU.add).then_inc(om_done, 1)
            dve.wait_ge(om_done, 2)

            def norm(k, s, loads):
                dve.wait_ge(x_in[s], 16 * loads)
                dve.wait_ge(rstd_ready, k)
                dve.bn_stats(stats[:], xt[s][:])
                dve.drain()
                dve.bn_aggr(mv[:], stats[:]).then_inc(stat_done, 1)
                dve.wait_ge(stat_done, k + 1)
                dve.wait_ge(xn_ready, k)
                dve.tensor_scalar(ve[:], mv[:, 1:2], LN_EPS, None, ALU.add).then_inc(ln_ready, 1)
                dve.tensor_scalar(nmean[:], mv[:, 0:1], -1.0, None, ALU.mult).then_inc(ln_ready, 1)
                dve.wait_ge(ln_ready, 2 * k + 2)
                dve.wait_ge(rstd_ready, k + 1)
                if later(k, 2):
                    dve.wait_ge(xT_full, k - 1)
                    dve.wait_ge(xm_ready, k - 1)
                dve.tensor_scalar(xn[s][:], xt[s][:], nmean[:, 0:1], rstd[:, 0:1], ALU.add, ALU.mult).then_inc(xn_ready, 1)

            def gate(k, s):
                dve.wait_ge(z_full, k + 1)
                dve.wait_ge(z_ready, k)
                dve.tensor_tensor(zt[:], Z[s][:], bg_b[:], ALU.add).then_inc(zt_ready, 1)

            def products(k, s, stored):
                dve.wait_ge(z_ready, k + 1)
                if later(k, 2):
                    dve.wait_ge(uc_out[s], 32 * stored)
                dve.tensor_tensor(u[s][:], z[:], om_b[:], ALU.mult).then_inc(u_ready, 1)
                dve.wait_ge(u_ready, k + 1)
                dve.wait_ge(xm_ready, k + 1)
                dve.tensor_tensor(cc[s][:], u[s][:], xm[:], ALU.mult).then_inc(c_ready, 1)

            norm(0, 0, 1)
            norm(1, 1, 1)
            gate(0, 0)
            products(0, 0, 0)
            norm(2, 0, 2)
            gate(1, 1)
            products(1, 1, 0)
            with dve.Fori(0, TILES // 2 - 2) as i:
                norm(2 * i + 3, 1, i + 2)
                gate(2 * i + 2, 0)
                products(2 * i + 2, 0, i + 1)
                norm(2 * i + 4, 0, i + 3)
                gate(2 * i + 3, 1)
                products(2 * i + 3, 1, i + 1)
            norm(TILES - 1, 1, TILES // 2)
            gate(TILES - 2, 0)
            products(TILES - 2, 0, TILES // 2 - 1)
            gate(TILES - 1, 1)
            products(TILES - 1, 1, TILES // 2 - 1)


class Routing:

    def __init__(self, nc, sh, stack):
        self.region = P + sh.N
        self.tiles = (2 * sh.N + sh.E * (P - 1)) // P
        self.spare = self.tiles - 2 * sh.N // P
        self.rows = sh.E * self.region + self.spare * P
        tiles, E = sh.N // P, sh.E

        def sb(name, shape, dt=F32):
            return stack.enter_context(nc.sbuf_tensor(name, shape, dt))

        self.x2 = sb("x2", [P, tiles, sh.D])
        self.picks = sb("picks", [P, tiles, 5])
        self.places = sb("places", [P, tiles, 2])
        self.rev = sb("rev", [P, E])
        self.acc = sb("acc", [P, E])
        self.first_row = sb("first_row", [P, E + 1])
        self.x_rows = nc.dram_tensor("routed_x", (self.rows, sh.D), F32, kind="Internal").ap()
        self.y_rows = nc.dram_tensor("routed_y", (self.tiles * P, sh.D), F32, kind="Internal").ap()


def recurrence(nc, sh, ident, x1, u_d, c_d, decay, Wr, Wo, bo, ln_w, ln_b, gate_w, rt, ex):
    D, C, E, B = sh.D, sh.C, sh.E, sh.B
    TILES, ST = sh.N // P, P // B
    TOP_OPS = 10
    with ExitStack() as stack:
        def sb(name, shape, dt=F32):
            return stack.enter_context(nc.sbuf_tensor(name, shape, dt))

        def sem(name):
            return stack.enter_context(nc.semaphore(name))

        def psum(name):
            return stack.enter_context(nc.psum_tensor(name, [P, 512], F32))

        w_rows = [sb(f"w_rows{i}", [P, C, D]) for i in range(2)]
        WrT = sb("WrT", [P, C, D])
        WoT = sb("WoT", [P, C, D])
        gw = sb("gw", [E, D])
        gwT = sb("gwT", [P, C, E])
        lnw = sb("lnw", [P, C])
        lnb = sb("lnb", [P, C])
        lnb_w = sb("lnb_w", [P, C, P])
        bo_b = sb("bo_b", [P, D])
        dec_h = sb("dec_h", [P, P])
        df_h = sb("df_h", [P, P])
        zero = sb("zero", [P, D])
        tri = sb("tri", [P, P])
        ones = sb("r_ones", [P, P])
        rev = rt.rev
        ebase = sb("ebase", [P, E])
        mhalf = sb("r_mhalf", [P, 1])
        ut = [sb(f"ut{s}", [P, ST, P]) for s in range(2)]
        ct = [sb(f"ct{s}", [P, ST, P]) for s in range(2)]
        xt = [sb(f"r_xt{s}", [P, D]) for s in range(2)]
        H = sb("H", [P, P])
        m = sb("m", [P, P])
        gd = sb("gd", [P, P])
        g = sb("g", [P, P])
        yT = [sb(f"yT{s}", [P, C, ST, B]) for s in range(2)]
        yn = sb("yn", [P, D])
        ynT = sb("ynT", [P, C, P])
        xn3 = [sb(f"xn3{s}", [P, D]) for s in range(2)]
        xn3T = sb("xn3T", [P, C, P])
        st2, st3 = sb("st2", [P, 6]), sb("st3", [P, 6])
        mv2, mv3 = sb("mv2", [P, 2]), sb("mv3", [P, 2])
        ve2, ve3 = sb("ve2", [P, 1]), sb("ve3", [P, 1])
        nm2, nm3 = sb("nm2", [P, 1]), sb("nm3", [P, 1])
        rs2, rs3 = sb("rs2", [P, 1]), sb("rs3", [P, 1])
        nmx = sb("r_nmx", [P, 1])
        ew = sb("ew", [P, E])
        pick = sb("pick", [P, 5])
        m1, m2, i1, i2, exs = (pick[:, i:i + 1] for i in range(5))
        t1, t2 = sb("t1", [P, E]), sb("t2", [P, E])
        exr = sb("exr", [P, E])
        oh1, oh2, oh = sb("oh1", [P, E]), sb("oh2", [P, E]), sb("oh", [P, E])
        row = sb("row", [P, E])
        p1, p2 = sb("p1", [P, E]), sb("p2", [P, E])
        pl = sb("pl", [P, 2])
        pl_i = sb("pl_i", [P, 2], I32)
        zero2 = sb("zero2", [P, 2], I32)
        pli = [sb(f"pli{s}", [P, 2], I32) for s in range(2)]

        Pb, HT, Yb, YT, Wb, XT, Lg, Rk = (psum(n) for n in ("Pb", "HT", "Yb", "YT", "Wb", "XT", "Lg", "Rk"))

        w_in = [sem(f"r_w_in{i}") for i in range(2)]
        row_in, decay_in = sem("r_row_in"), sem("r_decay_in")
        zero_set, zero_out = sem("zero_set"), sem("zero_out")
        uc_in = [sem(f"uc_in{s}") for s in range(2)]
        x_in = [sem(f"r_x_in{s}") for s in range(2)]
        consts, df_ready = sem("r_consts"), sem("df_ready")
        wT_full, wT_ready = sem("r_wT_full"), sem("r_wT_ready")
        lnb_ready, bo_full, bo_ready, wo_scaled = sem("lnb_ready"), sem("bo_full"), sem("bo_ready"), sem("wo_scaled")
        pred_full, m_done, gd_done, g_ready = sem("pred_full"), sem("m_done"), sem("gd_done"), sem("g_ready")
        h_ready, hT_full, yT_ready = sem("h_ready"), sem("hT_full"), sem("yT_ready")
        y_full, st2_done, ln2_ready, rs2_ready = sem("y_full"), sem("st2_done"), sem("ln2_ready"), sem("rs2_ready")
        yn_ready, yn_full, ynT_ready = sem("yn_ready"), sem("yn_full"), sem("ynT_ready")
        wo_done, xp_ready, x2_ready = sem("wo_done"), sem("xp_ready"), sem("x2_ready")
        st3_done, ln3_ready, rs3_ready = sem("st3_done"), sem("ln3_ready"), sem("rs3_ready")
        xn3_ready, xn3_full, xn3T_ready = sem("xn3_ready"), sem("xn3_full"), sem("xn3T_ready")
        lg_done, nmx_ready, ex_ready = sem("lg_done"), sem("r_nmx_ready"), sem("ex_ready")
        top_step, pfx_done, place_step, places_ready = sem("top_step"), sem("pfx_done"), sem("place_step"), sem("places_ready")
        kept, pli_ready = sem("kept"), sem("pli_ready")
        x_scattered = [sem(f"x_scattered{s}") for s in range(2)]
        block = stack.enter_context(nc.Block())

        x1_tiles = x1.rearrange("k p d -> (k p) d").rearrange("(b k t) d -> k t b d", t=ST, k=TILES)

        def first(k):
            return isinstance(k, int) and k == 0

        def has(j):
            return not isinstance(j, int) or 0 <= j < TILES

        def walk(eng, body, lag):
            for k in range(6):
                body(k, k % 2, True, k // 2 + 1)
            with eng.Fori(3, TILES // 2) as i:
                body(2 * i, 0, True, i + 1)
                body(2 * i + 1, 1, True, i + 1)
            for k in range(TILES, TILES + lag):
                body(k, k % 2, False, None)

        def idx(eng, k):
            return k if isinstance(k, int) else eng.snap(k)

        @block.sync
        def _(sp):
            for i, W in enumerate((Wr, Wo)):
                sp.dma_start(w_rows[i][:], W.rearrange("(k p) d -> p k d", p=P)).then_inc(w_in[i], 16)
            for c in range(C):
                sp.dma_start(dec_h[c * B:(c + 1) * B, :],
                             decay[c * P:(c + 1) * P].rearrange("(o d) -> o d", o=1).to_broadcast([B, P])).then_inc(decay_in, 16)
            sp.dma_start(gw[:], gate_w).then_inc(row_in, 16)
            sp.dma_start(bo_b[:], bcast_row(bo)).then_inc(row_in, 16)
            with nc.allow_non_contiguous_dma(reason="two small vectors, a column for each chunk"):
                sp.dma_start(lnw[:], ln_w.rearrange("(c p) -> p c", p=P)).then_inc(row_in, 16)
                sp.dma_start(lnb[:], ln_b.rearrange("(c p) -> p c", p=P)).then_inc(row_in, 16)

            def load_uc(k, s):
                steps = bass.ds(k * ST, ST) if isinstance(k, int) else bass.ds(sp.snap(k * ST), ST)
                sp.dma_start(ut[s][:], u_d[:, steps, :]).then_inc(uc_in[s], 16)
                sp.dma_start(ct[s][:], c_d[:, steps, :]).then_inc(uc_in[s], 16)

            def load_x(k, s):
                sp.dma_start(xt[s][:], x1_tiles[k]).then_inc(x_in[s], 16)

            load_uc(0, 0)
            load_uc(1, 1)
            sp.wait_ge(zero_set, 1)
            pads = [e * rt.region for e in range(E)] + [E * rt.region + i * P for i in range(rt.spare)]
            for r in pads:
                sp.dma_start(rt.x_rows[r:r + P, :], zero[:]).then_inc(zero_out, 16)
            for e in range(ex.SLOTS):
                ex.load(sp, e)

            def body(k, s, more):
                nxt = k + 2 if isinstance(k, int) else sp.snap(k + 2)
                cur = idx(sp, k)
                if more:
                    sp.wait_ge(h_ready, ST * k + ST)
                    load_uc(nxt, s)
                if later(k, 2):
                    sp.wait_ge(x2_ready, k - 1)
                load_x(cur, s)

            for k in range(2):
                body(k, k, True)
            with sp.Fori(1, TILES // 2 - 1) as i:
                body(2 * i, 0, True)
                body(2 * i + 1, 1, True)
            for k in range(TILES - 2, TILES):
                body(k, k % 2, False)
            sp.wait_ge(zero_out, 16 * len(pads))

        @block.gpsimd
        def _(pool):
            pool.memset(mhalf[:], -0.5).then_inc(consts, 1)
            pool.memset(zero[:], 0.0).then_inc(zero_set, 1)
            pool.memset(ones[:], 1.0).then_inc(consts, 1)
            pool.memset(zero2[:], 0).then_inc(consts, 1)
            pool.memset(rt.acc[:], 0.0).then_inc(consts, 1)
            for e in range(E):
                pool.memset(rev[:, e:e + 1], float(E - e)).then_inc(consts, 1)
                pool.memset(ebase[:, e:e + 1], float(e * rt.region + P)).then_inc(consts, 1)
            pool.wait_ge(consts, 4 + 2 * E)
            pool.affine_select(out=tri[:], in_=ones[:], compare_op=ALU.is_gt, fill=0.0, base=0,
                               pattern=[[1, P]], channel_multiplier=-1).then_inc(consts, 1)
            pool.wait_ge(df_ready, 1)

            def scatter(j, s, which):
                if which == 0:
                    pool.wait_ge(places_ready, j + 1)
                    pool.tensor_tensor(pli[s][:], pl_i[:], zero2[:], ALU.add).then_inc(pli_ready, 1)
                    pool.drain()
                pool.indirect_dma_start(out=rt.x_rows,
                                        out_offset=bass.IndirectOffsetOnAxis(ap=pli[s][:, which:which + 1], axis=0),
                                        in_=xn3[s][:], in_offset=None).then_inc(x_scattered[s], 16)

            def body(k, s, scan, loads):
                for st in range(ST):
                    if scan and not (st == 0 and first(k)):
                        t = ST * k + st
                        pool.wait_ge(h_ready, t)
                        if st == 0:
                            pool.wait_ge(uc_in[s], 32 * loads)
                        pool.tensor_tensor(gd[:], H[:], df_h[:], ALU.mult).then_inc(gd_done, 1)
                        pool.wait_ge(gd_done, t)
                        pool.tensor_tensor(g[:], gd[:], ct[s][:, st, :], ALU.add).then_inc(g_ready, 1)
                    if st == 0 and has(k - 5):
                        scatter(k - 5, 1 - s, 1)
                    if st == 1 and has(k - 3):
                        pool.wait_ge(ln3_ready, 2 * (k - 2))
                        pool.tensor_tensor(rs3[:], ve3[:], mhalf[:], ALU.pow).then_inc(rs3_ready, 1)
                    if st == 2 and has(k - 1):
                        pool.wait_ge(ln2_ready, 2 * k)
                        pool.tensor_tensor(rs2[:], ve2[:], mhalf[:], ALU.pow).then_inc(rs2_ready, 1)
                    if st == 3 and has(k - 4):
                        scatter(k - 4, s, 0)

            walk(pool, body, 6)
            for s in range(2):
                pool.wait_ge(x_scattered[s], 16 * TILES)

        @block.tensor
        def _(pe):
            for i in range(2):
                pe.wait_ge(w_in[i], 16)
                for k in range(C):
                    n = C * i + k
                    if n >= 2:
                        pe.wait_ge(wT_ready, n - 1)
                    bank = (YT, XT)[n % 2]
                    for c in range(C):
                        last = pe.transpose(bank[:, c * P:(c + 1) * P], w_rows[i][:, k, c * P:(c + 1) * P], ident[:])
                    last.then_inc(wT_full, 1)
            pe.wait_ge(row_in, 64)
            pe.wait_ge(wT_ready, 2 * C - 1)
            for c in range(C):
                last = pe.transpose(YT[:, c * E:(c + 1) * E], gw[:, c * P:(c + 1) * P], ident[0:E, 0:E])
            last.then_inc(wT_full, 1)
            pe.wait_ge(wT_ready, 2 * C + 1)
            pe.wait_ge(lnb_ready, 1)
            for c in range(C):
                last = pe.matmul(Wb[:], lnb_w[:, c, :], WoT[:, c, :], start=(c == 0), stop=(c == C - 1))
            last.then_inc(bo_full, 1)

            def predict(k, s, st):
                pe.wait_ge(yT_ready, ST * k + st)
                src, prev = (yT[s], st - 1) if st else (yT[1 - s], ST - 1)
                for c in range(C):
                    for o in range(C):
                        last = pe.matmul(Pb[o * B:(o + 1) * B, 0:P], src[:, c, prev, :], WrT[:, c, o * P:(o + 1) * P],
                                         start=(c == 0), stop=(c == C - 1))
                last.then_inc(pred_full, 1)

            def body(k, s, scan, loads):
                for st in range(ST):
                    if scan and not (st == 0 and first(k)):
                        predict(k, s, st)
                    if has(k - 2):
                        if st == 0:
                            pe.wait_ge(ynT_ready, k - 1)
                            if has(k - 3):
                                pe.wait_ge(x2_ready, k - 2)
                            if first(k - 2):
                                pe.wait_ge(wo_scaled, 1)
                        mm = pe.matmul(Wb[:], ynT[:, st, :], WoT[:, st, :], start=(st == 0), stop=(st == C - 1))
                        if st == ST - 1:
                            mm.then_inc(wo_done, 1)
                    if st == 2 and has(k - 4):
                        pe.wait_ge(top_step, TOP_OPS * (k - 3))
                        if has(k - 5):
                            pe.wait_ge(places_ready, k - 4)
                        pe.matmul(Rk[:, 0:P], tri[:], oh[:, None, :].to_broadcast([P, P // E, E]), start=True, stop=False)
                        pe.matmul(Rk[:, 0:P], ones[:], rt.acc[:, None, :].to_broadcast([P, P // E, E]),
                                  start=False, stop=True).then_inc(pfx_done, 1)
                    if scan:
                        pe.wait_ge(h_ready, ST * k + st + 1)
                        pe.transpose(HT[:, 0:P], H[:], ident[:]).then_inc(hT_full, 1)
                    if st == 0 and has(k - 1):
                        if has(k - 2):
                            pe.wait_ge(yn_ready, k - 1)
                        if not scan:
                            pe.wait_ge(yT_ready, ST * k)
                        for c in range(C):
                            last = pe.transpose(Yb[:, c * P:(c + 1) * P], yT[1 - s][:, c].rearrange("p t b -> p (t b)"), ident[:])
                        last.then_inc(y_full, 1)
                    if st == 2 and has(k - 3):
                        pe.wait_ge(xn3_ready, k - 2)
                        if has(k - 4):
                            pe.wait_ge(xn3T_ready, k - 3)
                        for c in range(C):
                            last = pe.transpose(XT[:, c * P:(c + 1) * P], xn3[1 - s][:, c * P:(c + 1) * P], ident[:])
                        last.then_inc(xn3_full, 1)
                    if st == 3 and has(k - 1):
                        pe.wait_ge(yn_ready, k)
                        if has(k - 2):
                            pe.wait_ge(ynT_ready, k - 1)
                        for c in range(C):
                            last = pe.transpose(YT[:, c * P:(c + 1) * P], yn[:, c * P:(c + 1) * P], ident[:])
                        last.then_inc(yn_full, 1)
                    if st == 3 and has(k - 3):
                        pe.wait_ge(xn3T_ready, k - 2)
                        if has(k - 4):
                            pe.wait_ge(ex_ready, k - 3)
                        for c in range(C):
                            last = pe.matmul(Lg[:, 0:P], xn3T[:, c, :], gwT[:, c, None, :].to_broadcast([P, P // E, E]),
                                             start=(c == 0), stop=(c == C - 1))
                        last.then_inc(lg_done, 1)

            walk(pe, body, 5)

        @block.scalar
        def _(act):
            act.wait_ge(decay_in, 16 * C)
            act.activation(df_h[:], dec_h[:], ACT.Sigmoid).then_inc(df_ready, 1)
            for i, WT in enumerate((WrT, WoT)):
                for k in range(C):
                    n = C * i + k
                    act.wait_ge(wT_full, n + 1)
                    bank = (YT, XT)[n % 2]
                    act.copy(WT[:, :, k * P:(k + 1) * P], bank[:].rearrange("p (c e) -> p c e", c=C)).then_inc(wT_ready, 1)
            act.wait_ge(wT_full, 2 * C + 1)
            act.copy(gwT[:], YT[:, 0:C * E].rearrange("p (c e) -> p c e", c=C)).then_inc(wT_ready, 1)

            def body(k, s, scan, loads):
                for st in range(ST):
                    if scan:
                        act.wait_ge(hT_full, ST * k + st + 1)
                        act.copy(yT[s][:, :, st, :], HT[:, 0:P].rearrange("p (c b) -> p c b", c=C)).then_inc(yT_ready, 1)
                    if st == 0 and has(k - 4):
                        act.wait_ge(nmx_ready, k - 3)
                        act.wait_ge(kept, k - 4)
                        if has(k - 5):
                            act.wait_ge(top_step, TOP_OPS * (k - 4))
                        act.activation(ew[:], Lg[:, 0:E], ACT.Exp, bias=nmx[:, 0:1], accum_out=exs).then_inc(ex_ready, 1)
                    if st == 2 and has(k - 3):
                        act.wait_ge(xn3_full, k - 2)
                        if has(k - 4):
                            act.wait_ge(lg_done, k - 3)
                        act.copy(xn3T[:], XT[:].rearrange("p (c i) -> p c i", c=C)).then_inc(xn3T_ready, 1)
                    if st == 3 and has(k - 1):
                        act.wait_ge(yn_full, k)
                        if has(k - 2):
                            act.wait_ge(wo_done, k - 1)
                        act.copy(ynT[:], YT[:].rearrange("p (c i) -> p c i", c=C)).then_inc(ynT_ready, 1)

            walk(act, body, 5)

        @block.vector
        def _(dve):
            dve.wait_ge(row_in, 64)
            dve.tensor_copy(lnb_w[:], lnb[:, :, None].to_broadcast([P, C, P])).then_inc(lnb_ready, 1)
            dve.wait_ge(bo_full, 1)
            dve.tensor_tensor(bo_b[:], bo_b[:], Wb[:], ALU.add).then_inc(bo_ready, 1)
            dve.tensor_tensor(WoT[:], WoT[:], lnw[:, :, None].to_broadcast([P, C, D]), ALU.mult).then_inc(wo_scaled, 1)
            dve.wait_ge(bo_ready, 1)
            dve.wait_ge(consts, 5 + 2 * E)

            def norm_stats(src, st, mv, ve, nm, done, ready, j):
                dve.bn_stats(st[:], src)
                dve.drain()
                dve.bn_aggr(mv[:], st[:]).then_inc(done, 1)
                dve.wait_ge(done, j + 1)
                dve.tensor_scalar(ve[:], mv[:, 1:2], LN_EPS, None, ALU.add).then_inc(ready, 1)
                dve.tensor_scalar(nm[:], mv[:, 0:1], -1.0, None, ALU.mult).then_inc(ready, 1)

            def top_two(j):
                n = TOP_OPS * j
                col = idx(dve, j)
                dve.wait_ge(ex_ready, j + 1)
                if later(j, 1):
                    dve.wait_ge(places_ready, j)
                dve.tensor_reduce(m1, ew[:], axis=AX.X, op=ALU.max).then_inc(top_step, 1)
                dve.wait_ge(top_step, n + 1)
                dve.scalar_tensor_tensor(t1[:], ew[:], m1, rev[:], ALU.is_equal, ALU.mult).then_inc(top_step, 1)
                dve.wait_ge(top_step, n + 2)
                dve.tensor_reduce(i1, t1[:], axis=AX.X, op=ALU.max).then_inc(top_step, 1)
                dve.wait_ge(top_step, n + 3)
                dve.tensor_scalar(oh1[:], rev[:], i1, None, ALU.is_equal).then_inc(top_step, 1)
                dve.wait_ge(top_step, n + 4)
                dve.scalar_tensor_tensor(exr[:], oh1[:], -4.0, ew[:], ALU.mult, ALU.add).then_inc(top_step, 1)
                dve.wait_ge(top_step, n + 5)
                dve.tensor_reduce(m2, exr[:], axis=AX.X, op=ALU.max).then_inc(top_step, 1)
                dve.wait_ge(top_step, n + 6)
                dve.scalar_tensor_tensor(t2[:], exr[:], m2, rev[:], ALU.is_equal, ALU.mult).then_inc(top_step, 1)
                dve.wait_ge(top_step, n + 7)
                dve.tensor_reduce(i2, t2[:], axis=AX.X, op=ALU.max).then_inc(top_step, 1)
                dve.wait_ge(top_step, n + 8)
                dve.tensor_scalar(oh2[:], rev[:], i2, None, ALU.is_equal).then_inc(top_step, 1)
                dve.wait_ge(top_step, n + 9)
                dve.tensor_tensor(oh[:], oh1[:], oh2[:], ALU.add).then_inc(top_step, 1)
                dve.tensor_copy(rt.picks[:, col, :], pick[:]).then_inc(kept, 1)

            def row_places(j, s):
                col = idx(dve, j)
                n = 4 * j
                dve.wait_ge(pfx_done, j + 1)
                dve.tensor_tensor(row[:], Rk[:, 0:E], ebase[:], ALU.add).then_inc(place_step, 1)
                dve.tensor_tensor(rt.acc[:], rt.acc[:], oh[:], ALU.add).then_inc(place_step, 1)
                dve.wait_ge(place_step, n + 1)
                dve.tensor_tensor_reduce(out=p1[:], in0=row[:], in1=oh1[:], scale=1.0, scalar=0.0,
                                         op0=ALU.mult, op1=ALU.add, accum_out=pl[:, 0:1]).then_inc(place_step, 1)
                dve.tensor_tensor_reduce(out=p2[:], in0=row[:], in1=oh2[:], scale=1.0, scalar=0.0,
                                         op0=ALU.mult, op1=ALU.add, accum_out=pl[:, 1:2]).then_inc(place_step, 1)
                dve.wait_ge(place_step, n + 4)
                dve.tensor_copy(rt.places[:, col, :], pl[:])
                dve.wait_ge(pli_ready, j)
                dve.tensor_copy(pl_i[:], pl[:]).then_inc(places_ready, 1)

            def body(k, s, scan, loads):
                for st in range(ST):
                    if scan:
                        t = ST * k + st
                        if st == 0:
                            dve.wait_ge(uc_in[s], 32 * loads)
                        if st == 0 and first(k):
                            dve.tensor_copy(H[:], ct[s][:, st, :]).then_inc(h_ready, 1)
                        else:
                            dve.wait_ge(pred_full, t)
                            dve.tensor_tensor(m[:], Pb[:, 0:P], ut[s][:, st, :], ALU.mult).then_inc(m_done, 1)
                            dve.wait_ge(m_done, t)
                            dve.wait_ge(g_ready, t)
                            dve.tensor_tensor(H[:], g[:], m[:], ALU.subtract).then_inc(h_ready, 1)
                    if st == 0 and has(k - 3):
                        j = k - 3
                        dve.wait_ge(bo_ready, 1)
                        dve.wait_ge(x2_ready, j + 1)
                        if has(k - 4):
                            dve.wait_ge(xn3_ready, j)
                        norm_stats(rt.x2[:, idx(dve, j), :], st3, mv3, ve3, nm3, st3_done, ln3_ready, j)
                    if st == 0 and has(k - 4):
                        dve.wait_ge(lg_done, k - 3)
                        dve.tensor_reduce(nmx[:], Lg[:, 0:E], axis=AX.X, op=ALU.max, negate=True).then_inc(nmx_ready, 1)
                    if st == 1 and has(k - 1):
                        j = k - 1
                        dve.wait_ge(y_full, j + 1)
                        if has(k - 2):
                            dve.wait_ge(yn_ready, j)
                        norm_stats(Yb[:], st2, mv2, ve2, nm2, st2_done, ln2_ready, j)
                    if st == 1 and has(k - 3):
                        j = k - 3
                        dve.wait_ge(rs3_ready, j + 1)
                        if has(k - 5):
                            dve.wait_ge(x_scattered[1 - s], 32 * (loads - 3 + s) if scan else 32 * ((k - 3) // 2))
                        dve.tensor_scalar(xn3[1 - s][:], rt.x2[:, idx(dve, j), :], nm3[:, 0:1], rs3[:, 0:1],
                                          ALU.add, ALU.mult).then_inc(xn3_ready, 1)
                    if st == 1 and has(k - 4):
                        top_two(k - 4)
                    if st == 2 and has(k - 1):
                        j = k - 1
                        dve.wait_ge(rs2_ready, j + 1)
                        if has(k - 2):
                            dve.wait_ge(yn_full, j)
                        dve.tensor_scalar(yn[:], Yb[:], nm2[:, 0:1], rs2[:, 0:1], ALU.add, ALU.mult).then_inc(yn_ready, 1)
                    if st == 2 and has(k - 4):
                        row_places(k - 4, s)
                    if st == 2 and has(k - 2):
                        j = k - 2
                        dve.wait_ge(x_in[s], 16 * ((loads - 1) if scan else (j // 2 + 1)))
                        dve.tensor_tensor(xt[s][:], xt[s][:], bo_b[:], ALU.add).then_inc(xp_ready, 1)
                    if st == 3 and has(k - 2):
                        j = k - 2
                        dve.wait_ge(wo_done, j + 1)
                        dve.wait_ge(xp_ready, j + 1)
                        dve.tensor_tensor(rt.x2[:, idx(dve, j), :], Wb[:], xt[s][:], ALU.add).then_inc(x2_ready, 1)

            walk(dve, body, 5)


class Experts:
    SLOTS = 3

    def __init__(self, nc, sh, gate_up, down, stack):
        self.gate_up, self.down = gate_up, down
        self.F = down.shape[1]
        self.wgu = stack.enter_context(nc.sbuf_tensor("wgu", [P, self.SLOTS, sh.C, 2 * self.F], F32))
        self.wdn = stack.enter_context(nc.sbuf_tensor("wdn", [P, self.SLOTS, self.F // P, sh.D], F32))
        self.w_next = [stack.enter_context(nc.semaphore(f"expert_w_next{s}")) for s in range(self.SLOTS)]
        self.w_in = [stack.enter_context(nc.semaphore(f"expert_w_in{s}")) for s in range(self.SLOTS)]

    def load(self, eng, e):
        s = e % self.SLOTS
        loaded = (self.w_in if e < self.SLOTS else self.w_next)[s]
        eng.dma_start(self.wgu[:, s], self.gate_up[e].rearrange("(c p) f -> p c f", p=P)).then_inc(loaded, 16)
        eng.dma_start(self.wdn[:, s], self.down[e].rearrange("(c p) d -> p c d", p=P)).then_inc(loaded, 16)


def experts(nc, sh, ident, ex, rt):
    D, C, E, F, SLOTS = sh.D, sh.C, sh.E, ex.F, ex.SLOTS
    FC = F // P
    TILES = rt.tiles
    MAXT = sh.N // P
    assert TILES % 2 == 1 and F == D
    with ExitStack() as stack:
        def sb(name, shape, dt=F32):
            return stack.enter_context(nc.sbuf_tensor(name, shape, dt))

        def sem(name):
            return stack.enter_context(nc.semaphore(name))

        def psum(name):
            return stack.enter_context(nc.psum_tensor(name, [P, 512], F32))

        ones = sb("f_ones", [P, P])
        tile_no = sb("tile_no", [P, TILES])
        tile_no_i = sb("tile_no_i", [P, TILES], I32)
        step_no = sb("step_no", [P, MAXT])
        step_no_i = sb("step_no_i", [P, MAXT], I32)
        low = sb("low", [P, E, E])
        base = sb("base", [P, E])
        cnt = sb("cnt", [P, E])
        more = sb("more", [P, E, MAXT])
        nt = sb("nt", [P, E])
        upto = sb("upto", [P, E, E])
        te = sb("te", [P, E])
        first_row = rt.first_row
        jump = sb("jump", [P, E])
        past = sb("past", [P, TILES, E])
        hop = sb("hop", [P, TILES, E])
        rowf = sb("rowf", [P, TILES])
        ef = sb("ef", [P, TILES])
        s3, s6 = sb("s3", [P, TILES]), sb("s6", [P, TILES])
        slotf = sb("slotf", [P, TILES])
        te_i = sb("te_i", [P, E], I32)
        row_i = sb("row_i", [P, TILES], I32)
        e_i = sb("e_i", [P, TILES], I32)
        slot_i = sb("slot_i", [P, TILES], I32)

        xt = [sb(f"f_xt{s}", [P, D]) for s in range(2)]
        xT = [sb(f"f_xT{s}", [P, C, P]) for s in range(2)]
        sg = sb("sg", [P, F])
        h = sb("f_h", [P, F])
        hT = sb("f_hT", [P, FC, P])
        yt = [sb(f"f_yt{s}", [P, D]) for s in range(2)]
        Cn, G, U, Dn, TX, TH = (psum(n) for n in ("f_Cn", "f_G", "f_U", "f_Dn", "f_TX", "f_TH"))

        consts, iotas = sem("f_consts"), sem("f_iotas")
        cnt_full, plan_step, plan_ready = sem("cnt_full"), sem("plan_step"), sem("plan_ready")
        w_ready, tile_done = sem("w_ready"), sem("tile_done")
        x_in = [sem(f"f_x_in{s}") for s in range(2)]
        y_out = [sem(f"f_y_out{s}") for s in range(2)]
        x_full, xT_ready = sem("f_x_full"), sem("f_xT_ready")
        g_full, sg_ready, u_full, h_ready = sem("f_g_full"), sem("sg_ready"), sem("f_u_full"), sem("f_h_ready")
        h_full, hT_ready, y_ready = sem("f_h_full"), sem("f_hT_ready"), sem("f_y_ready")
        block = stack.enter_context(nc.Block())

        def entry(eng, tab, t, lo, hi):
            return eng.value_load(tab[0:1, bass.ds(t if isinstance(t, int) else eng.snap(t), 1)], min_val=lo, max_val=hi)

        def walk(eng, body):
            body(0, 0, 1)
            with eng.Fori(0, TILES // 2) as i:
                body(2 * i + 1, 1, i + 1)
                body(2 * i + 2, 0, i + 2)

        @block.sync
        def _(sp):
            last_row = rt.rows - P
            sp.wait_ge(plan_ready, 1)

            def load(t, s):
                r = entry(sp, row_i, t, 0, last_row)
                sp.dma_start(xt[s][:], rt.x_rows[bass.ds(r, P), :]).then_inc(x_in[s], 16)

            def store(t, s):
                rows = bass.ds(t * P if isinstance(t, int) else sp.snap(t * P), P)
                sp.wait_ge(y_ready, t + 1)
                sp.dma_start(rt.y_rows[rows, :], yt[s][:]).then_inc(y_out[s], 16)

            def body(t, s, more):
                if more:
                    sp.wait_ge(x_full, t + 1)
                    load(t + 2, s)
                if later(t, 1):
                    store(t - 1, 1 - s)

            load(0, 0)
            load(1, 1)
            body(0, 0, True)
            with sp.Fori(0, TILES // 2 - 1) as i:
                body(2 * i + 1, 1, True)
                body(2 * i + 2, 0, True)
            body(TILES - 2, 1, False)
            body(TILES - 1, 0, False)
            store(TILES - 1, 0)
            for s in range(2):
                sp.wait_ge(y_out[s], 16 * ((TILES + 1 - s) // 2))

        @block.gpsimd
        def _(pool):
            pool.memset(ones[:], 1.0).then_inc(consts, 1)
            pool.iota(tile_no_i[:], pattern=[[1, TILES]], base=0, channel_multiplier=0).then_inc(iotas, 1)
            pool.iota(step_no_i[:], pattern=[[1, MAXT]], base=0, channel_multiplier=0).then_inc(iotas, 1)
            pool.memset(low[:], 0.0).then_inc(consts, 1)
            pool.wait_ge(consts, 2)
            for e in range(E):
                pool.memset(low[:, e, 0:e + 1], 1.0).then_inc(consts, 1)
                pool.memset(base[:, e:e + 1], float(e * rt.region + P)).then_inc(consts, 1)
            for e in range(SLOTS):
                pool.wait_ge(ex.w_in[e], 32)
                pool.sem_inc(w_ready, 1)
            pool.wait_ge(plan_ready, 1)
            for e in range(SLOTS, E):
                n = pool.value_load(te_i[0:1, e - SLOTS:e - SLOTS + 1], min_val=1, max_val=TILES + 1)
                pool.wait_ge(plan_ready, 1)
                pool.wait_ge(tile_done, n)
                ex.load(pool, e)
                pool.wait_ge(ex.w_next[e % SLOTS], 32 * (e // SLOTS))
                pool.sem_inc(w_ready, 1)

        @block.tensor
        def _(pe):
            pe.wait_ge(consts, 1)
            pe.matmul(Cn[:, 0:P], ones[:], rt.acc[:, None, :].to_broadcast([P, P // E, E]), start=True, stop=True).then_inc(cnt_full, 1)

            def turn_x(t, s, n):
                pe.wait_ge(x_in[s], 16 * n)
                if later(t, 1):
                    pe.wait_ge(xT_ready, t)
                for c in range(C):
                    last = pe.transpose(TX[:, c * P:(c + 1) * P], xt[s][:, c * P:(c + 1) * P], ident[:])
                last.then_inc(x_full, 1)

            def turn_h(t):
                pe.wait_ge(h_ready, t + 1)
                if later(t, 1):
                    pe.wait_ge(hT_ready, t)
                for c in range(FC):
                    last = pe.transpose(TH[:, c * P:(c + 1) * P], h[:, c * P:(c + 1) * P], ident[:])
                last.then_inc(h_full, 1)

            def down(t):
                slot = entry(pe, slot_i, t, 0, SLOTS - 1)
                pe.wait_ge(hT_ready, t + 1)
                if later(t, 1):
                    pe.wait_ge(y_ready, t)
                for c in range(FC):
                    last = pe.matmul(Dn[:], hT[:, c, :], ex.wdn[:, slot, c, :], start=(c == 0), stop=(c == FC - 1))
                last.then_inc(tile_done, 1)

            def body(t, s, n):
                e = entry(pe, e_i, t, 0, E - 1)
                slot = entry(pe, slot_i, t, 0, SLOTS - 1)
                pe.wait_ge(xT_ready, t + 1)
                pe.wait_ge(w_ready, pe.snap(e + 1))
                if later(t, 1):
                    pe.wait_ge(sg_ready, t)
                for c in range(C):
                    last = pe.matmul(G[:], xT[s][:, c, :], ex.wgu[:, slot, c, 0:F], start=(c == 0), stop=(c == C - 1))
                last.then_inc(g_full, 1)
                if later(t, 1):
                    turn_h(t - 1)
                for c in range(C):
                    last = pe.matmul(U[:], xT[s][:, c, :], ex.wgu[:, slot, c, F:2 * F], start=(c == 0), stop=(c == C - 1))
                last.then_inc(u_full, 1)
                if n is not None:
                    turn_x(t + 1, 1 - s, n)
                if later(t, 1):
                    down(t - 1)

            pe.sem_inc(tile_done, 1)
            pe.wait_ge(plan_ready, 1)
            turn_x(0, 0, 1)
            body(0, 0, 1)
            with pe.Fori(0, TILES // 2 - 1) as i:
                body(2 * i + 1, 1, i + 2)
                body(2 * i + 2, 0, i + 2)
            body(TILES - 2, 1, (TILES + 1) // 2)
            body(TILES - 1, 0, None)
            turn_h(TILES - 1)
            down(TILES - 1)

        @block.scalar
        def _(act):
            def take_x(t, s):
                act.wait_ge(x_full, t + 1)
                if later(t, 2):
                    act.wait_ge(u_full, t - 1)
                act.copy(xT[s][:], TX[:].rearrange("p (c i) -> p c i", c=C)).then_inc(xT_ready, 1)

            def take_h(t):
                act.wait_ge(h_full, t + 1)
                act.wait_ge(tile_done, t + 1)
                act.copy(hT[:], TH[:].rearrange("p (c i) -> p c i", c=FC)).then_inc(hT_ready, 1)

            def body(t, s, more):
                act.wait_ge(g_full, t + 1)
                act.wait_ge(h_ready, t)
                act.activation(sg[:], G[:], ACT.Silu).then_inc(sg_ready, 1)
                if later(t, 1):
                    take_h(t - 1)
                if more:
                    take_x(t + 1, 1 - s)

            take_x(0, 0)
            body(0, 0, True)
            with act.Fori(0, TILES // 2 - 1) as i:
                body(2 * i + 1, 1, True)
                body(2 * i + 2, 0, True)
            body(TILES - 2, 1, True)
            body(TILES - 1, 0, False)
            take_h(TILES - 1)

        @block.vector
        def _(dve):
            n = 0

            def then(*ops):
                nonlocal n
                for op in ops:
                    op.then_inc(plan_step, 1)
                n += len(ops)
                dve.wait_ge(plan_step, n)

            dve.wait_ge(iotas, 2)
            dve.wait_ge(consts, 2 + 2 * E)
            dve.wait_ge(cnt_full, 1)
            then(dve.tensor_copy(tile_no[:], tile_no_i[:]), dve.tensor_copy(step_no[:], step_no_i[:]),
                 dve.tensor_copy(cnt[:], Cn[:, 0:E]))
            then(dve.tensor_scalar(step_no[:], step_no[:], float(P), None, ALU.mult))
            then(dve.tensor_tensor(more[:], cnt[:, :, None].to_broadcast([P, E, MAXT]),
                                   step_no[:, None, :].to_broadcast([P, E, MAXT]), ALU.is_gt))
            then(dve.tensor_reduce(nt[:], more[:], axis=AX.X, op=ALU.add))
            then(dve.tensor_tensor(upto[:], low[:], nt[:, None, :].to_broadcast([P, E, E]), ALU.mult))
            then(dve.tensor_reduce(te[:], upto[:], axis=AX.X, op=ALU.add))
            then(dve.tensor_tensor(base[:], base[:], cnt[:], ALU.add),
                 dve.tensor_scalar(te_i[:], te[:], 1.0, None, ALU.add),
                 dve.memset(first_row[:, E:E + 1], float(E * rt.region - P * (TILES - rt.spare))))
            then(dve.scalar_tensor_tensor(first_row[:, 0:E], te[:], -float(P), base[:], ALU.mult, ALU.add))
            then(dve.tensor_tensor(jump[:], first_row[:, 1:E + 1], first_row[:, 0:E], ALU.subtract))
            then(dve.tensor_tensor(past[:], tile_no[:, :, None].to_broadcast([P, TILES, E]),
                                   te[:, None, :].to_broadcast([P, TILES, E]), ALU.is_ge))
            then(dve.tensor_tensor(hop[:], past[:], jump[:, None, :].to_broadcast([P, TILES, E]), ALU.mult),
                 dve.tensor_reduce(ef[:], past[:], axis=AX.X, op=ALU.add))
            then(dve.tensor_reduce(rowf[:], hop[:], axis=AX.X, op=ALU.add),
                 dve.tensor_scalar(ef[:], ef[:], float(E - 1), None, ALU.min))
            then(dve.tensor_scalar(rowf[:], rowf[:], first_row[:, 0:1], None, ALU.add),
                 dve.tensor_scalar(s3[:], ef[:], float(SLOTS), -float(SLOTS), ALU.is_ge, ALU.mult),
                 dve.tensor_scalar(s6[:], ef[:], float(2 * SLOTS), -float(SLOTS), ALU.is_ge, ALU.mult))
            then(dve.scalar_tensor_tensor(rowf[:], tile_no[:], float(P), rowf[:], ALU.mult, ALU.add),
                 dve.tensor_tensor(slotf[:], s3[:], s6[:], ALU.add))
            then(dve.tensor_tensor(slotf[:], slotf[:], ef[:], ALU.add))
            then(dve.tensor_copy(row_i[:], rowf[:]), dve.tensor_copy(e_i[:], ef[:]), dve.tensor_copy(slot_i[:], slotf[:]))
            dve.sem_inc(plan_ready, 1)

            def gate(t, s):
                dve.wait_ge(u_full, t + 1)
                dve.wait_ge(sg_ready, t + 1)
                if later(t, 1):
                    dve.wait_ge(h_full, t)
                dve.tensor_tensor(h[:], U[:], sg[:], ALU.mult).then_inc(h_ready, 1)

            def take_y(t, s, stored):
                dve.wait_ge(tile_done, t + 2)
                if later(t, 2):
                    dve.wait_ge(y_out[s], 16 * stored)
                dve.tensor_copy(yt[s][:], Dn[:]).then_inc(y_ready, 1)

            gate(0, 0)
            gate(1, 1)
            take_y(0, 0, 0)
            gate(2, 0)
            take_y(1, 1, 0)
            with dve.Fori(1, TILES // 2) as i:
                gate(2 * i + 1, 1)
                take_y(2 * i, 0, i)
                gate(2 * i + 2, 0)
                take_y(2 * i + 1, 1, i)
            take_y(TILES - 1, 0, TILES // 2)


def combine(nc, sh, rt, out):
    D, B, E = sh.D, sh.B, sh.E
    TILES, ST, BUFS = sh.N // P, P // sh.B, 4
    EPS = 1e-9
    with ExitStack() as stack:
        def sb(name, shape, dt=F32):
            return stack.enter_context(nc.sbuf_tensor(name, shape, dt))

        def sem(name):
            return stack.enter_context(nc.semaphore(name))

        rs = sb("c_rs", [P, TILES])
        total = sb("c_total", [P, TILES])
        part = sb("c_part", [P, TILES, 2])
        hot = sb("c_hot", [P, 2 * TILES, E])
        first = sb("c_first", [P, 2 * TILES])
        place = sb("c_place", [P, 2 * TILES], I32)
        y = [[sb(f"c_y{s}{w}", [P, D]) for w in range(2)] for s in range(BUFS)]
        y_in = [sem(f"c_y_in{s}") for s in range(BUFS)]
        place_step = sem("c_place_step")
        w_step, first_added, o_ready, o_out = sem("c_w_step"), sem("c_first_added"), sem("c_o_ready"), sem("c_o_out")
        block = stack.enter_context(nc.Block())
        out_tiles = out.rearrange("b (k t) d -> k t b d", t=ST)

        @block.gpsimd
        def _(pool):
            pool.wait_ge(place_step, 4)
            for k in range(TILES):
                s = k % BUFS
                if k >= BUFS:
                    pool.wait_ge(o_ready, k - BUFS + 1)
                for w in range(2):
                    pool.indirect_dma_start(out=y[s][w][:], out_offset=None, in_=rt.y_rows,
                                            in_offset=bass.IndirectOffsetOnAxis(ap=place[:, 2 * k + w:2 * k + w + 1], axis=0)
                                            ).then_inc(y_in[s], 16)

        @block.vector
        def _(dve):
            picked = rt.picks[:, :, 2:4]
            dve.tensor_tensor(hot[:].rearrange("p (k w) e -> p k w e", w=2), picked[:, :, :, None].to_broadcast([P, TILES, 2, E]),
                              rt.rev[:, None, None, :].to_broadcast([P, TILES, 2, E]), ALU.is_equal).then_inc(place_step, 1)
            dve.wait_ge(place_step, 1)
            dve.tensor_tensor(hot[:], hot[:], rt.first_row[:, None, 0:E].to_broadcast([P, 2 * TILES, E]), ALU.mult).then_inc(place_step, 1)
            dve.wait_ge(place_step, 2)
            dve.tensor_reduce(first[:], hot[:], axis=AX.X, op=ALU.add).then_inc(place_step, 1)
            dve.wait_ge(place_step, 3)
            dve.tensor_tensor(place[:], rt.places[:].rearrange("p k w -> p (k w)"), first[:], ALU.subtract).then_inc(place_step, 1)
            dve.reciprocal(rs[:], rt.picks[:, :, 4]).then_inc(w_step, 1)
            dve.wait_ge(w_step, 1)
            dve.tensor_tensor(part[:], rt.picks[:, :, 0:2], rs[:, :, None].to_broadcast([P, TILES, 2]), ALU.mult).then_inc(w_step, 1)
            dve.wait_ge(w_step, 2)
            for i in range(2):
                n = 2 + 4 * i
                dve.tensor_reduce(total[:], part[:], axis=AX.X, op=ALU.add).then_inc(w_step, 1)
                dve.wait_ge(w_step, n + 1)
                dve.tensor_scalar(total[:], total[:], EPS, None, ALU.add).then_inc(w_step, 1)
                dve.wait_ge(w_step, n + 2)
                dve.reciprocal(rs[:], total[:]).then_inc(w_step, 1)
                dve.wait_ge(w_step, n + 3)
                dve.tensor_tensor(part[:], part[:], rs[:, :, None].to_broadcast([P, TILES, 2]), ALU.mult).then_inc(w_step, 1)
                dve.wait_ge(w_step, n + 4)
            for k in range(TILES):
                s = k % BUFS
                x2 = rt.x2[:, k, :]
                dve.wait_ge(y_in[s], 32 * (k // BUFS + 1))
                dve.scalar_tensor_tensor(x2, y[s][0][:], part[:, k, 0:1], x2, ALU.mult, ALU.add).then_inc(first_added, 1)
                dve.wait_ge(first_added, k + 1)
                dve.scalar_tensor_tensor(x2, y[s][1][:], part[:, k, 1:2], x2, ALU.mult, ALU.add).then_inc(o_ready, 1)

        @block.sync
        def _(sp):
            for k in range(TILES):
                sp.wait_ge(o_ready, k + 1)
                sp.dma_start(out_tiles[k], rt.x2[:, k, :]).then_inc(o_out, 16)
            sp.wait_ge(o_out, 16 * TILES)


def program(nc, x, ctx, w_sim, b_sim, W_qv, b_qv, decay, Wr, br, Wg, bg, Wo, bo, ln_w, ln_b, gate_w, gate_up, down, out):
    sh = Shapes(x, ctx, gate_w)
    C = sh.C
    x1 = nc.dram_tensor("x1", (sh.PAIRS, P, sh.D), F32, kind="Internal").ap()
    u_d = nc.dram_tensor("u", (C * sh.B, sh.L, P), F32, kind="Internal").ap()
    c_d = nc.dram_tensor("c", (C * sh.B, sh.L, P), F32, kind="Internal").ap()
    with ExitStack() as stack:
        ident = stack.enter_context(nc.sbuf_tensor("ident", [P, P], F32))
        make_identity(nc, ident)
        cross_attention(nc, sh, ident, x.rearrange("(p b) l d -> p (b l) d", b=2), ctx.rearrange("(p b) j d -> p b j d", b=2),
                        w_sim, b_sim, W_qv, b_qv, x1)
        recurrence_gates(nc, sh, ident, x1, Wg, bg, br, decay, u_d, c_d)
        rt = Routing(nc, sh, stack)
        ex = Experts(nc, sh, gate_up, down, stack)
        recurrence(nc, sh, ident, x1, u_d, c_d, decay, Wr, Wo, bo, ln_w, ln_b, gate_w, rt, ex)
        experts(nc, sh, ident, ex, rt)
        combine(nc, sh, rt, out)


_INS = ["x", "ctx_1024", "L0_xattn_w_sim", "L0_xattn_b_sim", "L0_xattn_W_qv", "L0_xattn_b_qv",
        "L0_attn_decay", "L0_attn_Wr", "L0_attn_br", "L0_attn_Wg", "L0_attn_bg", "L0_attn_Wo", "L0_attn_bo",
        "L0_attn_ln_w", "L0_attn_ln_b", "L0_ffn_gate_w", "L0_ffn_gate_up_proj", "L0_ffn_down_proj"]


def kernel(**inputs):
    import numpy as _np
    import concourse.bacc as _bacc
    from concourse.bass_utils import run_bass_kernel_spmd as _run

    nc = _bacc.Bacc("TRN2", target_bir_lowering=False, num_devices=1)
    arrays, args = {}, []
    for name in _INS:
        a = _np.ascontiguousarray(inputs[name])
        arrays[f"in_{name}_dram"] = a
        args.append(nc.dram_tensor(f"in_{name}_dram", a.shape, mybir.dt.from_np(a.dtype), kind="ExternalInput").ap())
    out = nc.dram_tensor("out_0_dram", inputs["x"].shape, F32, kind="ExternalOutput").ap()
    program(nc, *args, out)
    r = _run(nc, [arrays], core_ids=[0])
    return r.results[0]["out_0_dram"]
```

```python
from contextlib import ExitStack

import concourse.bass as bass
from concourse import mybir

F32 = mybir.dt.float32
F32R = mybir.dt.float32r
BF16 = mybir.dt.bfloat16
I32 = mybir.dt.int32
U32 = mybir.dt.uint32
ALU = mybir.AluOpType
ACT = mybir.ActivationFunctionType
AX = mybir.AxisListType

P = 128
LN_EPS = 1e-5


class Shapes:

    def __init__(self, x, ctx, gate_w):
        self.B, self.L, self.D = x.shape
        self.J = ctx.shape[1]
        self.E = gate_w.shape[0]
        self.N = self.B * self.L
        self.C = self.D // P
        self.PAIRS = self.N // P
        self.JT = -(-self.J // P)
        self.JMAIN = (self.JT - 1) * P
        self.JTAIL = self.J - self.JMAIN
        assert P == 2 * self.L and self.D == 4 * P and self.B == 32 and self.JT == 13


def bcast_row(vec):
    return vec.rearrange("(o d) -> o d", o=1).to_broadcast([P, vec.shape[0]])


BLOCKS = [(0, 3, 0, 0), (3, 3, 1, 0), (6, 3, 2, 0), (9, 2, 3, 0), (11, 2, 3, 256)]
NBLK = len(BLOCKS)
BANK_TILES = [(0, 3), (3, 3), (6, 3), (9, 4)]
TWO_SLOTS = 2
AV_ORDER = [t for j in [*range(TWO_SLOTS, NBLK), *range(TWO_SLOTS)] for t in range(BLOCKS[j][0], BLOCKS[j][0] + BLOCKS[j][1])]
AT_TILES = [(0, 4), (4, 3), (7, 3), (10, 3)]


def turn_order(front, back):
    bank = ([], [])
    for j, (_, n, _, _) in enumerate(BLOCKS):
        for u in range(2 * n if front else 0):
            bank[u % 2].append(f"ctx{j}.{u}")
    if front:
        bank[0].insert(1, "hc")
    if back:
        bank[1].insert(1 if front else 0, "trow")
        bank[0].append("hqh")
    for q in range(len(AT_TILES) if front else 0):
        bank[q % 2].append(f"probs{q}")
    return bank


FIRST_TURNS = turn_order(True, False)
FULL_TURNS = turn_order(True, True)
LAST_TURNS = turn_order(False, True)


def turn(bank, name, p, step):
    if step == "first":
        return FIRST_TURNS[bank].index(name)
    order = LAST_TURNS if step == "last" else FULL_TURNS
    return len(FIRST_TURNS[bank]) + p * len(FULL_TURNS[bank]) + order[bank].index(name)


def before(p):
    return p - 1, "first" if isinstance(p, int) and p == 0 else "full"


def later(p, n):
    return not isinstance(p, int) or p >= n


def cross_attention(nc, sh, ident, x, ctx, w_sim, b_sim, W_qv, b_qv, x1):
    D, C, JT, JMAIN, JTAIL, PAIRS = sh.D, sh.C, sh.JT, sh.JMAIN, sh.JTAIL, sh.PAIRS
    BW = 3 * P
    sems = []

    with ExitStack() as stack:
        def sb(name, shape, dt=F32):
            return stack.enter_context(nc.sbuf_tensor(name, shape, dt))

        def sem(name):
            sems.append(nc.alloc_semaphore(name=name))
            return sems[-1]

        TWO = BLOCKS[TWO_SLOTS][0]
        ctx_two = [[sb(f"ctx_two{s}{b}", [P, TWO, D]) for b in range(2)] for s in range(2)]
        ctx_one = [sb(f"ctx_one{b}", [P, JT - TWO, D]) for b in range(2)]
        ctxT = [sb(f"ctxT{s}", [P, 2, C, BW]) for s in range(2)]
        w0, w3 = sb("w0", [P, C, D]), sb("w3", [P, C, D])
        w12H, w12L = sb("w12H", [P, 2 * C, D], F32R), sb("w12L", [P, 2 * C, D], F32R)
        x_sb = sb("x_sb", [P, D])
        xb = [sb(f"xb{s}", [P, D]) for s in range(2)]
        tok_rows = sb("tok_rows", [P, D])
        hcT = [sb(f"hcT{s}", [P, C, P]) for s in range(2)]
        qT = sb("qT", [P, C, P])
        probs = sb("probs", [P, JT * P])
        probsT = sb("probsT", [P, JT, P])
        hqhH, hqhL = sb("hqhH", [P, C, P], F32R), sb("hqhL", [P, C, P], F32R)
        wb = sb("wb", [P, 2, C, D])
        f2H, f2L = sb("f2H", [P, C, P], F32R), sb("f2L", [P, C, P], F32R)
        f3 = sb("f3", [P, C, P])
        w1_b = sb("w1_b", [P, D])
        bqv_b = sb("bqv_b", [P, D])
        w2T = sb("w2T", [P, C])
        w3T = sb("w3T", [P, C])
        bsim_b = sb("bsim_b", [P, 1])
        stats = sb("stats", [P, 6])
        mv = sb("mv", [P, 2])
        ve = sb("ve", [P, 1])
        nmean = sb("nmean", [P, 1])
        rstd = sb("rstd", [P, 1])
        mhalf = sb("mhalf", [P, 1])
        s1 = sb("s1", [P, 1])
        mx4 = sb("mx4", [P, 4])
        mx = sb("mx", [P, 1])
        nmx = sb("nmx", [P, 1])
        z4 = sb("z4", [P, 4])
        zsum = sb("zsum", [P, 1])
        rz = sb("rz", [P, 1])
        tcol = sb("tcol", [P, 1])
        nrm = sb("nrm", [1, 2])
        erow = sb("erow", [1, P])
        rsum = sb("rsum", [1, 2])
        rinv = sb("rinv", [1, 2])
        brow = sb("brow", [1, P])
        ones1 = sb("ones1", [1, P])
        hcb = sb("hcb", [P, C, 2])

        S = stack.enter_context(nc.psum_tensor("S", [P, 4, 512], F32))
        T = [stack.enter_context(nc.psum_tensor(f"T{s}", [P, 512], F32)) for s in range(2)]
        O = stack.enter_context(nc.psum_tensor("O", [P, 512], F32))
        Y = stack.enter_context(nc.psum_tensor("Y", [P, 512], F32))

        const_in = sem("const_in")
        wqv_in, w12_in = sem("wqv_in"), sem("w12_in")
        w12H_ready, w12L_ready = sem("w12H_ready"), sem("w12L_ready")
        hqhH_ready, hqhL_ready, f2H_ready = sem("hqhH_ready"), sem("hqhL_ready"), sem("f2H_ready")
        x_in = sem("x_in")
        ctx_in = [[sem(f"ctx_in{s}_{j}") for j in range(TWO_SLOTS)] for s in range(2)]
        ctx_one_in = [sem(f"ctx_one_in{j}") for j in range(TWO_SLOTS, NBLK)]
        av_one = sem("av_one")
        x1_out = sem("x1_out")
        consts = sem("consts")
        stat_done = sem("stat_done")
        ln_ready = sem("ln_ready")
        rstd_ready = sem("rstd_ready")
        hc_ready = sem("hc_ready")
        xb_ready = sem("xb_ready")
        q_ready = sem("q_ready")
        s1_ready = sem("s1_ready")
        t_full = [sem(f"t_full{s}") for s in range(2)]
        t_free = [sem(f"t_free{s}") for s in range(2)]
        qk_done = sem("qk_done")
        mx_done = sem("mx_done")
        nmx_ready = sem("nmx_ready")
        tcol_ready = sem("tcol_ready")
        exp_done = sem("exp_done")
        z_done = sem("z_done")
        rz_ready = sem("rz_ready")
        nrm_done = sem("nrm_done")
        erow_ready = sem("erow_ready")
        bsm_done = sem("bsm_done")
        brow_ready = sem("brow_ready")
        brow_full, hcb_step = sem("brow_full"), sem("hcb_step")
        hcb_done = sem("hcb_done")
        f2_ready = sem("f2_ready")
        wb_step = sem("wb_step")
        av_done = sem("av_done")
        hqh_ready = sem("hqh_ready")
        y_done = sem("y_done")
        x1_ready = sem("x1_ready")

        def first(p):
            return isinstance(p, int) and p == 0

        def tile_rows(t):
            return P if t < JT - 1 else JTAIL

        def bank_cols(k):
            t0, n = BANK_TILES[k]
            return sum(tile_rows(t) for t in range(t0, t0 + n))

        def context(s, b, t):
            return (ctx_two[s][b], t) if t < TWO else (ctx_one[b], t - TWO)

        def block_dmas(j):
            t0, n, _, _ = BLOCKS[j]
            return 2 * (2 if t0 + n == JT else 1)

        def block_cols(j):
            t0, n, _, _ = BLOCKS[j]
            return sum(tile_rows(t) for t in range(t0, t0 + n))

        def steps(eng, body):
            body(-1, 0, "first")
            body(0, 0, "full")
            with eng.Fori(0, (PAIRS - 2) // 2) as i:
                body(2 * i + 1, 1, "full")
                body(2 * i + 2, 0, "full")
            body(PAIRS - 1, 1, "last")

        block = stack.enter_context(nc.Block())

        @block.sync
        def _(sp):
            def load_x(row):
                sp.dma_start(x_sb[:], x[row]).then_inc(x_in, 16)

            def load_block(j, s, pair):
                t0, n, _, _ = BLOCKS[j]
                done = ctx_in[s][j] if j < TWO_SLOTS else ctx_one_in[j - TWO_SLOTS]
                for b in range(2):
                    src = ctx[pair, b]
                    dst, i = context(s, b, t0)
                    full = min(n, JT - 1 - t0)
                    sp.dma_start(dst[:, i:i + full, :],
                                 src[0:JMAIN, :].rearrange("(p t) d -> p t d", t=JT - 1)[:, t0:t0 + full, :]).then_inc(done, 16)
                    if full < n:
                        sp.dma_start(dst[0:JTAIL, i + full, :], src[JMAIN:sh.J, :]).then_inc(done, 16)

            load_x(0)
            sp.dma_start(w1_b[:], bcast_row(w_sim[0:D])).then_inc(const_in, 16)
            with nc.allow_non_contiguous_dma(reason="two small weight vectors, a column for each chunk"):
                sp.dma_start(w2T[:], w_sim[D:2 * D].rearrange("(c p) -> p c", p=P)).then_inc(const_in, 16)
                sp.dma_start(w3T[:], w_sim[2 * D:3 * D].rearrange("(c p) -> p c", p=P)).then_inc(const_in, 16)
            sp.dma_start(bsim_b[:], bcast_row(b_sim)).then_inc(const_in, 16)
            sp.dma_start(bqv_b[:], bcast_row(b_qv)).then_inc(const_in, 16)
            for j in range(NBLK):
                load_block(j, 0, 0)
            sp.wait_ge(hc_ready, 1)
            sp.wait_ge(xb_ready, 1)
            load_x(1)
            w_rows = W_qv.rearrange("(k p) e -> p k e", p=P)
            sp.dma_start(wb[:].rearrange("p b c d -> p (b c) d"), w_rows[:, C:3 * C, :]).then_inc(w12_in, 16)
            sp.dma_start(w0[:], w_rows[:, 0:C, :]).then_inc(wqv_in, 16)
            sp.dma_start(w3[:], w_rows[:, 3 * C:4 * C, :]).then_inc(wqv_in, 16)
            for j in range(TWO_SLOTS):
                load_block(j, 1, 1)

            def step(p, s, load, store):
                nxt = p + 1 if isinstance(p, int) else sp.snap(p + 1)
                if load:
                    ahead = p + 2 if isinstance(p, int) else sp.snap(p + 2)
                if store:
                    prev = p - 1 if isinstance(p, int) else sp.snap(p - 1)
                for j in range(TWO_SLOTS, NBLK):
                    sp.wait_ge(av_one, (NBLK - TWO_SLOTS) * p + j - TWO_SLOTS + 1)
                    load_block(j, None, nxt)
                if store:
                    sp.wait_ge(x1_ready, p)
                    sp.dma_start(x1[prev], xb[1 - s][:]).then_inc(x1_out, 16)
                if load:
                    sp.wait_ge(hc_ready, p + 2)
                    sp.wait_ge(xb_ready, p + 2)
                    load_x(ahead)
                    sp.wait_ge(av_done, p + 1)
                    for j in range(TWO_SLOTS):
                        load_block(j, s, ahead)

            step(0, 0, True, False)
            with sp.Fori(0, (PAIRS - 4) // 2) as i:
                step(2 * i + 1, 1, True, True)
                step(2 * i + 2, 0, True, True)
            step(PAIRS - 3, 1, True, True)
            step(PAIRS - 2, 0, False, True)
            sp.wait_ge(x1_ready, PAIRS - 1)
            sp.dma_start(x1[PAIRS - 2], xb[0][:]).then_inc(x1_out, 16)
            sp.wait_ge(x1_ready, PAIRS)
            sp.dma_start(x1[PAIRS - 1], xb[1][:]).then_inc(x1_out, 16)
            sp.wait_ge(x1_out, 16 * PAIRS)

        @block.gpsimd
        def _(pool):
            pool.memset(mhalf[:], -0.5).then_inc(consts, 1)
            pool.memset(ones1[:], 1.0).then_inc(consts, 1)
            pool.wait_ge(consts, 2)
            pool.wait_ge(const_in, 80)

            def body(p, s, step):
                if step != "last":
                    f = p + 1
                    pool.wait_ge(ln_ready, 2 * f + 2)
                    pool.tensor_tensor(rstd[:], ve[:], mhalf[:], ALU.pow).then_inc(rstd_ready, 1)
                    if not (isinstance(f, int) and f < 2):
                        pool.wait_ge(x1_out, 16 * (f - 1))
                    pool.tensor_tensor(xb[1 - s if step != "first" else 0][:], x_sb[:], bqv_b[:], ALU.add).then_inc(xb_ready, 1)
                if step != "first":
                    pool.wait_ge(hcb_done, p + 1)
                    pool.wait_ge(y_done, p)
                    if first(p):
                        pool.wait_ge(wqv_in, 32)
                        pool.wait_ge(w12L_ready, 1)
                    for b in range(2 if step == "full" else 0):
                        pool.tensor_tensor(wb[:, b], w3[:], hcb[:, :, b, None].to_broadcast([P, C, D]),
                                           ALU.mult).then_inc(wb_step, 1)
                    for b in range(2 if step == "full" else 0):
                        pool.wait_ge(wb_step, 4 * p + b + 1)
                        pool.tensor_tensor(wb[:, b], wb[:, b], w0[:], ALU.add).then_inc(wb_step, 1)

            steps(pool, body)

        @block.tensor
        def _(pe):
            def fill(bank, name, p, step):
                pe.wait_ge(t_free[bank], turn(bank, name, p, step))

            def turn_ctx(j, u, p, fs, loads, step):
                t0, n, _, _ = BLOCKS[j]
                t, b, bank = t0 + u // 2, u % 2, u % 2
                rows = tile_rows(t)
                if u == 0 and j < TWO_SLOTS:
                    pe.wait_ge(ctx_in[fs][j], block_dmas(j) * 16 * loads)
                elif u == 0:
                    pe.wait_ge(ctx_one_in[j - TWO_SLOTS], block_dmas(j) * 16 * (p + 2))
                src, i = context(fs, b, t)
                fill(bank, f"ctx{j}.{u}", p, step)
                for c in range(C):
                    last = pe.transpose(T[bank][:, c * P:c * P + rows], src[0:rows, i, c * P:(c + 1) * P],
                                        ident[0:rows, 0:rows])
                last.then_inc(t_full[bank], 1)

            def turn_tile(bank, name, src, p, step):
                fill(bank, name, p, step)
                for c in range(C):
                    last = pe.transpose(T[bank][:, c * P:(c + 1) * P], src[:, c * P:(c + 1) * P], ident[:])
                last.then_inc(t_full[bank], 1)

            def turn_probs(q, p, step):
                t0, n = AT_TILES[q]
                if q == 0:
                    pe.wait_ge(exp_done, 4 * (p + 2))
                fill(q % 2, f"probs{q}", p, step)
                for i in range(n):
                    rows = tile_rows(t0 + i)
                    last = pe.transpose(T[q % 2][0:rows, i * P:(i + 1) * P],
                                        probs[:, (t0 + i) * P:(t0 + i) * P + rows], ident[:])
                last.then_inc(t_full[q % 2], 1)

            def scores(j, p, f, fs, loads, step):
                t0, n, k, col = BLOCKS[j]
                w = block_cols(j)
                buf = ctxT[(j + fs) % 2]
                for bank in range(2):
                    pe.wait_ge(t_free[bank], turn(bank, f"ctx{j}.{2 * n - 2 + bank}", p, step) + 1)
                if j == 0:
                    pe.wait_ge(q_ready, C * (f + 1))
                    pe.wait_ge(exp_done, 4 * f)
                for c in range(C):
                    if j + 1 < NBLK and c < BLOCKS[j + 1][1]:
                        turn_ctx(j + 1, 2 * c, p, fs, loads, step)
                        turn_ctx(j + 1, 2 * c + 1, p, fs, loads, step)
                    for b in range(2):
                        last = pe.matmul(S[64 * b:64 * b + 64, k, col:col + w], qT[:, c, 64 * b:64 * b + 64],
                                         buf[:, b, c, 0:w], start=(c == 0), stop=(c == C - 1))
                last.then_inc(qk_done, 1)

            def product(c, aH, aL, w, start, stop):
                pe.matmul(Y[:], aH[:, c, :], w12H[:, w, :], start=start, stop=False)
                pe.matmul(Y[:], aH[:, c, :], w12L[:, w, :], start=False, stop=False)
                return pe.matmul(Y[:], aL[:, c, :], w12H[:, w, :], start=False, stop=stop)

            def body(p, s, step, loads):
                front, back = step != "last", step != "first"
                f, fs = p + 1, (1 - s) if back else 0
                if back:
                    for bank in range(2):
                        pe.wait_ge(t_free[bank], turn(bank, f"probs{2 + bank}", *before(p)) + 1)
                    pe.wait_ge(hqh_ready, p)
                for n, t in enumerate(AV_ORDER):
                    if n == 1:
                        if front:
                            pe.wait_ge(hc_ready, f + 1)
                            turn_tile(0, "hc", tok_rows, p, step)
                        if back:
                            pe.wait_ge(tcol_ready, p + 1)
                            fill(1, "trow", p, step)
                            pe.transpose(T[1][0:1, 0:P], tcol[:], ident[:]).then_inc(t_full[1], 1)
                    elif front and n in (0, 2, 3):
                        u = 2 * max(n - 1, 0)
                        turn_ctx(0, u, p, fs, loads, step)
                        turn_ctx(0, u + 1, p, fs, loads, step)
                    for b in range(2 if back else 0):
                        rows = tile_rows(t)
                        src, i = context(s, b, t)
                        last = pe.matmul(O[64 * b:64 * b + 64, :], probsT[0:rows, t, 64 * b:64 * b + 64],
                                         src[0:rows, i, :], start=(n == 0), stop=(n == JT - 1))
                    if back and n == 10:
                        pe.wait_ge(x1_ready, p)
                        pe.wait_ge(brow_ready, p + 1)
                        pe.matmul(Y[:, 0:P], ones1[:], brow[:], start=True, stop=True).then_inc(brow_full, 1)
                    if back and t in [t0 + n - 1 for t0, n, _, _ in BLOCKS[TWO_SLOTS:]]:
                        last.then_inc(av_one, 1)
                if back:
                    last.then_inc(av_done, 1)
                if front:
                    scores(0, p, f, fs, loads, step)
                    for j in range(1, NBLK - 1):
                        scores(j, p, f, fs, loads, step)
                if back:
                    pe.wait_ge(hqh_ready, p + 1)
                    turn_tile(0, "hqh", tok_rows, p, step)
                if front:
                    scores(NBLK - 1, p, f, fs, loads, step)
                if back:
                    if first(p):
                        pe.wait_ge(w12L_ready, 1)
                    pe.wait_ge(hcb_step, p + 1)
                    pe.wait_ge(hqhL_ready, p + 1)
                    for c in range(C):
                        product(c, hqhH, hqhL, c, c == 0, False)
                    pe.wait_ge(wb_step, 4 * (p + 1))
                    for c in range(C):
                        if front and c >= 2:
                            turn_probs(c - 2, p, step)
                        for b in range(2):
                            pe.matmul(Y[64 * b:64 * b + 64, :], hcT[s][:, c, 64 * b:64 * b + 64], wb[:, b, c, :],
                                      start=False, stop=False)
                    pe.wait_ge(t_free[0], turn(0, "hqh", p, step) + 1)
                    for c in range(C):
                        if front and c < 2:
                            turn_probs(2 + c, p, step)
                        last = product(c, f2H, f2L, C + c, False, c == C - 1)
                    last.then_inc(y_done, 1)
                elif front:
                    for q in range(len(AT_TILES)):
                        turn_probs(q, p, step)

            body(-1, 0, "first", 1)
            body(0, 0, "full", 1)
            with pe.Fori(0, (PAIRS - 2) // 2) as i:
                body(2 * i + 1, 1, "full", i + 2)
                body(2 * i + 2, 0, "full", i + 2)
            body(PAIRS - 1, 1, "last", None)

        def drain_ctx(eng, copy, bank, j, p, fs, step, only=None):
            t0, n, _, _ = BLOCKS[j]
            buf = ctxT[(j + fs) % 2]
            if not (step == "first" and j < 2):
                eng.wait_ge(qk_done, NBLK * (p + 1) + j - 1)
            for u in range(bank, 2 * n, 2) if only is None else only:
                t = t0 + u // 2
                rows, i = tile_rows(t), u // 2
                eng.wait_ge(t_full[bank], turn(bank, f"ctx{j}.{u}", p, step) + 1)
                copy(buf[:, bank, :, i * P:i * P + rows],
                     T[bank][:].rearrange("p (c j) -> p c j", c=C)[:, :, 0:rows]).then_inc(t_free[bank], 1)

        def drain_probs(eng, copy, bank, p, step):
            eng.wait_ge(av_done, p + 1)
            for q in range(bank, len(AT_TILES), 2):
                t0, n = AT_TILES[q]
                eng.wait_ge(t_full[bank], turn(bank, f"probs{q}", p, step) + 1)
                full = n if t0 + n < JT else n - 1
                last = copy(probsT[:, t0:t0 + full, :], T[bank][:, 0:full * P].rearrange("p (t i) -> p t i", i=P))
                if full < n:
                    last = copy(probsT[0:JTAIL, JT - 1, :], T[bank][0:JTAIL, full * P:n * P])
                last.then_inc(t_free[bank], 1)

        @block.scalar
        def _(act):
            copy = nc.scalar.copy

            def body(p, s, step):
                front, back = step != "last", step != "first"
                f, fs = p + 1, (1 - s) if back else 0
                if first(p):
                    act.wait_ge(w12_in, 16)
                    act.copy(w12H[:], wb[:].rearrange("p b c d -> p (b c) d")).then_inc(w12H_ready, 1)
                if front:
                    drain_ctx(act, copy, 0, 0, p, fs, step, only=(0,))
                    act.wait_ge(t_full[0], turn(0, "hc", p, step) + 1)
                    if later(f, 2):
                        act.wait_ge(y_done, f - 1)
                    act.copy(hcT[fs][:], T[0][:].rearrange("p (c i) -> p c i", c=C)).then_inc(t_free[0], 1)
                    drain_ctx(act, copy, 0, 0, p, fs, step, only=(2, 4))
                if back:
                    act.wait_ge(t_free[1], turn(1, "trow", p, step) + 1)
                    act.wait_ge(brow_ready, p)
                    act.activation(erow[:], erow[:], ACT.Exp).then_inc(erow_ready, 1)
                if front:
                    drain_ctx(act, copy, 0, 1, p, fs, step)
                if back:
                    act.wait_ge(av_done, p + 1)
                    act.wait_ge(rz_ready, p + 1)
                    if front:
                        act.wait_ge(t_free[0], turn(0, "hc", p, step) + 1)
                        act.wait_ge(s1_ready, f + 1)
                    else:
                        act.wait_ge(t_free[0], turn(0, "hqh", *before(p)) + 1)
                    act.activation(tok_rows[:], O[:], ACT.Copy, scale=rz[:, 0:1]).then_inc(hqh_ready, 1)
                if front:
                    for j in range(2, NBLK):
                        drain_ctx(act, copy, 0, j, p, fs, step)
                if back:
                    act.wait_ge(t_full[0], turn(0, "hqh", p, step) + 1)
                    act.wait_ge(y_done, p)
                    act.copy(hqhH[:], T[0][:].rearrange("p (c i) -> p c i", c=C)).then_inc(hqhH_ready, 1)
                    act.wait_ge(f2_ready, p + 1)
                    act.copy(f2H[:], f3[:]).then_inc(f2H_ready, 1)
                if front:
                    act.wait_ge(nmx_ready, f + 1)
                    if back:
                        for bank in range(2):
                            act.wait_ge(t_free[bank], turn(bank, f"probs{2 + bank}", *before(p)) + 1)
                        act.wait_ge(rz_ready, f)
                    for k, (t0, _) in enumerate(BANK_TILES):
                        w = bank_cols(k)
                        act.activation(probs[:, t0 * P:t0 * P + w], S[:, k, 0:w], ACT.Exp, bias=nmx[:, 0:1],
                                       accum_out=z4[:, k:k + 1]).then_inc(exp_done, 1)
                    drain_probs(act, copy, 0, p, step)

            steps(act, body)

        @block.vector
        def _(dve):
            copy = nc.vector.tensor_copy
            dve.wait_ge(const_in, 80)

            def norm_stats(f):
                dve.wait_ge(x_in, 16 * f + 16)
                dve.wait_ge(hc_ready, f)
                dve.bn_stats(stats[:], x_sb[:])
                dve.drain()
                dve.bn_aggr(mv[:], stats[:]).then_inc(stat_done, 1)
                dve.wait_ge(stat_done, f + 1)
                dve.tensor_scalar(ve[:], mv[:, 1:2], LN_EPS, None, ALU.add).then_inc(ln_ready, 1)
                dve.tensor_scalar(nmean[:], mv[:, 0:1], -1.0, None, ALU.mult).then_inc(ln_ready, 1)

            def add_x(p, s):
                dve.wait_ge(y_done, p + 1)
                dve.tensor_tensor(xb[s][:], Y[:], xb[s][:], ALU.add).then_inc(x1_ready, 1)

            def body(p, s, step):
                front, back = step != "last", step != "first"
                f, fs = p + 1, (1 - s) if back else 0
                if front:
                    norm_stats(f)
                if back and later(p, 1):
                    add_x(p - 1, 1 - s)
                if front:
                    dve.wait_ge(rstd_ready, f + 1)
                    if back:
                        if later(p, 1):
                            dve.wait_ge(t_free[0], turn(0, "hqh", *before(p)) + 1)
                        else:
                            dve.wait_ge(t_free[0], turn(0, "hc", *before(p)) + 1)
                        dve.wait_ge(s1_ready, f)
                    dve.tensor_scalar(tok_rows[:], x_sb[:], nmean[:, 0:1], rstd[:, 0:1], ALU.add, ALU.mult).then_inc(hc_ready, 1)
                    drain_ctx(dve, copy, 1, 0, p, fs, step, only=(1,))
                if back:
                    row = T[1][0:1, 0:P].rearrange("o (b i) -> o b i", b=2)
                    dve.wait_ge(t_full[1], turn(1, "trow", p, step) + 1)
                    dve.tensor_reduce(nrm[:], row, axis=AX.X, op=ALU.max, negate=True).then_inc(nrm_done, 1)
                    dve.wait_ge(nrm_done, p + 1)
                    dve.wait_ge(brow_ready, p)
                    dve.tensor_tensor(erow[:].rearrange("o (b i) -> o b i", b=2), row,
                                      nrm[:, :, None].to_broadcast([1, 2, 64]), ALU.add).then_inc(t_free[1], 1)
                if front:
                    drain_ctx(dve, copy, 1, 0, p, fs, step, only=(3, 5))
                    dve.wait_ge(hc_ready, f + 1)
                    dve.wait_ge(tcol_ready, f)
                    if later(p, 1):
                        dve.wait_ge(t_free[0], turn(0, "hqh", *before(p)) + 1)
                    dve.tensor_tensor_reduce(out=f3[:].rearrange("p c i -> p (c i)"), in0=tok_rows[:], in1=w1_b[:], scale=1.0, scalar=0.0,
                                             op0=ALU.mult, op1=ALU.add, accum_out=s1[:]).then_inc(s1_ready, 1)
                    dve.wait_ge(t_free[0], turn(0, "hc", p, step) + 1)
                    dve.wait_ge(qk_done, NBLK * f)
                    for c in range(C):
                        dve.tensor_scalar(qT[:, c, :], hcT[fs][:, c, :], w3T[:, c:c + 1], w2T[:, c:c + 1],
                                          ALU.mult, ALU.add).then_inc(q_ready, 1)
                if back:
                    dve.wait_ge(erow_ready, p + 1)
                    e3 = erow[:].rearrange("o (b i) -> o b i", b=2)
                    dve.tensor_reduce(rsum[:], e3, axis=AX.X, op=ALU.add).then_inc(bsm_done, 1)
                    dve.wait_ge(bsm_done, 2 * p + 1)
                    dve.reciprocal(rinv[:], rsum[:]).then_inc(bsm_done, 1)
                    dve.wait_ge(bsm_done, 2 * p + 2)
                    dve.wait_ge(brow_full, p)
                    dve.tensor_tensor(brow[:].rearrange("o (b i) -> o b i", b=2), e3,
                                      rinv[:, :, None].to_broadcast([1, 2, 64]), ALU.mult).then_inc(brow_ready, 1)
                    dve.wait_ge(brow_full, p + 1)
                    if front:
                        dve.wait_ge(s1_ready, f + 1)
                    else:
                        dve.wait_ge(hcb_done, p)
                    dve.tensor_tensor(f3[:], hcT[s][:], Y[:, None, 0:P].to_broadcast([P, C, P]),
                                      ALU.mult).then_inc(hcb_step, 1)
                    dve.wait_ge(hcb_step, p + 1)
                    dve.wait_ge(wb_step, 4 * p)
                    dve.tensor_reduce(hcb[:], f3[:].rearrange("p c (b i) -> p c b i", b=2), axis=AX.X,
                                      op=ALU.add).then_inc(hcb_done, 1)
                if first(p):
                    dve.wait_ge(w12H_ready, 1)
                    dve.tensor_tensor(w12L[:], wb[:].rearrange("p b c d -> p (b c) d"), w12H[:].bitcast(F32), ALU.subtract).then_inc(w12L_ready, 1)
                if step == "last":
                    dve.wait_ge(hcb_done, p + 1)
                    dve.wait_ge(y_done, p)
                    for b in range(2):
                        for c in range(C):
                            op = dve.scalar_tensor_tensor(wb[:, b, c, :], w3[:, c, :], hcb[:, c, b:b + 1], w0[:, c, :],
                                                          ALU.mult, ALU.add)
                            if c % 2:
                                op.then_inc(wb_step, 1)
                if front:
                    drain_ctx(dve, copy, 1, 1, p, fs, step)
                if front:
                    for j in range(2, NBLK):
                        drain_ctx(dve, copy, 1, j, p, fs, step)
                        bank_max(j - 2, f)
                if back:
                    dve.wait_ge(hqhH_ready, p + 1)
                    dve.wait_ge(hcb_done, p + 1)
                    dve.wait_ge(y_done, p)
                    dve.tensor_tensor(hqhL[:], T[0][:].rearrange("p (c i) -> p c i", c=C), hqhH[:].bitcast(F32),
                                      ALU.subtract).then_inc(hqhL_ready, 1)
                    dve.tensor_tensor(f3[:], hcT[s][:], T[0][:].rearrange("p (c i) -> p c i", c=C),
                                      ALU.mult).then_inc(f2_ready, 1)
                if front:
                    bank_max(3, f)
                    dve.wait_ge(mx_done, 5 * f + 4)
                    dve.tensor_reduce(mx[:], mx4[:], axis=AX.X, op=ALU.max).then_inc(mx_done, 1)
                    dve.wait_ge(mx_done, 5 * f + 5)
                    dve.tensor_scalar(nmx[:], mx[:], -1.0, None, ALU.mult).then_inc(nmx_ready, 1)
                    dve.wait_ge(s1_ready, f + 1)
                    dve.tensor_scalar(tcol[:], mx[:], s1[:, 0:1], bsim_b[:, 0:1], ALU.add, ALU.add).then_inc(tcol_ready, 1)
                if back:
                    dve.wait_ge(f2H_ready, p + 1)
                    dve.tensor_tensor(f2L[:], f3[:], f2H[:].bitcast(F32), ALU.subtract).then_inc(t_free[0], 1)
                if front:
                    dve.wait_ge(exp_done, 4 * f + 4)
                    dve.tensor_reduce(zsum[:], z4[:], axis=AX.X, op=ALU.add).then_inc(z_done, 1)
                    dve.wait_ge(z_done, f + 1)
                    dve.wait_ge(hqh_ready, f)
                    dve.reciprocal(rz[:], zsum[:]).then_inc(rz_ready, 1)
                    drain_probs(dve, copy, 1, p, step)

            def bank_max(k, f):
                dve.wait_ge(qk_done, NBLK * f + (k + 1 if k < 3 else NBLK))
                dve.tensor_reduce(mx4[:, k:k + 1], S[:, k, 0:bank_cols(k)], axis=AX.X, op=ALU.max).then_inc(mx_done, 1)

            steps(dve, body)
            add_x(PAIRS - 1, 1)

    nc.clear_and_free_semaphores(sems)
    nc.all_engine_barrier()


def make_identity(nc, ident):
    with nc.semaphore("ident_zero") as ident_zero, nc.Block() as block:
        @block.gpsimd
        def _(pool):
            pool.memset(ident[:], 0.0).then_inc(ident_zero, 1)
            pool.wait_ge(ident_zero, 1)
            pool.affine_select(out=ident[:], in_=ident[:], compare_op=ALU.not_equal, fill=1.0, base=0,
                               pattern=[[-1, P]], channel_multiplier=1).then_inc(ident_zero, 1)


class RecurrenceWeights:

    def __init__(self, nc, sh, Wr, Wo, stack):
        self.sources = Wr, Wo
        self.Wr, self.Wo = (stack.enter_context(nc.sbuf_tensor(n, [P, sh.C, sh.D], F32)) for n in ("wr_rows", "wo_rows"))
        self.loaded = stack.enter_context(nc.semaphore("recurrence_w_in"))

    def load(self, eng):
        for rows, src in zip((self.Wr, self.Wo), self.sources):
            eng.dma_start(rows[:], src.rearrange("(k p) d -> p k d", p=P)).then_inc(self.loaded, 16)


def recurrence_gates(nc, sh, ident, x1, Wg, bg, br, decay, u_d, c_d, rw):
    D, C, N = sh.D, sh.C, sh.N
    TILES = N // P
    with ExitStack() as stack:
        def sb(name, shape, dt=F32):
            return stack.enter_context(nc.sbuf_tensor(name, shape, dt))

        def sem(name):
            return stack.enter_context(nc.semaphore(name))

        wg_rows = sb("wg_rows", [P, C, D])
        wgT = sb("wgT", [P, C, D])
        bg_b = sb("bg_b", [P, D])
        br_b = sb("br_b", [P, D])
        om_b = sb("om_b", [P, D])
        dec_b = sb("dec_b", [P, D])
        xt = sb("g_xt", [P, TILES, D])
        xn = [sb(f"g_xn{s}", [P, D]) for s in range(2)]
        xnT = [sb(f"g_xnT{s}", [P, C, P]) for s in range(2)]
        zt = [sb(f"zt{s}", [P, D]) for s in range(2)]
        z = [sb(f"z{s}", [P, D]) for s in range(2)]
        xm = [sb(f"xm{s}", [P, D]) for s in range(2)]
        u = [sb(f"g_u{s}", [P, D]) for s in range(2)]
        cc = [sb(f"g_c{s}", [P, D]) for s in range(2)]
        stats = sb("g_stats", [P, 6])
        mv = sb("g_mv", [P, 2])
        ve = sb("g_ve", [P, 1])
        nmean = sb("g_nmean", [P, 1])
        rstd = sb("g_rstd", [P, 1])
        mhalf = sb("g_mhalf", [P, 1])
        T = [stack.enter_context(nc.psum_tensor(f"g_T{s}", [P, 512], F32)) for s in range(2)]
        Z = [stack.enter_context(nc.psum_tensor(f"g_Z{s}", [P, 512], F32)) for s in range(2)]

        w_in = sem("g_w_in")
        row_in = sem("g_row_in")
        x_in = [sem(f"g_x_in{i}") for i in range(3)]
        uc_out = [sem(f"g_uc_out{s}") for s in range(2)]
        half_set = sem("g_half_set")
        om_done = sem("g_om_done")
        wT_full = sem("g_wT_full")
        wT_ready = sem("g_wT_ready")
        stat_done = sem("g_stat_done")
        ln_ready = sem("g_ln_ready")
        rstd_ready = sem("g_rstd_ready")
        xn_ready = sem("g_xn_ready")
        xT_full = sem("g_xT_full")
        xnT_ready = sem("g_xnT_ready")
        z_full = sem("g_z_full")
        zt_ready = sem("g_zt_ready")
        z_ready = sem("g_z_ready")
        xm_ready = sem("g_xm_ready")
        u_ready = sem("g_u_ready")
        c_ready = sem("g_c_ready")
        block = stack.enter_context(nc.Block())

        u_rows = u_d.rearrange("(c b) l e -> (b l) c e", c=C)
        c_rows = c_d.rearrange("(c b) l e -> (b l) c e", c=C)

        @block.sync
        def _(sp):
            sp.dma_start(wg_rows[:], Wg.rearrange("(k p) d -> p k d", p=P)).then_inc(w_in, 16)
            sp.dma_start(xt[:, 0, :], x1[0]).then_inc(x_in[0], 16)
            sp.dma_start(bg_b[:], bcast_row(bg)).then_inc(row_in, 16)
            sp.dma_start(br_b[:], bcast_row(br)).then_inc(row_in, 16)
            sp.dma_start(dec_b[:], bcast_row(decay)).then_inc(row_in, 16)
            for i, (lo, hi) in enumerate(((1, 5), (5, TILES))):
                sp.dma_start(xt[:, lo:hi, :], x1[lo:hi].rearrange("k p d -> p k d")).then_inc(x_in[i + 1], 16)

            rw.load(sp)

            def store(k, s):
                base = bass.ds(k * P, P) if isinstance(k, int) else bass.ds(sp.snap(k * P), P)
                sp.wait_ge(u_ready, k + 1)
                sp.dma_start(u_rows[base], u[s][:].rearrange("p (c e) -> p c e", c=C)).then_inc(uc_out[s], 16)
                sp.wait_ge(c_ready, k + 1)
                sp.dma_start(c_rows[base], cc[s][:].rearrange("p (c e) -> p c e", c=C)).then_inc(uc_out[s], 16)

            with sp.Fori(0, TILES // 2) as i:
                store(2 * i, 0)
                store(2 * i + 1, 1)
            for s in range(2):
                sp.wait_ge(uc_out[s], 32 * (TILES // 2))

        @block.gpsimd
        def _(pool):
            pool.memset(mhalf[:], -0.5).then_inc(half_set, 1)
            pool.wait_ge(half_set, 1)

            def power(k):
                pool.wait_ge(ln_ready, 2 * k + 2)
                pool.tensor_tensor(rstd[:], ve[:], mhalf[:], ALU.pow).then_inc(rstd_ready, 1)

            def less_br(k, s):
                pool.wait_ge(xn_ready, k + 1)
                if later(k, 2):
                    pool.wait_ge(c_ready, k - 1)
                pool.tensor_tensor(xm[s][:], xn[s][:], br_b[:], ALU.subtract).then_inc(xm_ready, 1)

            for k in range(3):
                power(k)
            pool.wait_ge(row_in, 48)
            less_br(0, 0)
            power(3)
            less_br(1, 1)
            with pool.Fori(1, TILES // 2 - 1) as i:
                less_br(2 * i, 0)
                power(2 * i + 2)
                less_br(2 * i + 1, 1)
                power(2 * i + 3)
            less_br(TILES - 2, 0)
            less_br(TILES - 1, 1)

        @block.tensor
        def _(pe):
            pe.wait_ge(w_in, 16)
            for k in range(C):
                if k >= 2:
                    pe.wait_ge(wT_ready, k - 1)
                for c in range(C):
                    last = pe.transpose(T[k % 2][:, c * P:(c + 1) * P], wg_rows[:, k, c * P:(c + 1) * P], ident[:])
                last.then_inc(wT_full, 1)
            pe.wait_ge(wT_ready, C)

            def turn(k, s):
                pe.wait_ge(xn_ready, k + 1)
                if later(k, 2):
                    pe.wait_ge(xnT_ready, k - 1)
                for c in range(C):
                    last = pe.transpose(T[s][:, c * P:(c + 1) * P], xn[s][:, c * P:(c + 1) * P], ident[:])
                last.then_inc(xT_full, 1)

            def gates(k, s):
                pe.wait_ge(xnT_ready, k + 1)
                if later(k, 2):
                    pe.wait_ge(zt_ready, k - 1)
                for c in range(C):
                    last = pe.matmul(Z[s][:], xnT[s][:, c, :], wgT[:, c, :], start=(c == 0), stop=(c == C - 1))
                last.then_inc(z_full, 1)

            turn(0, 0)
            turn(1, 1)
            gates(0, 0)
            with pe.Fori(0, TILES // 2 - 1) as i:
                turn(2 * i + 2, 0)
                gates(2 * i + 1, 1)
                turn(2 * i + 3, 1)
                gates(2 * i + 2, 0)
            gates(TILES - 1, 1)

        @block.scalar
        def _(act):
            act.wait_ge(row_in, 48)
            act.activation(om_b[:], dec_b[:], ACT.Sigmoid).then_inc(om_done, 1)
            for k in range(0, C, 2):
                act.wait_ge(wT_full, k + 1)
                act.copy(wgT[:, :, k * P:(k + 1) * P], T[0][:].rearrange("p (c e) -> p c e", c=C)).then_inc(wT_ready, 1)
                act.wait_ge(wT_full, k + 2)
                act.copy(wgT[:, :, (k + 1) * P:(k + 2) * P], T[1][:].rearrange("p (c e) -> p c e", c=C)).then_inc(wT_ready, 1)

            def drain(k, s):
                act.wait_ge(xT_full, k + 1)
                if later(k, 2):
                    act.wait_ge(z_full, k - 1)
                act.copy(xnT[s][:], T[s][:].rearrange("p (c i) -> p c i", c=C)).then_inc(xnT_ready, 1)

            def gate(k, s):
                act.wait_ge(zt_ready, k + 1)
                if later(k, 2):
                    act.wait_ge(u_ready, k - 1)
                act.activation(z[s][:], zt[s][:], ACT.Sigmoid).then_inc(z_ready, 1)

            drain(0, 0)
            drain(1, 1)
            gate(0, 0)
            with act.Fori(0, TILES // 2 - 1) as i:
                drain(2 * i + 2, 0)
                gate(2 * i + 1, 1)
                drain(2 * i + 3, 1)
                gate(2 * i + 2, 0)
            gate(TILES - 1, 1)

        @block.vector
        def _(dve):
            def one_minus_decay():
                dve.wait_ge(om_done, 1)
                dve.tensor_scalar(om_b[:], om_b[:], -1.0, 1.0, ALU.mult, ALU.add).then_inc(om_done, 1)
                dve.wait_ge(om_done, 2)

            def statistics(k):
                tile = xt[:, k if isinstance(k, int) else dve.snap(k), :]
                if not later(k, 5):
                    dve.wait_ge(x_in[1 if later(k, 1) else 0], 16)
                if later(k, 5):
                    dve.wait_ge(x_in[2], 16)
                if later(k, 1):
                    dve.wait_ge(rstd_ready, k)
                    dve.wait_ge(xn_ready, k)
                dve.bn_stats(stats[:], tile)
                dve.drain()
                dve.bn_aggr(mv[:], stats[:]).then_inc(stat_done, 1)
                dve.wait_ge(stat_done, k + 1)
                dve.tensor_scalar(ve[:], mv[:, 1:2], LN_EPS, None, ALU.add).then_inc(ln_ready, 1)
                dve.tensor_scalar(nmean[:], mv[:, 0:1], -1.0, None, ALU.mult).then_inc(ln_ready, 1)

            def norm(k, s):
                tile = xt[:, k if isinstance(k, int) else dve.snap(k), :]
                dve.wait_ge(rstd_ready, k + 1)
                if later(k, 2):
                    dve.wait_ge(xT_full, k - 1)
                    dve.wait_ge(xm_ready, k - 1)
                dve.tensor_scalar(xn[s][:], tile, nmean[:, 0:1], rstd[:, 0:1], ALU.add, ALU.mult).then_inc(xn_ready, 1)

            def gate(k, s):
                dve.wait_ge(z_full, k + 1)
                if later(k, 2):
                    dve.wait_ge(z_ready, k - 1)
                dve.tensor_tensor(zt[s][:], Z[s][:], bg_b[:], ALU.add).then_inc(zt_ready, 1)

            def products(k, s, stored):
                dve.wait_ge(z_ready, k + 1)
                if later(k, 2):
                    dve.wait_ge(uc_out[s], 32 * stored)
                dve.tensor_tensor(u[s][:], z[s][:], om_b[:], ALU.mult).then_inc(u_ready, 1)
                dve.wait_ge(u_ready, k + 1)
                dve.wait_ge(xm_ready, k + 1)
                dve.tensor_tensor(cc[s][:], u[s][:], xm[s][:], ALU.mult).then_inc(c_ready, 1)

            statistics(0)
            norm(0, 0)
            statistics(1)
            norm(1, 1)
            statistics(2)
            one_minus_decay()
            norm(2, 0)
            gate(0, 0)
            statistics(3)
            norm(3, 1)
            products(0, 0, 0)
            gate(1, 1)
            statistics(4)
            norm(4, 0)
            products(1, 1, 0)
            gate(2, 0)
            with dve.Fori(1, TILES // 2 - 2) as i:
                statistics(2 * i + 3)
                norm(2 * i + 3, 1)
                products(2 * i, 0, i)
                gate(2 * i + 1, 1)
                statistics(2 * i + 4)
                norm(2 * i + 4, 0)
                products(2 * i + 1, 1, i)
                gate(2 * i + 2, 0)
            last = TILES - 1
            statistics(last)
            norm(last, 1)
            products(last - 3, 0, TILES // 2 - 2)
            gate(last - 2, 1)
            products(last - 2, 1, TILES // 2 - 2)
            gate(last - 1, 0)
            products(last - 1, 0, TILES // 2 - 1)
            gate(last, 1)
            products(last, 1, TILES // 2 - 1)


class Routing:

    def __init__(self, nc, sh, stack):
        self.region = P + sh.N
        self.tiles = (2 * sh.N + sh.E * (P - 1)) // P
        self.spare = self.tiles - 2 * sh.N // P
        self.rows = sh.E * self.region + self.spare * P
        tiles, E = sh.N // P, sh.E

        def sb(name, shape, dt=F32):
            return stack.enter_context(nc.sbuf_tensor(name, shape, dt))

        self.x2 = sb("x2", [P, tiles, sh.D])
        self.ew = sb("ew", [P, tiles, E])
        self.rank = sb("rank", [P, tiles, E])
        self.places = sb("places", [P, tiles, 2])
        self.second = sb("second", [P, 2])
        self.acc = sb("acc", [P, E], BF16)
        self.first_row = sb("first_row", [P, E + 1])
        self.row_i, self.slot_i, self.part_i = (sb(n, [P, self.tiles], I32) for n in ("row_i", "slot_i", "part_i"))
        self.te_i = sb("te_i", [P, E], I32)
        self.x_rows = nc.dram_tensor("routed_x", (self.rows, sh.D), F32, kind="Internal").ap()
        self.y_rows = nc.dram_tensor("routed_y", (self.tiles * P, sh.D), F32, kind="Internal").ap()


def recurrence(nc, sh, ident, x1, u_d, c_d, decay, rw, bo, ln_w, ln_b, gate_w, rt, ex):
    D, C, E, B = sh.D, sh.C, sh.E, sh.B
    TILES, ST = sh.N // P, P // B
    TOP_OPS = 7
    PLACE_OPS = 4
    LAG = 6
    with ExitStack() as stack:
        def sb(name, shape, dt=F32):
            return stack.enter_context(nc.sbuf_tensor(name, shape, dt))

        def sem(name):
            return stack.enter_context(nc.semaphore(name))

        def psum(name):
            return stack.enter_context(nc.psum_tensor(name, [P, 512], F32))

        w_perm = [sb(f"w_perm{i}", [P, C, P]) for i in range(2)]
        w_scaled = sb("w_scaled", [P, D])
        w_sum, w_nmean = sb("w_sum", [P, C]), sb("w_nmean", [P, C])
        bo_col = sb("bo_col", [P, C])
        WrT = sb("WrT", [P, C, D])
        gw = sb("gw", [E, D])
        gwT = sb("gwT", [P, C, E])
        lnw_b, lnb_b = sb("lnw_b", [P, D]), sb("lnb_b", [P, D])
        bo_b = sb("bo_b", [P, D])
        dec_h = sb("dec_h", [P, P])
        df_h = sb("df_h", [P, P])
        zero = sb("zero", [P, D])
        tri = sb("tri", [P, P], BF16)
        ones = sb("r_ones", [P, P], BF16)
        ebase = sb("ebase", [P, E])
        mhalf = sb("r_mhalf", [P, 1])
        ut = [sb(f"ut{s}", [P, ST, P]) for s in range(2)]
        ct = [sb(f"ct{s}", [P, ST, P]) for s in range(2)]
        xt = [sb(f"r_xt{s}", [P, D]) for s in range(2)]
        H = sb("H", [P, P])
        m = sb("m", [P, P])
        gd = sb("gd", [P, P])
        g = sb("g", [P, P])
        yT = [sb(f"yT{s}", [P, C, ST, B]) for s in range(2)]
        WoH, WoL = sb("WoH", [P, C, D], F32R), sb("WoL", [P, C, D], F32R)
        yH = [sb(f"yH{s}", [P, C, P], F32R) for s in range(2)]
        yL = [sb(f"yL{s}", [P, C, P], F32R) for s in range(2)]
        xn3 = [sb(f"xn3{s}", [P, D]) for s in range(2)]
        xn3T = sb("xn3T", [P, C, P])
        st2, st3 = sb("st2", [P, 6]), sb("st3", [P, 6])
        mv2, mv3 = sb("mv2", [P, 2]), sb("mv3", [P, 2])
        ve2, ve3 = sb("ve2", [P, 1]), sb("ve3", [P, 1])
        nm3 = sb("nm3", [P, 1])
        rs2 = [sb(f"rs2{s}", [P, 1]) for s in range(2)]
        rs3, nr3 = sb("rs3", [P, 1]), sb("nr3", [P, 1])
        nmx = sb("r_nmx", [P, 1])
        earlier = sb("earlier", [P, E, E])
        ahead, equal = sb("ahead", [P, E, E]), sb("equal", [P, E, E])
        rank, oh = sb("r_rank", [P, E]), sb("oh", [P, E], BF16)
        oh2 = sb("oh2", [P, 2, E])
        row, row2 = sb("row", [P, E]), sb("row2", [P, 2, E])
        xs = [sb(f"xs{s}", [P, D]) for s in range(2)]
        pl = sb("pl", [P, 2])
        pl_i = sb("pl_i", [P, 2], I32)
        zero2 = sb("zero2", [P, 2], I32)
        pli = [sb(f"pli{s}", [P, 2], I32) for s in range(2)]

        tile_no = sb("tile_no", [P, rt.tiles])
        tile_no_i = sb("tile_no_i", [P, rt.tiles], I32)
        step_no = sb("step_no", [P, TILES])
        step_no_i = sb("step_no_i", [P, TILES], I32)
        low = sb("low", [P, E, E])
        base = sb("p_base", [P, E])
        cnt = sb("cnt", [P, E])
        more = sb("more", [P, E, TILES])
        nt = sb("nt", [P, E])
        upto = sb("upto", [P, E, E])
        te = sb("te", [P, E])
        jump = sb("jump", [P, E])
        past = sb("past", [P, rt.tiles, E])
        hop = sb("hop", [P, rt.tiles, E])
        rowf = sb("rowf", [P, rt.tiles])
        ef = sb("ef", [P, rt.tiles])
        s3, s6 = sb("s3", [P, rt.tiles]), sb("s6", [P, rt.tiles])
        slotf = sb("slotf", [P, rt.tiles])

        Pb, Yb, YT, Wb, XT, Lg, Rk = (psum(n) for n in ("Pb", "Yb", "YT", "Wb", "XT", "Lg", "Rk"))

        row_in, decay_in = sem("r_row_in"), sem("r_decay_in")
        zero_set, zero_out = sem("zero_set"), sem("zero_out")
        uc_in = [sem(f"uc_in{s}") for s in range(2)]
        x_in = [sem(f"r_x_in{s}") for s in range(2)]
        consts, df_ready = sem("r_consts"), sem("df_ready")
        w_permuted, gwT_ready = sem("w_permuted"), sem("gwT_ready")
        wT_full, wT_ready = sem("r_wT_full"), sem("r_wT_ready")
        bo_step, bo_full, bo_ready = sem("bo_step"), sem("bo_full"), sem("bo_ready")
        wo_step, woH_ready, woL_ready = sem("wo_step"), sem("woH_ready"), sem("woL_ready")
        pred_full, m_done, gd_done, g_ready = sem("pred_full"), sem("m_done"), sem("gd_done"), sem("g_ready")
        h_ready, yT_ready = sem("h_ready"), sem("yT_ready")
        y_full, st2_done, ln2_ready, rs2_ready = sem("y_full"), sem("st2_done"), sem("ln2_ready"), sem("rs2_ready")
        yH_ready, yL_ready = sem("yH_ready"), sem("yL_ready")
        wo_done, xp_ready, x2_ready = sem("wo_done"), sem("xp_ready"), sem("x2_ready")
        st3_done, ln3_ready, rs3_ready = sem("st3_done"), sem("ln3_ready"), sem("rs3_ready")
        xn3_ready, xn3_full, xn3T_ready = sem("xn3_ready"), sem("xn3_full"), sem("xn3T_ready")
        lg_done, nmx_ready, ex_ready = sem("lg_done"), sem("r_nmx_ready"), sem("ex_ready")
        top_step, pfx_done, place_step, places_ready = sem("top_step"), sem("pfx_done"), sem("place_step"), sem("places_ready")
        pli_ready, xs_ready = sem("pli_ready"), sem("xs_ready")
        plan_consts, iotas, cnt_full, plan_step = sem("plan_consts"), sem("iotas"), sem("cnt_full"), sem("plan_step")
        x_scattered = [sem(f"x_scattered{s}") for s in range(2)]
        block = stack.enter_context(nc.Block())

        x1_tiles = x1.rearrange("k p d -> (k p) d").rearrange("(b k t) d -> k t b d", t=ST, k=TILES)

        def first(k):
            return isinstance(k, int) and k == 0

        def k1(k):
            return isinstance(k, int) and k == 1

        def has(j):
            return not isinstance(j, int) or 0 <= j < TILES

        def walk(eng, body):
            for k in range(LAG):
                body(k, k % 2, True, k // 2 + 1)
            with eng.Fori(LAG // 2, TILES // 2) as i:
                body(2 * i, 0, True, i + 1)
                body(2 * i + 1, 1, True, i + 1)
            for k in range(TILES, TILES + LAG):
                body(k, k % 2, False, None)

        def idx(eng, k):
            return k if isinstance(k, int) else eng.snap(k)

        @block.sync
        def _(sp):
            def load_uc(k, s):
                steps = bass.ds(k * ST, ST) if isinstance(k, int) else bass.ds(sp.snap(k * ST), ST)
                sp.dma_start(ut[s][:], u_d[:, steps, :]).then_inc(uc_in[s], 16)
                sp.dma_start(ct[s][:], c_d[:, steps, :]).then_inc(uc_in[s], 16)

            load_uc(0, 0)
            for c in range(C):
                sp.dma_start(dec_h[c * B:(c + 1) * B, :],
                             decay[c * P:(c + 1) * P].rearrange("(o d) -> o d", o=1).to_broadcast([B, P])).then_inc(decay_in, 16)
            sp.dma_start(lnw_b[:], bcast_row(ln_w)).then_inc(row_in, 16)
            sp.dma_start(lnb_b[:], bcast_row(ln_b)).then_inc(row_in, 16)
            sp.dma_start(gw[:], gate_w).then_inc(row_in, 16)
            sp.dma_start(bo_b[:], bcast_row(bo)).then_inc(row_in, 16)
            load_uc(1, 1)

            def load_x(k, s):
                sp.dma_start(xt[s][:], x1_tiles[k]).then_inc(x_in[s], 16)

            pads = [e * rt.region for e in range(E)] + [E * rt.region + i * P for i in range(rt.spare)]

            def load_ahead(k):
                if k == 0:
                    sp.wait_ge(zero_set, 1)
                for r in pads[k::LAG]:
                    sp.dma_start(rt.x_rows[r:r + P, :], zero[:]).then_inc(zero_out, 16)
                for i in range(3 * k // 2, 3 * (k + 1) // 2):
                    ex.load(sp, i // ex.PARTS, i % ex.PARTS)

            def body(k, s, more):
                nxt = k + 2 if isinstance(k, int) else sp.snap(k + 2)
                cur = idx(sp, k)
                if more:
                    sp.wait_ge(h_ready, ST * k + ST)
                    load_uc(nxt, s)
                if later(k, 2):
                    sp.wait_ge(x2_ready, k - 1)
                load_x(cur, s)

            assert 3 * LAG // 2 == ex.SLOTS * ex.PARTS
            for k in range(LAG):
                body(k, k % 2, True)
                load_ahead(k)
            with sp.Fori(LAG // 2, TILES // 2 - 1) as i:
                body(2 * i, 0, True)
                body(2 * i + 1, 1, True)
            for k in range(TILES - 2, TILES):
                body(k, k % 2, False)
            sp.wait_ge(zero_out, 16 * len(pads))

        @block.gpsimd
        def _(pool):
            pool.memset(mhalf[:], -0.5).then_inc(consts, 1)
            pool.memset(zero[:], 0.0).then_inc(zero_set, 1)
            pool.memset(ones[:], 1.0).then_inc(consts, 1)
            pool.memset(zero2[:], 0).then_inc(consts, 1)
            pool.memset(rt.acc[:], 0.0).then_inc(consts, 1)
            pool.memset(rt.second[:, 0:1], 0.0).then_inc(consts, 1)
            pool.memset(rt.second[:, 1:2], 1.0).then_inc(consts, 1)
            pool.memset(earlier[:], 0.0).then_inc(consts, 1)
            pool.wait_ge(consts, 7)
            for e in range(E):
                pool.memset(ebase[:, e:e + 1], float(e * rt.region + P)).then_inc(consts, 1)
                if e:
                    pool.memset(earlier[:, e, 0:e], 1.0).then_inc(consts, 1)
            pool.wait_ge(consts, 6 + 2 * E)
            pool.affine_select(out=tri[:], in_=ones[:], compare_op=ALU.is_gt, fill=0.0, base=0,
                               pattern=[[1, P]], channel_multiplier=-1).then_inc(consts, 1)
            pool.iota(tile_no_i[:], pattern=[[1, rt.tiles]], base=0, channel_multiplier=0).then_inc(iotas, 1)
            pool.iota(step_no_i[:], pattern=[[1, TILES]], base=0, channel_multiplier=0).then_inc(iotas, 1)
            pool.memset(low[:], 0.0).then_inc(plan_consts, 1)
            pool.wait_ge(plan_consts, 1)
            for e in range(E):
                pool.memset(low[:, e, 0:e + 1], 1.0).then_inc(plan_consts, 1)
                pool.memset(base[:, e:e + 1], float(e * rt.region + P)).then_inc(plan_consts, 1)
            pool.wait_ge(df_ready, 1)

            def scatter(j, s, which):
                if which == 0:
                    pool.wait_ge(xs_ready, j + 1)
                    pool.wait_ge(places_ready, j + 1)
                    pool.tensor_tensor(pli[s][:], pl_i[:], zero2[:], ALU.add).then_inc(pli_ready, 1)
                    pool.drain()
                pool.indirect_dma_start(out=rt.x_rows,
                                        out_offset=bass.IndirectOffsetOnAxis(ap=pli[s][:, which:which + 1], axis=0),
                                        in_=xs[s][:], in_offset=None).then_inc(x_scattered[s], 16)

            def power2(j, s):
                pool.wait_ge(ln2_ready, j + 1)
                if later(j, 2):
                    pool.wait_ge(x2_ready, j - 1)
                pool.tensor_tensor(rs2[s][:], ve2[:], mhalf[:], ALU.pow).then_inc(rs2_ready, 1)

            def power3(j):
                pool.wait_ge(ln3_ready, 2 * (j + 1))
                if later(j, 1):
                    pool.wait_ge(xn3_ready, j)
                pool.tensor_tensor(rs3[:], ve3[:], mhalf[:], ALU.pow).then_inc(rs3_ready, 1)
                pool.wait_ge(rs3_ready, 2 * j + 1)
                pool.tensor_tensor(nr3[:], nm3[:], rs3[:], ALU.mult).then_inc(rs3_ready, 1)

            def add_bo(j, s, half, loads):
                cols = slice(half * D // 2, (half + 1) * D // 2)
                if half == 0:
                    pool.wait_ge(x_in[s], 16 * loads)
                if first(j):
                    pool.wait_ge(bo_ready, 1)
                pool.tensor_tensor(xt[s][:, cols], xt[s][:, cols], bo_b[:, cols], ALU.add).then_inc(xp_ready, 1)

            def body(k, s, scan, loads):
                for st in range(ST):
                    if scan and not (st == 0 and first(k)):
                        t = ST * k + st
                        pool.wait_ge(h_ready, t)
                        if st == 0:
                            pool.wait_ge(uc_in[s], 32 * loads)
                        pool.tensor_tensor(gd[:], H[:], df_h[:], ALU.mult).then_inc(gd_done, 1)
                        pool.wait_ge(gd_done, t)
                        pool.tensor_tensor(g[:], gd[:], ct[s][:, st, :], ALU.add).then_inc(g_ready, 1)
                    if st == 0 and has(k - 6):
                        scatter(k - 6, s, 1)
                    if st == 1 and has(k - 3):
                        power3(k - 3)
                    if st == 2 and has(k - 1):
                        power2(k - 1, 1 - s)
                    if st in (1, 2) and has(k - 2):
                        add_bo(k - 2, s, st - 1, loads - 1 if scan else k // 2)
                    if st == 3 and has(k - 5):
                        scatter(k - 5, 1 - s, 0)

            walk(pool, body)
            for s in range(2):
                pool.wait_ge(x_scattered[s], 16 * TILES)

        @block.tensor
        def _(pe):
            def turn_weight(n):
                pe.wait_ge(w_permuted, n + 1)
                if n >= 2:
                    pe.wait_ge(wT_ready if n < C + 2 else woL_ready, n - 1 if n < C + 2 else n - C - 1)
                for c in range(C):
                    last = pe.transpose((YT, XT)[n % 2][:, c * P:(c + 1) * P], w_perm[n % 2][:, c, :], ident[:])
                last.then_inc(wT_full, 1)

            for n in range(C):
                turn_weight(n)
            pe.wait_ge(wT_ready, C)

            def bo_product(c):
                pe.wait_ge(bo_step, c + 1)
                pe.matmul(Wb[:, c * P:(c + 1) * P], bo_col[:, c:c + 1].to_broadcast([P, P]), ident[:],
                          start=True, stop=True).then_inc(bo_full, 1)

            def turn_router():
                pe.wait_ge(row_in, 64)
                for c in range(C):
                    last = pe.transpose(Lg[:, c * E:(c + 1) * E], gw[:, c * P:(c + 1) * P], ident[0:E, 0:E])
                last.then_inc(wT_full, 1)

            def predict(k, s, st):
                pe.wait_ge(yT_ready, ST * k + st)
                src, prev = (yT[s], st - 1) if st else (yT[1 - s], ST - 1)
                for c in range(C):
                    for o in range(C):
                        last = pe.matmul(Pb[o * B:(o + 1) * B, 0:P], src[:, c, prev, :], WrT[:, c, o * P:(o + 1) * P],
                                         start=(c == 0), stop=(c == C - 1))
                last.then_inc(pred_full, 1)

            def body(k, s, scan, loads):
                for st in range(ST):
                    if scan and not (st == 0 and first(k)):
                        predict(k, s, st)
                    if first(k):
                        turn_weight(C + st)
                        bo_product(st)
                    if k1(k) and st == 0:
                        turn_router()
                    if has(k - 2):
                        if st == 0:
                            pe.wait_ge(yL_ready, k - 1)
                            if has(k - 3):
                                pe.wait_ge(x2_ready, k - 2)
                            if first(k - 2):
                                pe.wait_ge(woL_ready, C)
                        pe.matmul(Wb[:], yH[s][:, st, :], WoH[:, st, :], start=(st == 0), stop=False)
                        pe.matmul(Wb[:], yH[s][:, st, :], WoL[:, st, :], start=False, stop=False)
                        mm = pe.matmul(Wb[:], yL[s][:, st, :], WoH[:, st, :], start=False, stop=(st == C - 1))
                        if st == ST - 1:
                            mm.then_inc(wo_done, 1)
                    if st == 1 and has(k - 5):
                        pe.wait_ge(top_step, TOP_OPS * (k - 4))
                        if has(k - 6):
                            pe.wait_ge(places_ready, k - 5)
                        pe.matmul(Rk[:, 0:P], tri[:], oh[:, None, :].to_broadcast([P, P // E, E]), start=True, stop=False)
                        pe.matmul(Rk[:, 0:P], ones[:], rt.acc[:, None, :].to_broadcast([P, P // E, E]),
                                  start=False, stop=True).then_inc(pfx_done, 1)
                    if st == 0 and has(k - 1):
                        if has(k - 2):
                            pe.wait_ge(st2_done, k - 1)
                        if not scan:
                            pe.wait_ge(yT_ready, ST * k)
                        for c in range(C):
                            last = pe.transpose(Yb[:, c * P:(c + 1) * P], yT[1 - s][:, c].rearrange("p t b -> p (t b)"), ident[:])
                        last.then_inc(y_full, 1)
                    if st == 2 and has(k - 3):
                        pe.wait_ge(xn3_ready, k - 2)
                        if has(k - 4):
                            pe.wait_ge(xn3T_ready, k - 3)
                        for c in range(C):
                            last = pe.transpose(XT[:, c * P:(c + 1) * P], xn3[1 - s][:, c * P:(c + 1) * P], ident[:])
                        last.then_inc(xn3_full, 1)
                    if st == 3 and has(k - 3):
                        pe.wait_ge(xn3T_ready, k - 2)
                        if first(k - 3):
                            pe.wait_ge(gwT_ready, 1)
                        if has(k - 4):
                            pe.wait_ge(ex_ready, k - 3)
                        for c in range(C):
                            last = pe.matmul(Lg[:, 0:P], xn3T[:, c, :], gwT[:, c, None, :].to_broadcast([P, P // E, E]),
                                             start=(c == 0), stop=(c == C - 1))
                        last.then_inc(lg_done, 1)

            walk(pe, body)
            pe.wait_ge(places_ready, TILES)
            pe.matmul(Rk[:, 0:P], ones[:], rt.acc[:, None, :].to_broadcast([P, P // E, E]), start=True, stop=True).then_inc(cnt_full, 1)

        @block.scalar
        def _(act):
            for n in range(C):
                act.wait_ge(wT_full, n + 1)
                act.copy(WrT[:, :, n * P:(n + 1) * P], (YT, XT)[n % 2][:].rearrange("p (c e) -> p c e", c=C)).then_inc(wT_ready, 1)
            act.wait_ge(decay_in, 16 * C)
            act.activation(df_h[:], dec_h[:], ACT.Sigmoid).then_inc(df_ready, 1)

            def take_wo(k):
                act.wait_ge(wT_full, C + k + 1)
                act.copy(WoH[:, :, k * P:(k + 1) * P],
                         (YT, XT)[k % 2][:].rearrange("p (c e) -> p c e", c=C)).then_inc(woH_ready, 1)

            def take_router():
                act.wait_ge(wT_full, 2 * C + 1)
                act.copy(gwT[:], Lg[:, 0:C * E].rearrange("p (c e) -> p c e", c=C)).then_inc(gwT_ready, 1)

            def body(k, s, scan, loads):
                for st in range(ST):
                    if first(k):
                        take_wo(st)
                    if st == 0 and k1(k):
                        take_router()
                    if st == 0 and has(k - 1):
                        if has(k - 3):
                            act.wait_ge(wo_done, k - 2)
                        act.wait_ge(yT_ready, ST * k)
                        act.copy(yH[1 - s][:], yT[1 - s][:].rearrange("p c t b -> p c (t b)")).then_inc(yH_ready, 1)
                    if st == 1 and has(k - 3):
                        j = k - 3
                        tile = rt.x2[:, idx(act, j), :]
                        act.wait_ge(df_ready, 1)
                        act.wait_ge(rs3_ready, 2 * (j + 1))
                        if has(k - 5):
                            act.wait_ge(xs_ready, j - 1)
                        act.activation(xn3[1 - s][:], tile, ACT.Identity, scale=rs3[:, 0:1], bias=nr3[:, 0:1]).then_inc(xn3_ready, 1)
                    if st == 2 and has(k - 4):
                        tile = rt.ew[:, idx(act, k - 4), :]
                        act.wait_ge(df_ready, 1)
                        act.wait_ge(nmx_ready, k - 3)
                        act.activation(tile, Lg[:, 0:E], ACT.Exp, bias=nmx[:, 0:1]).then_inc(ex_ready, 1)
                    if st == 3 and has(k - 4):
                        if has(k - 6):
                            act.wait_ge(x_scattered[s], 32 * (loads - 3) if scan else 32 * ((k - 4) // 2))
                        act.copy(xs[s][:], xn3[s][:]).then_inc(xs_ready, 1)
                    if st == 2 and has(k - 3):
                        act.wait_ge(xn3_full, k - 2)
                        if has(k - 4):
                            act.wait_ge(lg_done, k - 3)
                        act.copy(xn3T[:], XT[:].rearrange("p (c i) -> p c i", c=C)).then_inc(xn3T_ready, 1)
            walk(act, body)

        @block.vector
        def _(dve):
            def permute(n, src):
                if n >= 2:
                    dve.wait_ge(wT_full, n - 1)
                return (w_perm[n % 2][:].rearrange("p q (c r) -> p q c r", r=B),
                        src.rearrange("p (c q r) -> p q c r", q=C, r=B))

            dve.wait_ge(rw.loaded, 32)
            for n in range(C):
                dst, src = permute(n, rw.Wr[:, n])
                dve.tensor_copy(dst, src).then_inc(w_permuted, 1)

            def prepare_wo(k):
                if k == 0:
                    dve.wait_ge(row_in, 64)
                else:
                    dve.wait_ge(w_permuted, C + k)
                dve.tensor_tensor_reduce(out=w_scaled[:], in0=rw.Wo[:, k], in1=lnb_b[:], scale=1.0, scalar=0.0,
                                         op0=ALU.mult, op1=ALU.add, accum_out=bo_col[:, k:k + 1]).then_inc(bo_step, 1)
                dve.wait_ge(bo_step, k + 1)
                dve.tensor_tensor_reduce(out=w_scaled[:], in0=rw.Wo[:, k], in1=lnw_b[:], scale=1.0, scalar=0.0,
                                         op0=ALU.mult, op1=ALU.add, accum_out=w_sum[:, k:k + 1]).then_inc(wo_step, 1)
                dve.wait_ge(wo_step, 2 * k + 1)
                dve.tensor_scalar(w_nmean[:, k:k + 1], w_sum[:, k:k + 1], -1.0 / D, None, ALU.mult).then_inc(wo_step, 1)
                dve.wait_ge(wo_step, 2 * k + 2)
                dst, src = permute(C + k, w_scaled[:])
                dve.tensor_scalar(dst, src, w_nmean[:, k:k + 1], None, ALU.add).then_inc(w_permuted, 1)

            def low_wo(k):
                part = slice(k * P, (k + 1) * P)
                dve.wait_ge(woH_ready, k + 1)
                dve.tensor_tensor(WoL[:, :, part], (YT, XT)[k % 2][:].rearrange("p (c e) -> p c e", c=C),
                                  WoH[:, :, part].bitcast(F32), ALU.subtract).then_inc(woL_ready, 1)

            def add_lnb():
                dve.wait_ge(bo_full, C)
                dve.tensor_tensor(bo_b[:], bo_b[:], Wb[:], ALU.add).then_inc(bo_ready, 1)

            prepare_wo(0)
            dve.wait_ge(consts, 7 + 2 * E)

            def norm_stats(src, st, mv, ve, nm, done, ready, j):
                dve.bn_stats(st[:], src)
                dve.drain()
                dve.bn_aggr(mv[:], st[:]).then_inc(done, 1)
                dve.wait_ge(done, j + 1)
                dve.tensor_scalar(ve[:], mv[:, 1:2], LN_EPS, None, ALU.add).then_inc(ready, 1)
                if nm is not None:
                    dve.tensor_scalar(nm[:], mv[:, 0:1], -1.0, None, ALU.mult).then_inc(ready, 1)

            def rank_experts(j, half):
                n = TOP_OPS * j
                ew = rt.ew[:, idx(dve, j), :]
                other, this = ew[:, None, :].to_broadcast([P, E, E]), ew[:, :, None].to_broadcast([P, E, E])
                if half == 0:
                    dve.wait_ge(ex_ready, j + 1)
                    if later(j, 1):
                        dve.wait_ge(places_ready, j)
                    dve.tensor_tensor(equal[:], other, this, ALU.is_equal).then_inc(top_step, 1)
                    dve.tensor_tensor(ahead[:], other, this, ALU.is_gt).then_inc(top_step, 1)
                    dve.wait_ge(top_step, n + 1)
                    dve.tensor_tensor(equal[:], equal[:], earlier[:], ALU.mult).then_inc(top_step, 1)
                    dve.wait_ge(top_step, n + 3)
                    dve.tensor_tensor(ahead[:], ahead[:], equal[:], ALU.add).then_inc(top_step, 1)
                else:
                    dve.wait_ge(top_step, n + 4)
                    dve.tensor_reduce(rank[:], ahead[:], axis=AX.X, op=ALU.add).then_inc(top_step, 1)
                    dve.wait_ge(top_step, n + 5)
                    dve.tensor_tensor(oh2[:], rank[:, None, :].to_broadcast([P, 2, E]),
                                      rt.second[:, :, None].to_broadcast([P, 2, E]), ALU.is_equal).then_inc(top_step, 1)
                    dve.tensor_scalar(oh[:], rank[:], 2.0, None, ALU.is_lt).then_inc(top_step, 1)
                    dve.tensor_copy(rt.rank[:, idx(dve, j), :], rank[:])

            def row_places(j):
                col = idx(dve, j)
                n = PLACE_OPS * j
                dve.wait_ge(pfx_done, j + 1)
                dve.tensor_tensor(row[:], Rk[:, 0:E], ebase[:], ALU.add).then_inc(place_step, 1)
                dve.tensor_tensor(rt.acc[:], rt.acc[:], oh[:], ALU.add).then_inc(place_step, 1)
                dve.wait_ge(place_step, n + 1)
                dve.tensor_tensor(row2[:], oh2[:], row[:, None, :].to_broadcast([P, 2, E]), ALU.mult).then_inc(place_step, 1)
                dve.wait_ge(place_step, n + 3)
                dve.tensor_reduce(pl[:], row2[:], axis=AX.X, op=ALU.add).then_inc(place_step, 1)
                dve.wait_ge(place_step, n + 4)
                dve.tensor_copy(rt.places[:, col, :], pl[:])
                dve.wait_ge(pli_ready, j)
                dve.tensor_copy(pl_i[:], pl[:]).then_inc(places_ready, 1)

            def body(k, s, scan, loads):
                for st in range(ST):
                    if scan:
                        t = ST * k + st
                        if st == 0:
                            dve.wait_ge(uc_in[s], 32 * loads)
                        if st == 0 and first(k):
                            dve.tensor_copy(H[:], ct[s][:, st, :]).then_inc(h_ready, 1)
                        else:
                            dve.wait_ge(pred_full, t)
                            dve.tensor_tensor(m[:], Pb[:, 0:P], ut[s][:, st, :], ALU.mult).then_inc(m_done, 1)
                            dve.wait_ge(m_done, t)
                            dve.wait_ge(g_ready, t)
                            dve.tensor_tensor(H[:], g[:], m[:], ALU.subtract).then_inc(h_ready, 1)
                        dve.wait_ge(h_ready, t + 1)
                        dve.transpose(yT[s][:, :, st, :], H[:]).then_inc(yT_ready, 1)
                    if first(k):
                        if st < C - 1:
                            prepare_wo(st + 1)
                        if st:
                            low_wo(st - 1)
                    if st == 0 and k1(k):
                        low_wo(C - 1)
                        add_lnb()
                    if st == 0 and has(k - 3):
                        j = k - 3
                        tile = rt.x2[:, idx(dve, j), :]
                        dve.wait_ge(bo_ready, 1)
                        dve.wait_ge(x2_ready, j + 1)
                        if has(k - 4):
                            dve.wait_ge(xn3_ready, j)
                        norm_stats(tile, st3, mv3, ve3, nm3, st3_done, ln3_ready, j)
                    if st == 1 and has(k - 1):
                        j = k - 1
                        dve.wait_ge(y_full, j + 1)
                        if has(k - 2):
                            dve.wait_ge(rs2_ready, j)
                        norm_stats(Yb[:], st2, mv2, ve2, None, st2_done, ln2_ready, j)
                    if st == 2 and has(k - 4):
                        dve.wait_ge(lg_done, k - 3)
                        if has(k - 5):
                            dve.wait_ge(ex_ready, k - 4)
                        dve.tensor_reduce(nmx[:], Lg[:, 0:E], axis=AX.X, op=ALU.max, negate=True).then_inc(nmx_ready, 1)
                    if st == 2 and has(k - 5):
                        row_places(k - 5)
                    if st == 2 and has(k - 1):
                        dve.wait_ge(yH_ready, k)
                        if has(k - 3):
                            dve.wait_ge(wo_done, k - 2)
                        dve.tensor_tensor(yL[1 - s][:], yT[1 - s][:].rearrange("p c t b -> p c (t b)"),
                                          yH[1 - s][:].bitcast(F32), ALU.subtract).then_inc(yL_ready, 1)
                    if st == 3 and has(k - 4):
                        rank_experts(k - 4, 0)
                    if st == 3 and has(k - 2):
                        j = k - 2
                        tile = rt.x2[:, idx(dve, j), :]
                        dve.wait_ge(wo_done, j + 1)
                        dve.wait_ge(xp_ready, 2 * (j + 1))
                        dve.scalar_tensor_tensor(tile, Wb[:], rs2[s][:, 0:1], xt[s][:], ALU.mult, ALU.add).then_inc(x2_ready, 1)
                    if st == 3 and has(k - 4):
                        rank_experts(k - 4, 1)

            walk(dve, body)

            n = 0

            def then(*ops):
                nonlocal n
                for op in ops:
                    op.then_inc(plan_step, 1)
                n += len(ops)
                dve.wait_ge(plan_step, n)

            dve.wait_ge(iotas, 2)
            dve.wait_ge(plan_consts, 1 + 2 * E)
            dve.wait_ge(cnt_full, 1)
            then(dve.tensor_copy(tile_no[:], tile_no_i[:]), dve.tensor_copy(step_no[:], step_no_i[:]),
                 dve.tensor_copy(cnt[:], Rk[:, 0:E]))
            then(dve.tensor_scalar(step_no[:], step_no[:], float(P), None, ALU.mult))
            then(dve.tensor_tensor(more[:], cnt[:, :, None].to_broadcast([P, E, TILES]),
                                   step_no[:, None, :].to_broadcast([P, E, TILES]), ALU.is_gt))
            then(dve.tensor_reduce(nt[:], more[:], axis=AX.X, op=ALU.add))
            then(dve.tensor_tensor(upto[:], low[:], nt[:, None, :].to_broadcast([P, E, E]), ALU.mult))
            then(dve.tensor_reduce(te[:], upto[:], axis=AX.X, op=ALU.add))
            then(dve.tensor_tensor(base[:], base[:], cnt[:], ALU.add),
                 dve.tensor_scalar(rt.te_i[:], te[:], 1.0, None, ALU.add),
                 dve.memset(rt.first_row[:, E:E + 1], float(E * rt.region - P * (rt.tiles - rt.spare))))
            then(dve.scalar_tensor_tensor(rt.first_row[:, 0:E], te[:], -float(P), base[:], ALU.mult, ALU.add))
            then(dve.tensor_tensor(jump[:], rt.first_row[:, 1:E + 1], rt.first_row[:, 0:E], ALU.subtract))
            then(dve.tensor_tensor(past[:], tile_no[:, :, None].to_broadcast([P, rt.tiles, E]),
                                   te[:, None, :].to_broadcast([P, rt.tiles, E]), ALU.is_ge))
            then(dve.tensor_tensor(hop[:], past[:], jump[:, None, :].to_broadcast([P, rt.tiles, E]), ALU.mult),
                 dve.tensor_reduce(ef[:], past[:], axis=AX.X, op=ALU.add))
            then(dve.tensor_reduce(rowf[:], hop[:], axis=AX.X, op=ALU.add),
                 dve.tensor_scalar(ef[:], ef[:], float(E - 1), None, ALU.min))
            then(dve.tensor_scalar(rowf[:], rowf[:], rt.first_row[:, 0:1], None, ALU.add),
                 dve.tensor_scalar(s3[:], ef[:], float(ex.SLOTS), -float(ex.SLOTS), ALU.is_ge, ALU.mult),
                 dve.tensor_scalar(s6[:], ef[:], float(2 * ex.SLOTS), -float(ex.SLOTS), ALU.is_ge, ALU.mult))
            then(dve.scalar_tensor_tensor(rowf[:], tile_no[:], float(P), rowf[:], ALU.mult, ALU.add),
                 dve.tensor_tensor(slotf[:], s3[:], s6[:], ALU.add))
            then(dve.tensor_tensor(slotf[:], slotf[:], ef[:], ALU.add),
                 dve.tensor_scalar(ef[:], ef[:], float(ex.PARTS), None, ALU.mult))
            then(dve.tensor_copy(rt.row_i[:], rowf[:]), dve.tensor_copy(rt.part_i[:], ef[:]), dve.tensor_copy(rt.slot_i[:], slotf[:]))


class Experts:
    SLOTS, PARTS = 3, 3

    def __init__(self, nc, sh, gate_up, down, stack):
        F = down.shape[1]
        assert F == sh.D
        self.F = F
        self.sources = gate_up[:, :, 0:F], gate_up[:, :, F:2 * F], down
        self.low = stack.enter_context(nc.sbuf_tensor("w_low", [P, self.SLOTS, self.PARTS, sh.C, F], F32R))
        self.w_in = [stack.enter_context(nc.semaphore(f"expert_w_in{s}")) for s in range(self.SLOTS)]
        self.w_next = [stack.enter_context(nc.semaphore(f"expert_w_next{s}")) for s in range(self.PARTS)]

    def load(self, eng, e, part):
        s = e % self.SLOTS
        eng.dma_start(self.low[:, s, part].bitcast(F32), self.sources[part][e].rearrange("(c p) f -> p c f", p=P)
                      ).then_inc(self.w_in[s] if e < self.SLOTS else self.w_next[part], 16)


def experts(nc, sh, ident, ex, rt):
    D, C, E, F, SLOTS, PARTS = sh.D, sh.C, sh.E, ex.F, ex.SLOTS, ex.PARTS
    GATE, UP, DOWN = range(PARTS)
    TILES = rt.tiles
    assert TILES % 2 == 1
    with ExitStack() as stack:
        def sb(name, shape, dt=F32):
            return stack.enter_context(nc.sbuf_tensor(name, shape, dt))

        def sem(name):
            return stack.enter_context(nc.semaphore(name))

        def psum(name):
            return stack.enter_context(nc.psum_tensor(name, [P, 512], F32))

        xt = [sb(f"f_xt{s}", [P, D]) for s in range(2)]
        zero = sb("f_zero", [P, F])
        high = sb("w_high", [P, SLOTS, PARTS, C, F], F32R)
        xH = [sb(f"f_xH{s}", [P, C, P], F32R) for s in range(2)]
        xL = [sb(f"f_xL{s}", [P, C, P], F32R) for s in range(2)]
        sg = sb("sg", [P, F])
        h = sb("f_h", [P, F])
        hH, hL = sb("f_hH", [P, C, P], F32R), sb("f_hL", [P, C, P], F32R)
        yt = [sb(f"f_yt{s}", [P, D]) for s in range(2)]
        G, U, Dn, TX, TH = (psum(n) for n in ("f_G", "f_U", "f_Dn", "f_TX", "f_TH"))

        w_parts, w_high, tile_done = sem("w_parts"), sem("w_high_ready"), sem("tile_done")
        zero_set = sem("f_zero_set")
        x_in = [sem(f"f_x_in{s}") for s in range(2)]
        y_out = [sem(f"f_y_out{s}") for s in range(2)]
        x_full, xH_ready, xL_ready = sem("f_x_full"), sem("f_xH_ready"), sem("f_xL_ready")
        g_full, sg_ready, u_full, h_ready = sem("f_g_full"), sem("sg_ready"), sem("f_u_full"), sem("f_h_ready")
        h_full, hH_ready, hL_ready, y_ready = sem("f_h_full"), sem("f_hH_ready"), sem("f_hL_ready"), sem("f_y_ready")
        block = stack.enter_context(nc.Block())

        def entry(eng, tab, t, lo, hi):
            return eng.value_load(tab[0:1, bass.ds(t if isinstance(t, int) else eng.snap(t), 1)], min_val=lo, max_val=hi)

        @block.sync
        def _(sp):
            last_row = rt.rows - P

            def load(t, s):
                r = entry(sp, rt.row_i, t, 0, last_row)
                sp.dma_start(xt[s][:], rt.x_rows[bass.ds(r, P), :]).then_inc(x_in[s], 16)

            def store(t, s):
                rows = bass.ds(t * P if isinstance(t, int) else sp.snap(t * P), P)
                sp.wait_ge(y_ready, t + 1)
                sp.dma_start(rt.y_rows[rows, :], yt[s][:]).then_inc(y_out[s], 16)

            def body(t, s, more):
                if more:
                    sp.wait_ge(x_full, t + 1)
                    load(t + 2, s)
                if later(t, 1):
                    store(t - 1, 1 - s)

            load(0, 0)
            load(1, 1)
            body(0, 0, True)
            with sp.Fori(0, TILES // 2 - 1) as i:
                body(2 * i + 1, 1, True)
                body(2 * i + 2, 0, True)
            body(TILES - 2, 1, False)
            body(TILES - 1, 0, False)
            store(TILES - 1, 0)
            for s in range(2):
                sp.wait_ge(y_out[s], 16 * ((TILES + 1 - s) // 2))

        @block.gpsimd
        def _(pool):
            def split_low(e, part):
                low = ex.low[:, e % SLOTS, part]
                pool.wait_ge(w_high, PARTS * e + part + 1)
                pool.tensor_tensor(low, low.bitcast(F32), high[:, e % SLOTS, part].bitcast(F32), ALU.subtract).then_inc(w_parts, 1)

            pool.memset(zero[:], 0.0).then_inc(zero_set, 1)
            pool.wait_ge(zero_set, 1)
            pool.wait_ge(w_parts, PARTS)
            for e in range(1, E):
                if e < SLOTS:
                    pool.wait_ge(ex.w_in[e], 16 * PARTS)
                else:
                    n = pool.value_load(rt.te_i[0:1, e - SLOTS:e - SLOTS + 1], min_val=1, max_val=TILES + 1)
                    pool.wait_ge(zero_set, 1)
                    pool.wait_ge(tile_done, n)
                    for part in range(PARTS):
                        ex.load(pool, e, part)
                for part in range(PARTS):
                    if e >= SLOTS:
                        pool.wait_ge(ex.w_next[part], 16 * (e - SLOTS + 1))
                    pool.tensor_tensor(high[:, e % SLOTS, part], ex.low[:, e % SLOTS, part].bitcast(F32),
                                       zero[:, None, :].to_broadcast([P, C, F]), ALU.add).then_inc(w_high, 1)
                    split_low(e, part)

        @block.tensor
        def _(pe):
            def turn_x(t, s, n):
                pe.wait_ge(x_in[s], 16 * n)
                if later(t, 1):
                    pe.wait_ge(xL_ready, t)
                for c in range(C):
                    last = pe.transpose(TX[:, c * P:(c + 1) * P], xt[s][:, c * P:(c + 1) * P], ident[:])
                last.then_inc(x_full, 1)

            def turn_h(t):
                pe.wait_ge(h_ready, t + 1)
                if later(t, 1):
                    pe.wait_ge(hL_ready, t)
                for c in range(C):
                    last = pe.transpose(TH[:, c * P:(c + 1) * P], h[:, c * P:(c + 1) * P], ident[:])
                last.then_inc(h_full, 1)

            def product(bank, aH, aL, slot, part):
                for c in range(C):
                    pe.matmul(bank[:], aH[:, c, :], high[:, slot, part, c, :], start=(c == 0), stop=False)
                    pe.matmul(bank[:], aH[:, c, :], ex.low[:, slot, part, c, :], start=False, stop=False)
                    last = pe.matmul(bank[:], aL[:, c, :], high[:, slot, part, c, :], start=False, stop=(c == C - 1))
                return last

            def down(t):
                slot = entry(pe, rt.slot_i, t, 0, SLOTS - 1)
                parts = entry(pe, rt.part_i, t, 0, PARTS * (E - 1))
                pe.wait_ge(w_parts, pe.snap(parts + PARTS))
                pe.wait_ge(hL_ready, t + 1)
                if later(t, 1):
                    pe.wait_ge(y_ready, t)
                product(Dn, hH, hL, slot, DOWN).then_inc(tile_done, 1)

            def body(t, s, n):
                slot = entry(pe, rt.slot_i, t, 0, SLOTS - 1)
                parts = entry(pe, rt.part_i, t, 0, PARTS * (E - 1))
                pe.wait_ge(xL_ready, t + 1)
                pe.wait_ge(w_parts, pe.snap(parts + GATE + 1))
                if later(t, 1):
                    pe.wait_ge(sg_ready, t)
                product(G, xH[s], xL[s], slot, GATE).then_inc(g_full, 1)
                if later(t, 1):
                    turn_h(t - 1)
                pe.wait_ge(w_parts, pe.snap(parts + UP + 1))
                product(U, xH[s], xL[s], slot, UP).then_inc(u_full, 1)
                if n is not None:
                    turn_x(t + 1, 1 - s, n)
                if later(t, 1):
                    down(t - 1)

            pe.sem_inc(tile_done, 1)
            turn_x(0, 0, 1)
            body(0, 0, 1)
            with pe.Fori(0, TILES // 2 - 1) as i:
                body(2 * i + 1, 1, i + 2)
                body(2 * i + 2, 0, i + 2)
            body(TILES - 2, 1, (TILES + 1) // 2)
            body(TILES - 1, 0, None)
            turn_h(TILES - 1)
            down(TILES - 1)

        @block.scalar
        def _(act):
            def take_x(t, s):
                act.wait_ge(x_full, t + 1)
                if later(t, 2):
                    act.wait_ge(u_full, t - 1)
                act.copy(xH[s][:], TX[:].rearrange("p (c i) -> p c i", c=C)).then_inc(xH_ready, 1)

            def take_h(t):
                act.wait_ge(h_full, t + 1)
                act.wait_ge(tile_done, t + 1)
                act.copy(hH[:], TH[:].rearrange("p (c i) -> p c i", c=C)).then_inc(hH_ready, 1)

            def body(t, s, more):
                act.wait_ge(g_full, t + 1)
                act.wait_ge(h_ready, t)
                act.activation(sg[:], G[:], ACT.Silu).then_inc(sg_ready, 1)
                if later(t, 1):
                    take_h(t - 1)
                if more:
                    take_x(t + 1, 1 - s)

            def high_first(part):
                act.copy(high[:, 0, part], ex.low[:, 0, part].bitcast(F32)).then_inc(w_high, 1)

            act.wait_ge(ex.w_in[0], 16 * PARTS)
            high_first(GATE)
            take_x(0, 0)
            high_first(UP)
            high_first(DOWN)
            body(0, 0, True)
            with act.Fori(0, TILES // 2 - 1) as i:
                body(2 * i + 1, 1, True)
                body(2 * i + 2, 0, True)
            body(TILES - 2, 1, True)
            body(TILES - 1, 0, False)
            take_h(TILES - 1)

        @block.vector
        def _(dve):
            def low_first(part):
                raw = ex.low[:, 0, part]
                dve.wait_ge(w_high, part + 1)
                dve.tensor_tensor(raw, raw.bitcast(F32), high[:, 0, part].bitcast(F32), ALU.subtract).then_inc(w_parts, 1)

            def low_x(t, s):
                dve.wait_ge(xH_ready, t + 1)
                if later(t, 2):
                    dve.wait_ge(u_full, t - 1)
                dve.tensor_tensor(xL[s][:], TX[:].rearrange("p (c i) -> p c i", c=C), xH[s][:].bitcast(F32),
                                  ALU.subtract).then_inc(xL_ready, 1)

            def low_h(t):
                dve.wait_ge(hH_ready, t + 1)
                dve.wait_ge(tile_done, t + 1)
                dve.tensor_tensor(hL[:], TH[:].rearrange("p (c i) -> p c i", c=C), hH[:].bitcast(F32),
                                  ALU.subtract).then_inc(hL_ready, 1)

            def gate(t):
                dve.wait_ge(u_full, t + 1)
                dve.wait_ge(sg_ready, t + 1)
                if later(t, 1):
                    dve.wait_ge(h_full, t)
                dve.tensor_tensor(h[:], U[:], sg[:], ALU.mult).then_inc(h_ready, 1)

            def take_y(t, s, stored):
                dve.wait_ge(tile_done, t + 2)
                if later(t, 2):
                    dve.wait_ge(y_out[s], 16 * stored)
                dve.tensor_copy(yt[s][:], Dn[:]).then_inc(y_ready, 1)

            def body(t, s, stored, more):
                if later(t, 1):
                    low_h(t - 1)
                gate(t)
                if more:
                    low_x(t + 1, 1 - s)
                if later(t, 1):
                    take_y(t - 1, 1 - s, stored)

            low_first(GATE)
            low_x(0, 0)
            low_first(UP)
            low_first(DOWN)
            body(0, 0, 0, True)
            body(1, 1, 0, True)
            body(2, 0, 0, True)
            with dve.Fori(1, TILES // 2 - 1) as i:
                body(2 * i + 1, 1, i, True)
                body(2 * i + 2, 0, i, True)
            body(TILES - 2, 1, TILES // 2 - 1, True)
            body(TILES - 1, 0, TILES // 2 - 1, False)
            low_h(TILES - 1)
            take_y(TILES - 1, 0, TILES // 2)


def combine(nc, sh, rt, out):
    D, B, E = sh.D, sh.B, sh.E
    TILES, ST, BUFS = sh.N // P, P // sh.B, 4
    EPS = 1e-9
    with ExitStack() as stack:
        def sb(name, shape, dt=F32):
            return stack.enter_context(nc.sbuf_tensor(name, shape, dt))

        def sem(name):
            return stack.enter_context(nc.semaphore(name))

        rs = sb("c_rs", [P, TILES])
        total = sb("c_total", [P, TILES])
        part = sb("c_part", [P, TILES, 2])
        hot = sb("c_hot", [P, 2 * TILES, E])
        prod = sb("c_prod", [P, 2 * TILES, E])
        first = sb("c_first", [P, 2 * TILES])
        place = sb("c_place", [P, 2 * TILES], I32)
        y = [[sb(f"c_y{s}{w}", [P, D]) for w in range(2)] for s in range(BUFS)]
        y_in = [sem(f"c_y_in{s}") for s in range(BUFS)]
        place_step = sem("c_place_step")
        w_step, first_added, o_ready, o_out = sem("c_w_step"), sem("c_first_added"), sem("c_o_ready"), sem("c_o_out")
        block = stack.enter_context(nc.Block())
        out_tiles = out.rearrange("b (k t) d -> k t b d", t=ST)

        @block.gpsimd
        def _(pool):
            pool.wait_ge(place_step, 4)
            for k in range(TILES):
                s = k % BUFS
                if k >= BUFS:
                    pool.wait_ge(o_ready, k - BUFS + 1)
                for w in range(2):
                    pool.indirect_dma_start(out=y[s][w][:], out_offset=None, in_=rt.y_rows,
                                            in_offset=bass.IndirectOffsetOnAxis(ap=place[:, 2 * k + w:2 * k + w + 1], axis=0)
                                            ).then_inc(y_in[s], 16)

        @block.vector
        def _(dve):
            hot4 = hot[:].rearrange("p (k w) e -> p k w e", w=2)
            prod4 = prod[:].rearrange("p (k w) e -> p k w e", w=2)
            dve.tensor_tensor(hot4, rt.rank[:, :, None, :].to_broadcast([P, TILES, 2, E]),
                              rt.second[:, None, :, None].to_broadcast([P, TILES, 2, E]), ALU.is_equal).then_inc(place_step, 1)
            dve.wait_ge(place_step, 1)
            dve.tensor_tensor(prod[:], hot[:], rt.first_row[:, None, 0:E].to_broadcast([P, 2 * TILES, E]), ALU.mult).then_inc(place_step, 1)
            dve.wait_ge(place_step, 2)
            dve.tensor_reduce(first[:], prod[:], axis=AX.X, op=ALU.add).then_inc(place_step, 1)
            dve.wait_ge(place_step, 3)
            dve.tensor_tensor(place[:], rt.places[:].rearrange("p k w -> p (k w)"), first[:], ALU.subtract).then_inc(place_step, 1)
            dve.tensor_tensor(prod4, hot4, rt.ew[:, :, None, :].to_broadcast([P, TILES, 2, E]), ALU.mult).then_inc(place_step, 1)
            dve.tensor_reduce(total[:], rt.ew[:], axis=AX.X, op=ALU.add).then_inc(place_step, 1)
            dve.wait_ge(place_step, 6)
            dve.tensor_reduce(part[:].rearrange("p k w -> p (k w)"), prod[:], axis=AX.X, op=ALU.add).then_inc(place_step, 1)
            dve.reciprocal(rs[:], total[:]).then_inc(w_step, 1)
            dve.wait_ge(w_step, 1)
            dve.wait_ge(place_step, 7)
            dve.tensor_tensor(part[:], part[:], rs[:, :, None].to_broadcast([P, TILES, 2]), ALU.mult).then_inc(w_step, 1)
            dve.wait_ge(w_step, 2)
            for i in range(2):
                n = 2 + 4 * i
                dve.tensor_reduce(total[:], part[:], axis=AX.X, op=ALU.add).then_inc(w_step, 1)
                dve.wait_ge(w_step, n + 1)
                dve.tensor_scalar(total[:], total[:], EPS, None, ALU.add).then_inc(w_step, 1)
                dve.wait_ge(w_step, n + 2)
                dve.reciprocal(rs[:], total[:]).then_inc(w_step, 1)
                dve.wait_ge(w_step, n + 3)
                dve.tensor_tensor(part[:], part[:], rs[:, :, None].to_broadcast([P, TILES, 2]), ALU.mult).then_inc(w_step, 1)
                dve.wait_ge(w_step, n + 4)
            for k in range(TILES):
                s = k % BUFS
                x2 = rt.x2[:, k, :]
                dve.wait_ge(y_in[s], 32 * (k // BUFS + 1))
                dve.scalar_tensor_tensor(x2, y[s][0][:], part[:, k, 0:1], x2, ALU.mult, ALU.add).then_inc(first_added, 1)
                dve.wait_ge(first_added, k + 1)
                dve.scalar_tensor_tensor(x2, y[s][1][:], part[:, k, 1:2], x2, ALU.mult, ALU.add).then_inc(o_ready, 1)

        @block.sync
        def _(sp):
            for k in range(TILES):
                sp.wait_ge(o_ready, k + 1)
                sp.dma_start(out_tiles[k], rt.x2[:, k, :]).then_inc(o_out, 16)
            sp.wait_ge(o_out, 16 * TILES)


def program(nc, x, ctx, w_sim, b_sim, W_qv, b_qv, decay, Wr, br, Wg, bg, Wo, bo, ln_w, ln_b, gate_w, gate_up, down, out):
    sh = Shapes(x, ctx, gate_w)
    C = sh.C
    x1 = nc.dram_tensor("x1", (sh.PAIRS, P, sh.D), F32, kind="Internal").ap()
    u_d = nc.dram_tensor("u", (C * sh.B, sh.L, P), F32, kind="Internal").ap()
    c_d = nc.dram_tensor("c", (C * sh.B, sh.L, P), F32, kind="Internal").ap()
    with ExitStack() as stack:
        ident = stack.enter_context(nc.sbuf_tensor("ident", [P, P], F32))
        make_identity(nc, ident)
        cross_attention(nc, sh, ident, x.rearrange("(p b) l d -> p (b l) d", b=2), ctx.rearrange("(p b) j d -> p b j d", b=2),
                        w_sim, b_sim, W_qv, b_qv, x1)
        rt = Routing(nc, sh, stack)
        ex = Experts(nc, sh, gate_up, down, stack)
        with ExitStack() as inner:
            rw = RecurrenceWeights(nc, sh, Wr, Wo, inner)
            recurrence_gates(nc, sh, ident, x1, Wg, bg, br, decay, u_d, c_d, rw)
            recurrence(nc, sh, ident, x1, u_d, c_d, decay, rw, bo, ln_w, ln_b, gate_w, rt, ex)
        experts(nc, sh, ident, ex, rt)
        combine(nc, sh, rt, out)


_INS = ["x", "ctx_1024", "L0_xattn_w_sim", "L0_xattn_b_sim", "L0_xattn_W_qv", "L0_xattn_b_qv",
        "L0_attn_decay", "L0_attn_Wr", "L0_attn_br", "L0_attn_Wg", "L0_attn_bg", "L0_attn_Wo", "L0_attn_bo",
        "L0_attn_ln_w", "L0_attn_ln_b", "L0_ffn_gate_w", "L0_ffn_gate_up_proj", "L0_ffn_down_proj"]


def kernel(**inputs):
    import numpy as _np
    import concourse.bacc as _bacc
    from concourse.bass_utils import run_bass_kernel_spmd as _run

    nc = _bacc.Bacc("TRN2", target_bir_lowering=False, num_devices=1)
    arrays, args = {}, []
    for name in _INS:
        a = _np.ascontiguousarray(inputs[name])
        arrays[f"in_{name}_dram"] = a
        args.append(nc.dram_tensor(f"in_{name}_dram", a.shape, mybir.dt.from_np(a.dtype), kind="ExternalInput").ap())
    out = nc.dram_tensor("out_0_dram", inputs["x"].shape, F32, kind="ExternalOutput").ap()
    program(nc, *args, out)
    r = _run(nc, [arrays], core_ids=[0])
    return r.results[0]["out_0_dram"]
```

```python
from contextlib import ExitStack

import concourse.bass as bass
from concourse import mybir

F32 = mybir.dt.float32
F32R = mybir.dt.float32r
BF16 = mybir.dt.bfloat16
I32 = mybir.dt.int32
U32 = mybir.dt.uint32
ALU = mybir.AluOpType
ACT = mybir.ActivationFunctionType
AX = mybir.AxisListType

P = 128
LN_EPS = 1e-5


class Shapes:

    def __init__(self, x, ctx, gate_w):
        self.B, self.L, self.D = x.shape
        self.J = ctx.shape[1]
        self.E = gate_w.shape[0]
        self.N = self.B * self.L
        self.C = self.D // P
        self.PAIRS = self.N // P
        self.JT = -(-self.J // P)
        self.JMAIN = (self.JT - 1) * P
        self.JTAIL = self.J - self.JMAIN
        assert P == 2 * self.L and self.D == 4 * P and self.B == 32 and self.JT == 13


def bcast_row(vec):
    return vec.rearrange("(o d) -> o d", o=1).to_broadcast([P, vec.shape[0]])


BLOCKS = [(0, 3, 0, 0), (3, 3, 1, 0), (6, 3, 2, 0), (9, 2, 3, 0), (11, 2, 3, 256)]
NBLK = len(BLOCKS)
BANK_TILES = [(0, 3), (3, 3), (6, 3), (9, 4)]
TWO_SLOTS = 2
AV_ORDER = [t for j in [*range(TWO_SLOTS, NBLK), *range(TWO_SLOTS)] for t in range(BLOCKS[j][0], BLOCKS[j][0] + BLOCKS[j][1])]
AT_TILES = [(0, 4), (4, 3), (7, 3), (10, 3)]


def turn_order(front, back):
    bank = ([], [])
    for j, (_, n, _, _) in enumerate(BLOCKS):
        for u in range(2 * n if front else 0):
            bank[u % 2].append(f"ctx{j}.{u}")
    if front:
        bank[0].insert(1, "hc")
    if back:
        bank[1].insert(1 if front else 0, "trow")
        bank[0].append("hqh")
    for q in range(len(AT_TILES) if front else 0):
        bank[q % 2].append(f"probs{q}")
    return bank


FIRST_TURNS = turn_order(True, False)
FULL_TURNS = turn_order(True, True)
LAST_TURNS = turn_order(False, True)


def turn(bank, name, p, step):
    if step == "first":
        return FIRST_TURNS[bank].index(name)
    order = LAST_TURNS if step == "last" else FULL_TURNS
    return len(FIRST_TURNS[bank]) + p * len(FULL_TURNS[bank]) + order[bank].index(name)


def before(p):
    return p - 1, "first" if isinstance(p, int) and p == 0 else "full"


def later(p, n):
    return not isinstance(p, int) or p >= n


def cross_attention(nc, sh, ident, x, ctx, w_sim, b_sim, W_qv, b_qv, x1, x2, ahead):
    D, C, JT, JMAIN, JTAIL, PAIRS = sh.D, sh.C, sh.JT, sh.JMAIN, sh.JTAIL, sh.PAIRS
    BW = 3 * P
    sems = []

    with ExitStack() as stack:
        def sb(name, shape, dt=F32):
            return stack.enter_context(nc.sbuf_tensor(name, shape, dt))

        def sem(name):
            sems.append(nc.alloc_semaphore(name=name))
            return sems[-1]

        TWO = BLOCKS[TWO_SLOTS][0]
        ctx_two = [[x2[:, b * TWO:(b + 1) * TWO, :] for b in range(2)], [sb(f"ctx_two{b}", [P, TWO, D]) for b in range(2)]]
        ctx_one = [sb(f"ctx_one{b}", [P, JT - TWO, D]) for b in range(2)]
        ctxT = [sb(f"ctxT{s}", [P, 2, C, BW]) for s in range(2)]
        w0, w3 = x2[:, 2 * TWO:2 * TWO + C, :], sb("w3", [P, C, D])
        w12H, w12L = sb("w12H", [P, 2 * C, D], F32R), sb("w12L", [P, 2 * C, D], F32R)
        x_sb = sb("x_sb", [P, D])
        xb = [sb(f"xb{s}", [P, D]) for s in range(2)]
        tok_rows = sb("tok_rows", [P, D])
        hcT = [sb(f"hcT{s}", [P, C, P]) for s in range(2)]
        qT = sb("qT", [P, C, P])
        probs = sb("probs", [P, JT * P])
        probsT = sb("probsT", [P, JT, P])
        hqhH, hqhL = sb("hqhH", [P, C, P], F32R), sb("hqhL", [P, C, P], F32R)
        wb = sb("wb", [P, 2, C, D])
        f2H, f2L = sb("f2H", [P, C, P], F32R), sb("f2L", [P, C, P], F32R)
        f3 = sb("f3", [P, C, P])
        w1_b = sb("w1_b", [P, D])
        bqv_b = sb("bqv_b", [P, D])
        w2T = sb("w2T", [P, C])
        w3T = sb("w3T", [P, C])
        bsim_b = sb("bsim_b", [P, 1])
        stats = sb("stats", [P, 6])
        mv = sb("mv", [P, 2])
        ve = sb("ve", [P, 1])
        nmean = sb("nmean", [P, 1])
        rstd = sb("rstd", [P, 1])
        mhalf = sb("mhalf", [P, 1])
        s1 = sb("s1", [P, 1])
        mx4 = sb("mx4", [P, 4])
        mx = sb("mx", [P, 1])
        nmx = sb("nmx", [P, 1])
        z4 = sb("z4", [P, 4])
        zsum = sb("zsum", [P, 1])
        rz = sb("rz", [P, 1])
        tcol = sb("tcol", [P, 1])
        nrm = sb("nrm", [1, 2])
        erow = sb("erow", [1, P])
        rsum = sb("rsum", [1, 2])
        rinv = sb("rinv", [1, 2])
        brow = sb("brow", [1, P])
        ones1 = sb("ones1", [1, P])
        hcb = sb("hcb", [P, C, 2])

        S = stack.enter_context(nc.psum_tensor("S", [P, 4, 512], F32))
        T = [stack.enter_context(nc.psum_tensor(f"T{s}", [P, 512], F32)) for s in range(2)]
        O = stack.enter_context(nc.psum_tensor("O", [P, 512], F32))
        Y = stack.enter_context(nc.psum_tensor("Y", [P, 512], F32))

        const_in = sem("const_in")
        wqv_in, w12_in = sem("wqv_in"), sem("w12_in")
        w12H_ready, w12L_ready = sem("w12H_ready"), sem("w12L_ready")
        hqhH_ready, hqhL_ready, f2H_ready = sem("hqhH_ready"), sem("hqhL_ready"), sem("f2H_ready")
        x_in = sem("x_in")
        ctx_in = [[sem(f"ctx_in{s}_{j}") for j in range(TWO_SLOTS)] for s in range(2)]
        ctx_one_in = [sem(f"ctx_one_in{j}") for j in range(TWO_SLOTS, NBLK)]
        av_one = sem("av_one")
        x1_out = sem("x1_out")
        consts = sem("consts")
        stat_done = sem("stat_done")
        ln_ready = sem("ln_ready")
        rstd_ready = sem("rstd_ready")
        hc_ready = sem("hc_ready")
        xb_ready = sem("xb_ready")
        q_ready = sem("q_ready")
        s1_ready = sem("s1_ready")
        t_full = [sem(f"t_full{s}") for s in range(2)]
        t_free = [sem(f"t_free{s}") for s in range(2)]
        qk_done = sem("qk_done")
        mx_done = sem("mx_done")
        nmx_ready = sem("nmx_ready")
        tcol_ready = sem("tcol_ready")
        exp_done = sem("exp_done")
        z_done = sem("z_done")
        rz_ready = sem("rz_ready")
        nrm_done = sem("nrm_done")
        erow_ready = sem("erow_ready")
        bsm_done = sem("bsm_done")
        brow_ready = sem("brow_ready")
        brow_full, hcb_step = sem("brow_full"), sem("hcb_step")
        hcb_done = sem("hcb_done")
        f2_ready = sem("f2_ready")
        wb_step = sem("wb_step")
        av_done = sem("av_done")
        hqh_ready = sem("hqh_ready")
        y_done = sem("y_done")
        x1_ready = sem("x1_ready")

        def first(p):
            return isinstance(p, int) and p == 0

        def tile_rows(t):
            return P if t < JT - 1 else JTAIL

        def bank_cols(k):
            t0, n = BANK_TILES[k]
            return sum(tile_rows(t) for t in range(t0, t0 + n))

        def context(s, b, t):
            return (ctx_two[s][b], t) if t < TWO else (ctx_one[b], t - TWO)

        def block_dmas(j):
            t0, n, _, _ = BLOCKS[j]
            return 2 * (2 if t0 + n == JT else 1)

        def block_cols(j):
            t0, n, _, _ = BLOCKS[j]
            return sum(tile_rows(t) for t in range(t0, t0 + n))

        def steps(eng, body):
            body(-1, 0, "first")
            body(0, 0, "full")
            with eng.Fori(0, (PAIRS - 2) // 2) as i:
                body(2 * i + 1, 1, "full")
                body(2 * i + 2, 0, "full")
            body(PAIRS - 1, 1, "last")

        block = stack.enter_context(nc.Block())

        @block.sync
        def _(sp):
            def load_x(row):
                sp.dma_start(x_sb[:], x[row]).then_inc(x_in, 16)

            def load_block(j, s, pair):
                t0, n, _, _ = BLOCKS[j]
                done = ctx_in[s][j] if j < TWO_SLOTS else ctx_one_in[j - TWO_SLOTS]
                for b in range(2):
                    src = ctx[pair, b]
                    dst, i = context(s, b, t0)
                    full = min(n, JT - 1 - t0)
                    sp.dma_start(dst[:, i:i + full, :],
                                 src[0:JMAIN, :].rearrange("(p t) d -> p t d", t=JT - 1)[:, t0:t0 + full, :]).then_inc(done, 16)
                    if full < n:
                        sp.dma_start(dst[0:JTAIL, i + full, :], src[JMAIN:sh.J, :]).then_inc(done, 16)

            load_x(0)
            sp.dma_start(w1_b[:], bcast_row(w_sim[0:D])).then_inc(const_in, 16)
            with nc.allow_non_contiguous_dma(reason="two small weight vectors, a column for each chunk"):
                sp.dma_start(w2T[:], w_sim[D:2 * D].rearrange("(c p) -> p c", p=P)).then_inc(const_in, 16)
                sp.dma_start(w3T[:], w_sim[2 * D:3 * D].rearrange("(c p) -> p c", p=P)).then_inc(const_in, 16)
            sp.dma_start(bsim_b[:], bcast_row(b_sim)).then_inc(const_in, 16)
            sp.dma_start(bqv_b[:], bcast_row(b_qv)).then_inc(const_in, 16)
            for j in range(NBLK):
                load_block(j, 0, 0)
            sp.wait_ge(hc_ready, 1)
            sp.wait_ge(xb_ready, 1)
            load_x(1)
            w_rows = W_qv.rearrange("(k p) e -> p k e", p=P)
            sp.dma_start(wb[:].rearrange("p b c d -> p (b c) d"), w_rows[:, C:3 * C, :]).then_inc(w12_in, 16)
            sp.dma_start(w0, w_rows[:, 0:C, :]).then_inc(wqv_in, 16)
            sp.dma_start(w3[:], w_rows[:, 3 * C:4 * C, :]).then_inc(wqv_in, 16)
            for j in range(TWO_SLOTS):
                load_block(j, 1, 1)

            def step(p, s, load, store):
                nxt = p + 1 if isinstance(p, int) else sp.snap(p + 1)
                if load:
                    ahead = p + 2 if isinstance(p, int) else sp.snap(p + 2)
                if store:
                    prev = p - 1 if isinstance(p, int) else sp.snap(p - 1)
                for j in range(TWO_SLOTS, NBLK):
                    sp.wait_ge(av_one, (NBLK - TWO_SLOTS) * p + j - TWO_SLOTS + 1)
                    load_block(j, None, nxt)
                if store:
                    sp.wait_ge(x1_ready, p)
                    sp.dma_start(x1[prev], xb[1 - s][:]).then_inc(x1_out, 16)
                if load:
                    sp.wait_ge(hc_ready, p + 2)
                    sp.wait_ge(xb_ready, p + 2)
                    load_x(ahead)
                    sp.wait_ge(av_done, p + 1)
                    for j in range(TWO_SLOTS):
                        load_block(j, s, ahead)

            step(0, 0, True, False)
            with sp.Fori(0, (PAIRS - 4) // 2) as i:
                step(2 * i + 1, 1, True, True)
                step(2 * i + 2, 0, True, True)
            step(PAIRS - 3, 1, True, True)
            step(PAIRS - 2, 0, False, True)
            sp.wait_ge(av_done, PAIRS - 1)
            sp.wait_ge(x1_out, 16 * (PAIRS - 2))
            ahead.load(sp)
            sp.wait_ge(x1_ready, PAIRS - 1)
            sp.dma_start(x1[PAIRS - 2], xb[0][:]).then_inc(x1_out, 16)
            sp.wait_ge(x1_ready, PAIRS)
            sp.dma_start(x1[PAIRS - 1], xb[1][:]).then_inc(x1_out, 16)
            sp.wait_ge(x1_out, 16 * PAIRS)

        @block.gpsimd
        def _(pool):
            pool.memset(mhalf[:], -0.5).then_inc(consts, 1)
            pool.memset(ones1[:], 1.0).then_inc(consts, 1)
            pool.wait_ge(consts, 2)
            pool.wait_ge(const_in, 80)

            def body(p, s, step):
                if step != "last":
                    f = p + 1
                    pool.wait_ge(ln_ready, 2 * f + 2)
                    pool.tensor_tensor(rstd[:], ve[:], mhalf[:], ALU.pow).then_inc(rstd_ready, 1)
                    if not (isinstance(f, int) and f < 2):
                        pool.wait_ge(x1_out, 16 * (f - 1))
                    pool.tensor_tensor(xb[1 - s if step != "first" else 0][:], x_sb[:], bqv_b[:], ALU.add).then_inc(xb_ready, 1)
                if step != "first":
                    pool.wait_ge(hcb_done, p + 1)
                    pool.wait_ge(y_done, p)
                    if first(p):
                        pool.wait_ge(wqv_in, 32)
                        pool.wait_ge(w12L_ready, 1)
                    for b in range(2 if step == "full" else 0):
                        pool.tensor_tensor(wb[:, b], w3[:], hcb[:, :, b, None].to_broadcast([P, C, D]),
                                           ALU.mult).then_inc(wb_step, 1)
                    for b in range(2 if step == "full" else 0):
                        pool.wait_ge(wb_step, 4 * p + b + 1)
                        pool.tensor_tensor(wb[:, b], wb[:, b], w0, ALU.add).then_inc(wb_step, 1)

            steps(pool, body)

        @block.tensor
        def _(pe):
            def fill(bank, name, p, step):
                pe.wait_ge(t_free[bank], turn(bank, name, p, step))

            def turn_ctx(j, u, p, fs, loads, step):
                t0, n, _, _ = BLOCKS[j]
                t, b, bank = t0 + u // 2, u % 2, u % 2
                rows = tile_rows(t)
                if u == 0 and j < TWO_SLOTS:
                    pe.wait_ge(ctx_in[fs][j], block_dmas(j) * 16 * loads)
                elif u == 0:
                    pe.wait_ge(ctx_one_in[j - TWO_SLOTS], block_dmas(j) * 16 * (p + 2))
                src, i = context(fs, b, t)
                fill(bank, f"ctx{j}.{u}", p, step)
                for c in range(C):
                    last = pe.transpose(T[bank][:, c * P:c * P + rows], src[0:rows, i, c * P:(c + 1) * P],
                                        ident[0:rows, 0:rows])
                last.then_inc(t_full[bank], 1)

            def turn_tile(bank, name, src, p, step):
                fill(bank, name, p, step)
                for c in range(C):
                    last = pe.transpose(T[bank][:, c * P:(c + 1) * P], src[:, c * P:(c + 1) * P], ident[:])
                last.then_inc(t_full[bank], 1)

            def turn_probs(q, p, step):
                t0, n = AT_TILES[q]
                if q == 0:
                    pe.wait_ge(exp_done, 4 * (p + 2))
                fill(q % 2, f"probs{q}", p, step)
                for i in range(n):
                    rows = tile_rows(t0 + i)
                    last = pe.transpose(T[q % 2][0:rows, i * P:(i + 1) * P],
                                        probs[:, (t0 + i) * P:(t0 + i) * P + rows], ident[:])
                last.then_inc(t_full[q % 2], 1)

            def scores(j, p, f, fs, loads, step):
                t0, n, k, col = BLOCKS[j]
                w = block_cols(j)
                buf = ctxT[(j + fs) % 2]
                for bank in range(2):
                    pe.wait_ge(t_free[bank], turn(bank, f"ctx{j}.{2 * n - 2 + bank}", p, step) + 1)
                if j == 0:
                    pe.wait_ge(q_ready, C * (f + 1))
                    pe.wait_ge(exp_done, 4 * f)
                for c in range(C):
                    if j + 1 < NBLK and c < BLOCKS[j + 1][1]:
                        turn_ctx(j + 1, 2 * c, p, fs, loads, step)
                        turn_ctx(j + 1, 2 * c + 1, p, fs, loads, step)
                    for b in range(2):
                        last = pe.matmul(S[64 * b:64 * b + 64, k, col:col + w], qT[:, c, 64 * b:64 * b + 64],
                                         buf[:, b, c, 0:w], start=(c == 0), stop=(c == C - 1))
                last.then_inc(qk_done, 1)

            def product(c, aH, aL, w, start, stop):
                pe.matmul(Y[:], aH[:, c, :], w12H[:, w, :], start=start, stop=False)
                pe.matmul(Y[:], aH[:, c, :], w12L[:, w, :], start=False, stop=False)
                return pe.matmul(Y[:], aL[:, c, :], w12H[:, w, :], start=False, stop=stop)

            def body(p, s, step, loads):
                front, back = step != "last", step != "first"
                f, fs = p + 1, (1 - s) if back else 0
                if back:
                    for bank in range(2):
                        pe.wait_ge(t_free[bank], turn(bank, f"probs{2 + bank}", *before(p)) + 1)
                    pe.wait_ge(hqh_ready, p)
                for n, t in enumerate(AV_ORDER):
                    if n == 1:
                        if front:
                            pe.wait_ge(hc_ready, f + 1)
                            turn_tile(0, "hc", tok_rows, p, step)
                        if back:
                            pe.wait_ge(tcol_ready, p + 1)
                            fill(1, "trow", p, step)
                            pe.transpose(T[1][0:1, 0:P], tcol[:], ident[:]).then_inc(t_full[1], 1)
                    elif front and n in (0, 2, 3):
                        u = 2 * max(n - 1, 0)
                        turn_ctx(0, u, p, fs, loads, step)
                        turn_ctx(0, u + 1, p, fs, loads, step)
                    for b in range(2 if back else 0):
                        rows = tile_rows(t)
                        src, i = context(s, b, t)
                        last = pe.matmul(O[64 * b:64 * b + 64, :], probsT[0:rows, t, 64 * b:64 * b + 64],
                                         src[0:rows, i, :], start=(n == 0), stop=(n == JT - 1))
                    if back and n == (10 if front else 4):
                        pe.wait_ge(x1_ready, p)
                        pe.wait_ge(brow_ready, p + 1)
                        pe.matmul(Y[:, 0:P], ones1[:], brow[:], start=True, stop=True).then_inc(brow_full, 1)
                    if back and t in [t0 + n - 1 for t0, n, _, _ in BLOCKS[TWO_SLOTS:]]:
                        last.then_inc(av_one, 1)
                if back:
                    last.then_inc(av_done, 1)
                if front:
                    scores(0, p, f, fs, loads, step)
                    for j in range(1, NBLK - 1):
                        scores(j, p, f, fs, loads, step)
                if back:
                    pe.wait_ge(hqh_ready, p + 1)
                    turn_tile(0, "hqh", tok_rows, p, step)
                if front:
                    scores(NBLK - 1, p, f, fs, loads, step)
                if back:
                    if first(p):
                        pe.wait_ge(w12L_ready, 1)
                    pe.wait_ge(hcb_step, p + 1)
                    pe.wait_ge(hqhL_ready, p + 1)
                    for c in range(C):
                        product(c, hqhH, hqhL, c, c == 0, False)
                    pe.wait_ge(wb_step, 4 * (p + 1))
                    for c in range(C):
                        if front and c >= 2:
                            turn_probs(c - 2, p, step)
                        for b in range(2):
                            pe.matmul(Y[64 * b:64 * b + 64, :], hcT[s][:, c, 64 * b:64 * b + 64], wb[:, b, c, :],
                                      start=False, stop=False)
                    pe.wait_ge(t_free[0], turn(0, "hqh", p, step) + 1)
                    for c in range(C):
                        if front and c < 2:
                            turn_probs(2 + c, p, step)
                        last = product(c, f2H, f2L, C + c, False, c == C - 1)
                    last.then_inc(y_done, 1)
                elif front:
                    for q in range(len(AT_TILES)):
                        turn_probs(q, p, step)

            body(-1, 0, "first", 1)
            body(0, 0, "full", 1)
            with pe.Fori(0, (PAIRS - 2) // 2) as i:
                body(2 * i + 1, 1, "full", i + 2)
                body(2 * i + 2, 0, "full", i + 2)
            body(PAIRS - 1, 1, "last", None)

        def drain_ctx(eng, copy, bank, j, p, fs, step, only=None):
            t0, n, _, _ = BLOCKS[j]
            buf = ctxT[(j + fs) % 2]
            if not (step == "first" and j < 2):
                eng.wait_ge(qk_done, NBLK * (p + 1) + j - 1)
            for u in range(bank, 2 * n, 2) if only is None else only:
                t = t0 + u // 2
                rows, i = tile_rows(t), u // 2
                eng.wait_ge(t_full[bank], turn(bank, f"ctx{j}.{u}", p, step) + 1)
                copy(buf[:, bank, :, i * P:i * P + rows],
                     T[bank][:].rearrange("p (c j) -> p c j", c=C)[:, :, 0:rows]).then_inc(t_free[bank], 1)

        def drain_probs(eng, copy, bank, p, step):
            eng.wait_ge(av_done, p + 1)
            for q in range(bank, len(AT_TILES), 2):
                t0, n = AT_TILES[q]
                eng.wait_ge(t_full[bank], turn(bank, f"probs{q}", p, step) + 1)
                full = n if t0 + n < JT else n - 1
                last = copy(probsT[:, t0:t0 + full, :], T[bank][:, 0:full * P].rearrange("p (t i) -> p t i", i=P))
                if full < n:
                    last = copy(probsT[0:JTAIL, JT - 1, :], T[bank][0:JTAIL, full * P:n * P])
                last.then_inc(t_free[bank], 1)

        @block.scalar
        def _(act):
            copy = nc.scalar.copy

            def body(p, s, step):
                front, back = step != "last", step != "first"
                f, fs = p + 1, (1 - s) if back else 0
                if first(p):
                    act.wait_ge(w12_in, 16)
                    act.copy(w12H[:], wb[:].rearrange("p b c d -> p (b c) d")).then_inc(w12H_ready, 1)
                if front:
                    drain_ctx(act, copy, 0, 0, p, fs, step, only=(0,))
                    act.wait_ge(t_full[0], turn(0, "hc", p, step) + 1)
                    if later(f, 2):
                        act.wait_ge(y_done, f - 1)
                    act.copy(hcT[fs][:], T[0][:].rearrange("p (c i) -> p c i", c=C)).then_inc(t_free[0], 1)
                    drain_ctx(act, copy, 0, 0, p, fs, step, only=(2, 4))
                if back:
                    act.wait_ge(t_free[1], turn(1, "trow", p, step) + 1)
                    act.wait_ge(brow_ready, p)
                    act.activation(erow[:], erow[:], ACT.Exp).then_inc(erow_ready, 1)
                if front:
                    drain_ctx(act, copy, 0, 1, p, fs, step)
                if back:
                    act.wait_ge(av_done, p + 1)
                    act.wait_ge(rz_ready, p + 1)
                    if front:
                        act.wait_ge(t_free[0], turn(0, "hc", p, step) + 1)
                        act.wait_ge(s1_ready, f + 1)
                    else:
                        act.wait_ge(t_free[0], turn(0, "hqh", *before(p)) + 1)
                    act.activation(tok_rows[:], O[:], ACT.Copy, scale=rz[:, 0:1]).then_inc(hqh_ready, 1)
                if front:
                    for j in range(2, NBLK):
                        drain_ctx(act, copy, 0, j, p, fs, step)
                if back:
                    act.wait_ge(t_full[0], turn(0, "hqh", p, step) + 1)
                    act.wait_ge(y_done, p)
                    act.copy(hqhH[:], T[0][:].rearrange("p (c i) -> p c i", c=C)).then_inc(hqhH_ready, 1)
                    act.wait_ge(f2_ready, p + 1)
                    act.copy(f2H[:], f3[:]).then_inc(f2H_ready, 1)
                if front:
                    act.wait_ge(nmx_ready, f + 1)
                    if back:
                        for bank in range(2):
                            act.wait_ge(t_free[bank], turn(bank, f"probs{2 + bank}", *before(p)) + 1)
                        act.wait_ge(rz_ready, f)
                    for k, (t0, _) in enumerate(BANK_TILES):
                        w = bank_cols(k)
                        act.activation(probs[:, t0 * P:t0 * P + w], S[:, k, 0:w], ACT.Exp, bias=nmx[:, 0:1],
                                       accum_out=z4[:, k:k + 1]).then_inc(exp_done, 1)
                    drain_probs(act, copy, 0, p, step)

            steps(act, body)

        @block.vector
        def _(dve):
            copy = nc.vector.tensor_copy
            dve.wait_ge(const_in, 80)

            def norm_stats(f):
                dve.wait_ge(x_in, 16 * f + 16)
                dve.wait_ge(hc_ready, f)
                dve.bn_stats(stats[:], x_sb[:])
                dve.drain()
                dve.bn_aggr(mv[:], stats[:]).then_inc(stat_done, 1)
                dve.wait_ge(stat_done, f + 1)
                dve.tensor_scalar(ve[:], mv[:, 1:2], LN_EPS, None, ALU.add).then_inc(ln_ready, 1)
                dve.tensor_scalar(nmean[:], mv[:, 0:1], -1.0, None, ALU.mult).then_inc(ln_ready, 1)

            def add_x(p, s):
                dve.wait_ge(y_done, p + 1)
                dve.tensor_tensor(xb[s][:], Y[:], xb[s][:], ALU.add).then_inc(x1_ready, 1)

            def body(p, s, step):
                front, back = step != "last", step != "first"
                f, fs = p + 1, (1 - s) if back else 0
                if front:
                    norm_stats(f)
                if back and later(p, 1):
                    add_x(p - 1, 1 - s)
                if front:
                    dve.wait_ge(rstd_ready, f + 1)
                    if back:
                        if later(p, 1):
                            dve.wait_ge(t_free[0], turn(0, "hqh", *before(p)) + 1)
                        else:
                            dve.wait_ge(t_free[0], turn(0, "hc", *before(p)) + 1)
                        dve.wait_ge(s1_ready, f)
                    dve.tensor_scalar(tok_rows[:], x_sb[:], nmean[:, 0:1], rstd[:, 0:1], ALU.add, ALU.mult).then_inc(hc_ready, 1)
                    drain_ctx(dve, copy, 1, 0, p, fs, step, only=(1,))
                if back:
                    row = T[1][0:1, 0:P].rearrange("o (b i) -> o b i", b=2)
                    dve.wait_ge(t_full[1], turn(1, "trow", p, step) + 1)
                    dve.tensor_reduce(nrm[:], row, axis=AX.X, op=ALU.max, negate=True).then_inc(nrm_done, 1)
                    dve.wait_ge(nrm_done, p + 1)
                    dve.wait_ge(brow_ready, p)
                    dve.tensor_tensor(erow[:].rearrange("o (b i) -> o b i", b=2), row,
                                      nrm[:, :, None].to_broadcast([1, 2, 64]), ALU.add).then_inc(t_free[1], 1)
                if front:
                    drain_ctx(dve, copy, 1, 0, p, fs, step, only=(3, 5))
                    dve.wait_ge(hc_ready, f + 1)
                    dve.wait_ge(tcol_ready, f)
                    if later(p, 1):
                        dve.wait_ge(t_free[0], turn(0, "hqh", *before(p)) + 1)
                    dve.tensor_tensor_reduce(out=f3[:].rearrange("p c i -> p (c i)"), in0=tok_rows[:], in1=w1_b[:], scale=1.0, scalar=0.0,
                                             op0=ALU.mult, op1=ALU.add, accum_out=s1[:]).then_inc(s1_ready, 1)
                    dve.wait_ge(t_free[0], turn(0, "hc", p, step) + 1)
                    dve.wait_ge(qk_done, NBLK * f)
                    for c in range(C):
                        dve.tensor_scalar(qT[:, c, :], hcT[fs][:, c, :], w3T[:, c:c + 1], w2T[:, c:c + 1],
                                          ALU.mult, ALU.add).then_inc(q_ready, 1)
                if back:
                    dve.wait_ge(erow_ready, p + 1)
                    e3 = erow[:].rearrange("o (b i) -> o b i", b=2)
                    dve.tensor_reduce(rsum[:], e3, axis=AX.X, op=ALU.add).then_inc(bsm_done, 1)
                    dve.wait_ge(bsm_done, 2 * p + 1)
                    dve.reciprocal(rinv[:], rsum[:]).then_inc(bsm_done, 1)
                    dve.wait_ge(bsm_done, 2 * p + 2)
                    dve.wait_ge(brow_full, p)
                    dve.tensor_tensor(brow[:].rearrange("o (b i) -> o b i", b=2), e3,
                                      rinv[:, :, None].to_broadcast([1, 2, 64]), ALU.mult).then_inc(brow_ready, 1)
                    dve.wait_ge(brow_full, p + 1)
                    if front:
                        dve.wait_ge(s1_ready, f + 1)
                    else:
                        dve.wait_ge(hcb_done, p)
                    dve.tensor_tensor(f3[:], hcT[s][:], Y[:, None, 0:P].to_broadcast([P, C, P]),
                                      ALU.mult).then_inc(hcb_step, 1)
                    dve.wait_ge(hcb_step, p + 1)
                    dve.wait_ge(wb_step, 4 * p)
                    dve.tensor_reduce(hcb[:], f3[:].rearrange("p c (b i) -> p c b i", b=2), axis=AX.X,
                                      op=ALU.add).then_inc(hcb_done, 1)
                if first(p):
                    dve.wait_ge(w12H_ready, 1)
                    dve.tensor_tensor(w12L[:], wb[:].rearrange("p b c d -> p (b c) d"), w12H[:].bitcast(F32), ALU.subtract).then_inc(w12L_ready, 1)
                if step == "last":
                    dve.wait_ge(hcb_done, p + 1)
                    dve.wait_ge(y_done, p)
                    for b in range(2):
                        for c in range(C):
                            op = dve.scalar_tensor_tensor(wb[:, b, c, :], w3[:, c, :], hcb[:, c, b:b + 1], w0[:, c, :],
                                                          ALU.mult, ALU.add)
                            if c % 2:
                                op.then_inc(wb_step, 1)
                if front:
                    drain_ctx(dve, copy, 1, 1, p, fs, step)
                if front:
                    for j in range(2, NBLK):
                        drain_ctx(dve, copy, 1, j, p, fs, step)
                        bank_max(j - 2, f)
                if back:
                    dve.wait_ge(hqhH_ready, p + 1)
                    dve.wait_ge(hcb_done, p + 1)
                    dve.wait_ge(y_done, p)
                    dve.tensor_tensor(hqhL[:], T[0][:].rearrange("p (c i) -> p c i", c=C), hqhH[:].bitcast(F32),
                                      ALU.subtract).then_inc(hqhL_ready, 1)
                    dve.tensor_tensor(f3[:], hcT[s][:], T[0][:].rearrange("p (c i) -> p c i", c=C),
                                      ALU.mult).then_inc(f2_ready, 1)
                if front:
                    bank_max(3, f)
                    dve.wait_ge(mx_done, 5 * f + 4)
                    dve.tensor_reduce(mx[:], mx4[:], axis=AX.X, op=ALU.max).then_inc(mx_done, 1)
                    dve.wait_ge(mx_done, 5 * f + 5)
                    dve.tensor_scalar(nmx[:], mx[:], -1.0, None, ALU.mult).then_inc(nmx_ready, 1)
                    dve.wait_ge(s1_ready, f + 1)
                    dve.tensor_scalar(tcol[:], mx[:], s1[:, 0:1], bsim_b[:, 0:1], ALU.add, ALU.add).then_inc(tcol_ready, 1)
                if back:
                    dve.wait_ge(f2H_ready, p + 1)
                    dve.tensor_tensor(f2L[:], f3[:], f2H[:].bitcast(F32), ALU.subtract).then_inc(t_free[0], 1)
                if front:
                    dve.wait_ge(exp_done, 4 * f + 4)
                    dve.tensor_reduce(zsum[:], z4[:], axis=AX.X, op=ALU.add).then_inc(z_done, 1)
                    dve.wait_ge(z_done, f + 1)
                    dve.wait_ge(hqh_ready, f)
                    dve.reciprocal(rz[:], zsum[:]).then_inc(rz_ready, 1)
                    drain_probs(dve, copy, 1, p, step)

            def bank_max(k, f):
                dve.wait_ge(qk_done, NBLK * f + (k + 1 if k < 3 else NBLK))
                dve.tensor_reduce(mx4[:, k:k + 1], S[:, k, 0:bank_cols(k)], axis=AX.X, op=ALU.max).then_inc(mx_done, 1)

            steps(dve, body)
            add_x(PAIRS - 1, 1)

    nc.clear_and_free_semaphores(sems)
    nc.all_engine_barrier()


def make_identity(nc, ident):
    with nc.semaphore("ident_zero") as ident_zero, nc.Block() as block:
        @block.gpsimd
        def _(pool):
            pool.memset(ident[:], 0.0).then_inc(ident_zero, 1)
            pool.wait_ge(ident_zero, 1)
            pool.affine_select(out=ident[:], in_=ident[:], compare_op=ALU.not_equal, fill=1.0, base=0,
                               pattern=[[-1, P]], channel_multiplier=1).then_inc(ident_zero, 1)


class RecurrenceWeights:

    def __init__(self, nc, sh, Wr, Wo, decay, ln_w, ln_b, bo, gate_w, stack):
        def sb(name, shape):
            return stack.enter_context(nc.sbuf_tensor(name, shape, F32))

        self.Wr, self.Wo = (sb(n, [P, sh.C, sh.D]) for n in ("wr_rows", "wo_rows"))
        self.ln_w, self.ln_b, self.bo = (sb(n, [P, sh.D]) for n in ("lnw_b", "lnb_b", "bo_b"))
        self.gate_w = sb("gw", [sh.E, sh.D])
        self.decay = sb("dec_h", [P, P])
        self.transfers = [(rows[:], src.rearrange("(k p) d -> p k d", p=P)) for rows, src in ((self.Wr, Wr), (self.Wo, Wo))]
        self.transfers += [(rows[:], bcast_row(src)) for rows, src in ((self.ln_w, ln_w), (self.ln_b, ln_b), (self.bo, bo))]
        self.transfers += [(self.gate_w[:], gate_w)]
        self.transfers += [(self.decay[c * sh.B:(c + 1) * sh.B, :],
                            decay[c * P:(c + 1) * P].rearrange("(o d) -> o d", o=1).to_broadcast([sh.B, P])) for c in range(sh.C)]
        self.loaded = stack.enter_context(nc.semaphore("recurrence_w_in"))
        self.u, self.c = ([sb(f"g_{n}{s}", [P, sh.D]) for s in range(2)] for n in "uc")
        self.uc_out = [stack.enter_context(nc.semaphore(f"uc_out{s}")) for s in range(2)]
        self.all_out = 32 * (sh.N // P // 2)
        self.all_loaded = 16 * len(self.transfers)

    def load(self, eng):
        for dst, src in self.transfers:
            eng.dma_start(dst, src).then_inc(self.loaded, 16)


class GatesAhead:

    def __init__(self, nc, sh, x1, Wg, x2, stack):
        self.tiles = 8
        self.wg_rows = x2[:, self.tiles:self.tiles + sh.C, :]
        self.x_in, self.w_in = (stack.enter_context(nc.semaphore(n)) for n in ("gates_x_in", "gates_w_in"))
        self.transfers = [(self.wg_rows, Wg.rearrange("(k p) d -> p k d", p=P), self.w_in),
                          (x2[:, 0:self.tiles, :], x1[0:self.tiles].rearrange("k p d -> p k d"), self.x_in)]

    def load(self, eng):
        for dst, src, done in self.transfers:
            eng.dma_start(dst, src).then_inc(done, 16)


def recurrence_gates(nc, sh, ident, x1, bg, br, decay, u_d, c_d, rw, rt, ahead):
    D, C, N = sh.D, sh.C, sh.N
    TILES = N // P
    with ExitStack() as stack:
        def sb(name, shape, dt=F32):
            return stack.enter_context(nc.sbuf_tensor(name, shape, dt))

        def sem(name):
            return stack.enter_context(nc.semaphore(name))

        wg_rows = ahead.wg_rows
        wgH, wgL = sb("wgH", [P, C, D], F32R), sb("wgL", [P, C, D], F32R)
        bg_b = sb("bg_b", [P, D])
        br_b = sb("br_b", [P, D])
        om_b = sb("om_b", [P, D])
        dec_b = sb("dec_b", [P, D])
        xt = rt.x2
        xn = [sb(f"g_xn{s}", [P, D]) for s in range(2)]
        xnH = [sb(f"g_xnH{s}", [P, C, P], F32R) for s in range(2)]
        xnL = [sb(f"g_xnL{s}", [P, C, P], F32R) for s in range(2)]
        zt = [sb(f"zt{s}", [P, D]) for s in range(2)]
        z = [sb(f"z{s}", [P, D]) for s in range(2)]
        xm = [sb(f"xm{s}", [P, D]) for s in range(4)]
        u, cc = rw.u, rw.c
        stats = sb("g_stats", [P, 6])
        mv = sb("g_mv", [P, 2])
        ve, nmean, rstd, nr = ([sb(f"g_{n}{s}", [P, 1]) for s in range(2)] for n in ("ve", "nmean", "rstd", "nr"))
        mhalf = sb("g_mhalf", [P, 1])
        T = [stack.enter_context(nc.psum_tensor(f"g_T{s}", [P, 512], F32)) for s in range(2)]
        Z = [stack.enter_context(nc.psum_tensor(f"g_Z{s}", [P, 512], F32)) for s in range(2)]
        WT = T + Z

        row_in = sem("g_row_in")
        x_mid, x_end = sem("g_x_mid"), sem("g_x_end")
        MID, END = ahead.tiles, ahead.tiles + C
        uc_out = rw.uc_out
        half_set = sem("g_half_set")
        om_done = sem("g_om_done")
        wT_full = sem("g_wT_full")
        wH_ready, wL_ready = sem("g_wH_ready"), sem("g_wL_ready")
        stat_done = sem("g_stat_done")
        ln_ready = sem("g_ln_ready")
        rstd_ready, nr_ready = sem("g_rstd_ready"), sem("g_nr_ready")
        xn_ready = sem("g_xn_ready")
        xT_full = sem("g_xT_full")
        xnH_ready, xnL_ready = sem("g_xnH_ready"), sem("g_xnL_ready")
        z_full = sem("g_z_full")
        zt_ready = sem("g_zt_ready")
        z_ready = sem("g_z_ready")
        xm_ready = sem("g_xm_ready")
        u_ready = sem("g_u_ready")
        c_ready = sem("g_c_ready")
        block = stack.enter_context(nc.Block())

        u_rows = u_d.rearrange("(c b) l e -> (b l) c e", c=C)
        c_rows = c_d.rearrange("(c b) l e -> (b l) c e", c=C)

        @block.sync
        def _(sp):
            sp.dma_start(bg_b[:], bcast_row(bg)).then_inc(row_in, 16)
            sp.dma_start(br_b[:], bcast_row(br)).then_inc(row_in, 16)
            sp.dma_start(dec_b[:], bcast_row(decay)).then_inc(row_in, 16)
            sp.dma_start(xt[:, END:TILES, :], x1[END:TILES].rearrange("k p d -> p k d")).then_inc(x_end, 16)
            rw.load(sp)
            sp.wait_ge(wT_full, C)
            sp.dma_start(xt[:, MID:END, :], x1[MID:END].rearrange("k p d -> p k d")).then_inc(x_mid, 16)

            def store(k, s):
                base = bass.ds(k * P, P) if isinstance(k, int) else bass.ds(sp.snap(k * P), P)
                sp.wait_ge(u_ready, k + 1)
                sp.dma_start(u_rows[base], u[s][:].rearrange("p (c e) -> p c e", c=C)).then_inc(uc_out[s], 16)
                sp.wait_ge(c_ready, k + 1)
                sp.dma_start(c_rows[base], cc[s][:].rearrange("p (c e) -> p c e", c=C)).then_inc(uc_out[s], 16)

            with sp.Fori(0, TILES // 2) as i:
                store(2 * i, 0)
                store(2 * i + 1, 1)

        @block.gpsimd
        def _(pool):
            pool.memset(mhalf[:], -0.5).then_inc(half_set, 1)
            pool.wait_ge(half_set, 1)

            def power(k, s):
                pool.wait_ge(ln_ready, 2 * k + 2)
                if later(k, 2):
                    pool.wait_ge(xn_ready, k - 1)
                pool.tensor_tensor(rstd[s][:], ve[s][:], mhalf[:], ALU.pow).then_inc(rstd_ready, 1)
                pool.wait_ge(rstd_ready, k + 1)
                pool.tensor_tensor(nr[s][:], nmean[s][:], rstd[s][:], ALU.mult).then_inc(nr_ready, 1)

            def less_br(k, m):
                pool.wait_ge(xn_ready, k + 1)
                if later(k, 4):
                    pool.wait_ge(c_ready, k - 3)
                pool.tensor_tensor(xm[m][:], xn[m % 2][:], br_b[:], ALU.subtract).then_inc(xm_ready, 1)

            def c_product(k, m, stored):
                s = m % 2
                pool.wait_ge(u_ready, k + 1)
                pool.wait_ge(xm_ready, k + 1)
                if later(k, 2):
                    pool.wait_ge(uc_out[s], 32 * stored)
                pool.tensor_tensor(cc[s][:], u[s][:], xm[m][:], ALU.mult).then_inc(c_ready, 1)

            def step(k, m, stored):
                if not (isinstance(k, int) and k + 2 >= TILES):
                    power(k + 2, m % 2)
                if not (isinstance(k, int) and k + 1 >= TILES):
                    less_br(k + 1, (m + 1) % 4)
                if later(k, 2):
                    c_product(k - 2, (m - 2) % 4, stored)

            power(0, 0)
            power(1, 1)
            pool.wait_ge(row_in, 48)
            less_br(0, 0)
            for k in range(4):
                step(k, k, (k - 2) // 2)
            with pool.Fori(1, TILES // 4 - 1) as i:
                for m in range(4):
                    step(4 * i + m, m, 2 * i + (m - 2) // 2)
            for k in range(TILES - 4, TILES):
                step(k, k % 4, (k - 2) // 2)
            for k in (TILES - 2, TILES - 1):
                c_product(k, k % 4, k // 2)

        @block.tensor
        def _(pe):
            pe.wait_ge(ahead.w_in, 16)
            for k in range(C):
                for c in range(C):
                    last = pe.transpose(WT[k][:, c * P:(c + 1) * P], wg_rows[:, k, c * P:(c + 1) * P], ident[:])
                last.then_inc(wT_full, 1)
            pe.wait_ge(wL_ready, C)

            def turn(k, s):
                pe.wait_ge(xn_ready, k + 1)
                if later(k, 2):
                    pe.wait_ge(xnL_ready, k - 1)
                for c in range(C):
                    last = pe.transpose(T[s][:, c * P:(c + 1) * P], xn[s][:, c * P:(c + 1) * P], ident[:])
                last.then_inc(xT_full, 1)

            def gates(k, s):
                pe.wait_ge(xnL_ready, k + 1)
                if later(k, 2):
                    pe.wait_ge(zt_ready, k - 1)
                for c in range(C):
                    pe.matmul(Z[s][:], xnH[s][:, c, :], wgH[:, c, :], start=(c == 0), stop=False)
                    pe.matmul(Z[s][:], xnH[s][:, c, :], wgL[:, c, :], start=False, stop=False)
                    last = pe.matmul(Z[s][:], xnL[s][:, c, :], wgH[:, c, :], start=False, stop=(c == C - 1))
                last.then_inc(z_full, 1)

            turn(0, 0)
            turn(1, 1)
            gates(0, 0)
            with pe.Fori(0, TILES // 2 - 1) as i:
                turn(2 * i + 2, 0)
                gates(2 * i + 1, 1)
                turn(2 * i + 3, 1)
                gates(2 * i + 2, 0)
            gates(TILES - 1, 1)

        @block.scalar
        def _(act):
            for k in range(C):
                act.wait_ge(wT_full, k + 1)
                act.copy(wgH[:, :, k * P:(k + 1) * P], WT[k][:].rearrange("p (c e) -> p c e", c=C)).then_inc(wH_ready, 1)

            def norm(k, s):
                tile = xt[:, k if isinstance(k, int) else act.snap(k), :]
                act.wait_ge(ahead.x_in, 16)
                act.wait_ge(nr_ready, k + 1)
                if later(k, 2):
                    act.wait_ge(xT_full, k - 1)
                    act.wait_ge(xm_ready, k - 1)
                act.activation(xn[s][:], tile, ACT.Identity, scale=rstd[s][:, 0:1], bias=nr[s][:, 0:1]).then_inc(xn_ready, 1)

            def drain(k, s):
                act.wait_ge(xT_full, k + 1)
                if later(k, 2):
                    act.wait_ge(z_full, k - 1)
                act.copy(xnH[s][:], T[s][:].rearrange("p (c i) -> p c i", c=C)).then_inc(xnH_ready, 1)

            def gate(k, s):
                act.wait_ge(zt_ready, k + 1)
                if later(k, 2):
                    act.wait_ge(u_ready, k - 1)
                act.activation(z[s][:], zt[s][:], ACT.Sigmoid).then_inc(z_ready, 1)

            def step(k, s):
                if not (isinstance(k, int) and k + 1 >= TILES):
                    drain(k + 1, 1 - s)
                if later(k, 1):
                    gate(k - 1, 1 - s)
                if not (isinstance(k, int) and k + 2 >= TILES):
                    norm(k + 2, s)

            norm(0, 0)
            norm(1, 1)
            drain(0, 0)
            act.wait_ge(row_in, 48)
            act.activation(om_b[:], dec_b[:], ACT.Sigmoid).then_inc(om_done, 1)
            for k in range(4):
                step(k, k % 2)
            with act.Fori(2, TILES // 2 - 1) as i:
                step(2 * i, 0)
                step(2 * i + 1, 1)
            for k in (TILES - 2, TILES - 1):
                step(k, k % 2)
            gate(TILES - 1, 1)

        @block.vector
        def _(dve):
            def one_minus_decay():
                dve.wait_ge(om_done, 1)
                dve.tensor_scalar(om_b[:], om_b[:], -1.0, 1.0, ALU.mult, ALU.add).then_inc(om_done, 1)
                dve.wait_ge(om_done, 2)

            def statistics(k, s):
                tile = xt[:, k if isinstance(k, int) else dve.snap(k), :]
                dve.wait_ge(ahead.x_in, 16)
                if later(k, MID):
                    dve.wait_ge(x_mid, 16)
                    dve.wait_ge(x_end, 16)
                if later(k, 1):
                    dve.wait_ge(ln_ready, 2 * k)
                if later(k, 2):
                    dve.wait_ge(nr_ready, k - 1)
                dve.bn_stats(stats[:], tile)
                dve.drain()
                dve.bn_aggr(mv[:], stats[:]).then_inc(stat_done, 1)
                dve.wait_ge(stat_done, k + 1)
                dve.tensor_scalar(ve[s][:], mv[:, 1:2], LN_EPS, None, ALU.add).then_inc(ln_ready, 1)
                dve.tensor_scalar(nmean[s][:], mv[:, 0:1], -1.0, None, ALU.mult).then_inc(ln_ready, 1)

            def low_w(k):
                dve.wait_ge(wH_ready, k + 1)
                part = slice(k * P, (k + 1) * P)
                dve.tensor_tensor(wgL[:, :, part], WT[k][:].rearrange("p (c e) -> p c e", c=C), wgH[:, :, part].bitcast(F32),
                                  ALU.subtract).then_inc(wL_ready, 1)

            def low_x(k, s):
                dve.wait_ge(xnH_ready, k + 1)
                if later(k, 2):
                    dve.wait_ge(z_full, k - 1)
                dve.tensor_tensor(xnL[s][:], T[s][:].rearrange("p (c i) -> p c i", c=C), xnH[s][:].bitcast(F32),
                                  ALU.subtract).then_inc(xnL_ready, 1)

            def gate(k, s):
                dve.wait_ge(z_full, k + 1)
                if later(k, 2):
                    dve.wait_ge(z_ready, k - 1)
                dve.tensor_tensor(zt[s][:], Z[s][:], bg_b[:], ALU.add).then_inc(zt_ready, 1)

            def u_product(k, s, stored):
                dve.wait_ge(z_ready, k + 1)
                if later(k, 2):
                    dve.wait_ge(c_ready, k - 1)
                    dve.wait_ge(uc_out[s], 32 * stored)
                dve.tensor_tensor(u[s][:], z[s][:], om_b[:], ALU.mult).then_inc(u_ready, 1)

            def step(k, s, stored):
                if later(k, 2):
                    u_product(k - 2, s, stored)
                if not (isinstance(k, int) and k + 1 >= TILES):
                    low_x(k + 1, 1 - s)
                if not (isinstance(k, int) and k + 3 >= TILES):
                    statistics(k + 3, 1 - s)
                gate(k, s)

            statistics(0, 0)
            statistics(1, 1)
            for k in range(C):
                low_w(k)
            statistics(2, 0)
            low_x(0, 0)
            one_minus_decay()
            for k in range(4):
                step(k, k % 2, (k - 2) // 2)
            with dve.Fori(2, TILES // 2 - 2) as i:
                step(2 * i, 0, i - 1)
                step(2 * i + 1, 1, i - 1)
            for k in range(TILES - 4, TILES):
                step(k, k % 2, (k - 2) // 2)
            for k in (TILES - 2, TILES - 1):
                u_product(k, k % 2, k // 2)


class Routing:

    def __init__(self, nc, sh, x2, stack):
        self.region = P + sh.N
        self.tiles = (2 * sh.N + sh.E * (P - 1)) // P
        self.spare = self.tiles - 2 * sh.N // P
        self.rows = sh.E * self.region + self.spare * P
        tiles, E = sh.N // P, sh.E

        def sb(name, shape, dt=F32):
            return stack.enter_context(nc.sbuf_tensor(name, shape, dt))

        self.x2 = x2
        self.ew = sb("ew", [P, tiles, E])
        self.rank = sb("rank", [P, tiles, E])
        self.places = sb("places", [P, tiles, 2])
        self.second = sb("second", [P, 2])
        self.acc = sb("acc", [P, E], BF16)
        self.first_row = sb("first_row", [P, E + 1])
        self.row_i, self.slot_i, self.part_i = (sb(n, [P, self.tiles], I32) for n in ("row_i", "slot_i", "part_i"))
        self.te_i = sb("te_i", [P, E], I32)
        self.x_rows = nc.dram_tensor("routed_x", (self.rows, sh.D), F32, kind="Internal").ap()
        self.y_rows = nc.dram_tensor("routed_y", (self.tiles * P, sh.D), F32, kind="Internal").ap()


def recurrence(nc, sh, ident, x1, u_d, c_d, rw, rt, ex):
    D, C, E, B = sh.D, sh.C, sh.E, sh.B
    TILES, ST = sh.N // P, P // B
    TOP_OPS = 7
    PLACE_OPS = 4
    LAG = 6
    with ExitStack() as stack:
        def sb(name, shape, dt=F32):
            return stack.enter_context(nc.sbuf_tensor(name, shape, dt))

        def sem(name):
            return stack.enter_context(nc.semaphore(name))

        def psum(name):
            return stack.enter_context(nc.psum_tensor(name, [P, 512], F32))

        w_perm = [sb(f"w_perm{i}", [P, C, P]) for i in range(2)]
        w_scaled = sb("w_scaled", [P, D])
        w_sum, w_nmean = sb("w_sum", [P, C]), sb("w_nmean", [P, C])
        bo_col = sb("bo_col", [P, C])
        WrT = sb("WrT", [P, C, D])
        gwT = sb("gwT", [P, C, E])
        xt, xs = rw.c, rw.u
        lnw_b, lnb_b, bo_b, gw, dec_h = rw.ln_w, rw.ln_b, rw.bo, rw.gate_w, rw.decay
        df_h = sb("df_h", [P, P])
        zero = sb("zero", [P, D])
        tri = sb("tri", [P, P], BF16)
        ones = sb("r_ones", [P, P], BF16)
        ebase = sb("ebase", [P, E])
        mhalf = sb("r_mhalf", [P, 1])
        ut = [sb(f"ut{s}", [P, ST, P]) for s in range(2)]
        ct = [sb(f"ct{s}", [P, ST, P]) for s in range(2)]
        H = sb("H", [P, P])
        m = sb("m", [P, P])
        gd = sb("gd", [P, P])
        g = sb("g", [P, P])
        yT = [sb(f"yT{s}", [P, C, ST, B]) for s in range(2)]
        WoH, WoL = sb("WoH", [P, C, D], F32R), sb("WoL", [P, C, D], F32R)
        yH = [sb(f"yH{s}", [P, C, P], F32R) for s in range(2)]
        yL = [sb(f"yL{s}", [P, C, P], F32R) for s in range(2)]
        xn3 = [sb(f"xn3{s}", [P, D]) for s in range(2)]
        xn3T = sb("xn3T", [P, C, P])
        st2, st3 = sb("st2", [P, 6]), sb("st3", [P, 6])
        mv2, mv3 = sb("mv2", [P, 2]), sb("mv3", [P, 2])
        ve2, ve3 = sb("ve2", [P, 1]), sb("ve3", [P, 1])
        nm3 = sb("nm3", [P, 1])
        rs2 = [sb(f"rs2{s}", [P, 1]) for s in range(2)]
        rs3, nr3 = sb("rs3", [P, 1]), sb("nr3", [P, 1])
        nmx = sb("r_nmx", [P, 1])
        earlier = sb("earlier", [P, E, E])
        ahead, equal = sb("ahead", [P, E, E]), sb("equal", [P, E, E])
        rank, oh = sb("r_rank", [P, E]), sb("oh", [P, E], BF16)
        oh2 = sb("oh2", [P, 2, E])
        row, row2 = sb("row", [P, E]), sb("row2", [P, 2, E])
        pl = sb("pl", [P, 2])
        pl_i = sb("pl_i", [P, 2], I32)
        zero2 = sb("zero2", [P, 2], I32)
        pli = [sb(f"pli{s}", [P, 2], I32) for s in range(2)]

        tile_no = sb("tile_no", [P, rt.tiles])
        tile_no_i = sb("tile_no_i", [P, rt.tiles], I32)
        step_no = sb("step_no", [P, TILES])
        step_no_i = sb("step_no_i", [P, TILES], I32)
        low = sb("low", [P, E, E])
        base = sb("p_base", [P, E])
        cnt = sb("cnt", [P, E])
        more = sb("more", [P, E, TILES])
        nt = sb("nt", [P, E])
        upto = sb("upto", [P, E, E])
        te = sb("te", [P, E])
        jump = sb("jump", [P, E])
        past = sb("past", [P, rt.tiles, E])
        hop = sb("hop", [P, rt.tiles, E])
        rowf = sb("rowf", [P, rt.tiles])
        ef = sb("ef", [P, rt.tiles])
        s3, s6 = sb("s3", [P, rt.tiles]), sb("s6", [P, rt.tiles])
        slotf = sb("slotf", [P, rt.tiles])

        Pb, Yb, YT, Wb, XT, Lg, Rk = (psum(n) for n in ("Pb", "Yb", "YT", "Wb", "XT", "Lg", "Rk"))

        zero_set, zero_out = sem("zero_set"), sem("zero_out")
        uc_in = [sem(f"uc_in{s}") for s in range(2)]
        x_in = [sem(f"r_x_in{s}") for s in range(2)]
        consts, df_ready = sem("r_consts"), sem("df_ready")
        w_permuted, gwT_ready = sem("w_permuted"), sem("gwT_ready")
        wT_full, wT_ready = sem("r_wT_full"), sem("r_wT_ready")
        bo_step, bo_full, bo_ready = sem("bo_step"), sem("bo_full"), sem("bo_ready")
        wo_step, woH_ready, woL_ready = sem("wo_step"), sem("woH_ready"), sem("woL_ready")
        pred_full, m_done, gd_done, g_ready = sem("pred_full"), sem("m_done"), sem("gd_done"), sem("g_ready")
        h_ready, yT_ready = sem("h_ready"), sem("yT_ready")
        y_full, st2_done, ln2_ready, rs2_ready = sem("y_full"), sem("st2_done"), sem("ln2_ready"), sem("rs2_ready")
        yH_ready, yL_ready = sem("yH_ready"), sem("yL_ready")
        wo_done, xp_ready, x2_ready = sem("wo_done"), sem("xp_ready"), sem("x2_ready")
        st3_done, ln3_ready, rs3_ready = sem("st3_done"), sem("ln3_ready"), sem("rs3_ready")
        xn3_ready, xn3_full, xn3T_ready = sem("xn3_ready"), sem("xn3_full"), sem("xn3T_ready")
        lg_done, nmx_ready, ex_ready = sem("lg_done"), sem("r_nmx_ready"), sem("ex_ready")
        top_step, pfx_done, place_step, places_ready = sem("top_step"), sem("pfx_done"), sem("place_step"), sem("places_ready")
        pli_ready, xs_ready = sem("pli_ready"), sem("xs_ready")
        plan_consts, iotas, cnt_full, plan_step = sem("plan_consts"), sem("iotas"), sem("cnt_full"), sem("plan_step")
        x_scattered = [sem(f"x_scattered{s}") for s in range(2)]
        block = stack.enter_context(nc.Block())

        x1_tiles = x1.rearrange("k p d -> (k p) d").rearrange("(b k t) d -> k t b d", t=ST, k=TILES)

        def first(k):
            return isinstance(k, int) and k == 0

        def k1(k):
            return isinstance(k, int) and k == 1

        def has(j):
            return not isinstance(j, int) or 0 <= j < TILES

        def walk(eng, body):
            for k in range(LAG):
                body(k, k % 2, True, k // 2 + 1)
            with eng.Fori(LAG // 2, TILES // 2) as i:
                body(2 * i, 0, True, i + 1)
                body(2 * i + 1, 1, True, i + 1)
            for k in range(TILES, TILES + LAG):
                body(k, k % 2, False, None)

        def idx(eng, k):
            return k if isinstance(k, int) else eng.snap(k)

        @block.sync
        def _(sp):
            def load_uc(k, s):
                steps = bass.ds(k * ST, ST) if isinstance(k, int) else bass.ds(sp.snap(k * ST), ST)
                sp.dma_start(ut[s][:], u_d[:, steps, :]).then_inc(uc_in[s], 16)
                sp.dma_start(ct[s][:], c_d[:, steps, :]).then_inc(uc_in[s], 16)

            for s in range(2):
                sp.wait_ge(rw.uc_out[s], rw.all_out)
            load_uc(0, 0)
            load_uc(1, 1)

            def load_x(k, s):
                sp.dma_start(xt[s][:], x1_tiles[k]).then_inc(x_in[s], 16)

            pads = [e * rt.region for e in range(E)] + [E * rt.region + i * P for i in range(rt.spare)]

            first_unwritten = sh.N // P
            unwritten = [range(first_unwritten + i, rt.tiles, LAG) for i in range(LAG)]

            def load_ahead(k):
                if k == 0:
                    sp.wait_ge(zero_set, 1)
                for r in pads[k::LAG]:
                    sp.dma_start(rt.x_rows[r:r + P, :], zero[:]).then_inc(zero_out, 16)
                for t in unwritten[k]:
                    sp.dma_start(rt.y_rows[t * P:(t + 1) * P, :], zero[:]).then_inc(zero_out, 16)
                for i in range(3 * k // 2, 3 * (k + 1) // 2):
                    ex.load(sp, i // ex.PARTS, i % ex.PARTS)

            def body(k, s, more):
                nxt = k + 2 if isinstance(k, int) else sp.snap(k + 2)
                cur = idx(sp, k)
                if more:
                    sp.wait_ge(h_ready, ST * k + ST)
                    load_uc(nxt, s)
                if later(k, 2):
                    sp.wait_ge(x2_ready, k - 1)
                load_x(cur, s)

            assert 3 * LAG // 2 == ex.SLOTS * ex.PARTS
            for k in range(LAG):
                body(k, k % 2, True)
                load_ahead(k)
            with sp.Fori(LAG // 2, TILES // 2 - 1) as i:
                body(2 * i, 0, True)
                body(2 * i + 1, 1, True)
            for k in range(TILES - 2, TILES):
                body(k, k % 2, False)
            sp.wait_ge(zero_out, 16 * (len(pads) + sum(len(u) for u in unwritten)))

        @block.gpsimd
        def _(pool):
            pool.memset(mhalf[:], -0.5).then_inc(consts, 1)
            pool.memset(zero[:], 0.0).then_inc(zero_set, 1)
            pool.memset(ones[:], 1.0).then_inc(consts, 1)
            pool.memset(zero2[:], 0).then_inc(consts, 1)
            pool.memset(rt.acc[:], 0.0).then_inc(consts, 1)
            pool.memset(rt.second[:, 0:1], 0.0).then_inc(consts, 1)
            pool.memset(rt.second[:, 1:2], 1.0).then_inc(consts, 1)
            pool.memset(earlier[:], 0.0).then_inc(consts, 1)
            pool.wait_ge(consts, 7)
            for e in range(E):
                pool.memset(ebase[:, e:e + 1], float(e * rt.region + P)).then_inc(consts, 1)
                if e:
                    pool.memset(earlier[:, e, 0:e], 1.0).then_inc(consts, 1)
            pool.wait_ge(consts, 6 + 2 * E)
            pool.affine_select(out=tri[:], in_=ones[:], compare_op=ALU.is_gt, fill=0.0, base=0,
                               pattern=[[1, P]], channel_multiplier=-1).then_inc(consts, 1)
            pool.iota(tile_no_i[:], pattern=[[1, rt.tiles]], base=0, channel_multiplier=0).then_inc(iotas, 1)
            pool.iota(step_no_i[:], pattern=[[1, TILES]], base=0, channel_multiplier=0).then_inc(iotas, 1)
            pool.memset(low[:], 0.0).then_inc(plan_consts, 1)
            pool.wait_ge(plan_consts, 1)
            for e in range(E):
                pool.memset(low[:, e, 0:e + 1], 1.0).then_inc(plan_consts, 1)
                pool.memset(base[:, e:e + 1], float(e * rt.region + P)).then_inc(plan_consts, 1)
            pool.wait_ge(df_ready, 1)

            def scatter(j, s, which):
                if which == 0:
                    pool.wait_ge(xs_ready, j + 1)
                    pool.wait_ge(places_ready, j + 1)
                    pool.tensor_tensor(pli[s][:], pl_i[:], zero2[:], ALU.add).then_inc(pli_ready, 1)
                    pool.drain()
                pool.indirect_dma_start(out=rt.x_rows,
                                        out_offset=bass.IndirectOffsetOnAxis(ap=pli[s][:, which:which + 1], axis=0),
                                        in_=xs[s][:], in_offset=None).then_inc(x_scattered[s], 16)

            def power2(j, s):
                pool.wait_ge(ln2_ready, j + 1)
                if later(j, 2):
                    pool.wait_ge(x2_ready, j - 1)
                pool.tensor_tensor(rs2[s][:], ve2[:], mhalf[:], ALU.pow).then_inc(rs2_ready, 1)

            def power3(j):
                pool.wait_ge(ln3_ready, 2 * (j + 1))
                if later(j, 1):
                    pool.wait_ge(xn3_ready, j)
                pool.tensor_tensor(rs3[:], ve3[:], mhalf[:], ALU.pow).then_inc(rs3_ready, 1)
                pool.wait_ge(rs3_ready, 2 * j + 1)
                pool.tensor_tensor(nr3[:], nm3[:], rs3[:], ALU.mult).then_inc(rs3_ready, 1)

            def add_bo(j, s, half, loads):
                cols = slice(half * D // 2, (half + 1) * D // 2)
                if half == 0:
                    pool.wait_ge(x_in[s], 16 * loads)
                if first(j):
                    pool.wait_ge(bo_ready, 1)
                pool.tensor_tensor(xt[s][:, cols], xt[s][:, cols], bo_b[:, cols], ALU.add).then_inc(xp_ready, 1)

            def body(k, s, scan, loads):
                for st in range(ST):
                    if scan and not (st == 0 and first(k)):
                        t = ST * k + st
                        pool.wait_ge(h_ready, t)
                        if st == 0:
                            pool.wait_ge(uc_in[s], 32 * loads)
                        pool.tensor_tensor(gd[:], H[:], df_h[:], ALU.mult).then_inc(gd_done, 1)
                        pool.wait_ge(gd_done, t)
                        pool.tensor_tensor(g[:], gd[:], ct[s][:, st, :], ALU.add).then_inc(g_ready, 1)
                    if st == 0 and has(k - 6):
                        scatter(k - 6, s, 1)
                    if st == 1 and has(k - 3):
                        power3(k - 3)
                    if st == 2 and has(k - 1):
                        power2(k - 1, 1 - s)
                    if st in (1, 2) and has(k - 2):
                        add_bo(k - 2, s, st - 1, loads - 1 if scan else k // 2)
                    if st == 3 and has(k - 5):
                        scatter(k - 5, 1 - s, 0)

            walk(pool, body)
            for s in range(2):
                pool.wait_ge(x_scattered[s], 16 * TILES)

        @block.tensor
        def _(pe):
            def turn_weight(n):
                pe.wait_ge(w_permuted, n + 1)
                if n >= 2:
                    pe.wait_ge(wT_ready if n < C + 2 else woL_ready, n - 1 if n < C + 2 else n - C - 1)
                for c in range(C):
                    last = pe.transpose((YT, XT)[n % 2][:, c * P:(c + 1) * P], w_perm[n % 2][:, c, :], ident[:])
                last.then_inc(wT_full, 1)

            for n in range(C):
                turn_weight(n)
            pe.wait_ge(wT_ready, C)

            def bo_product(c):
                pe.wait_ge(bo_step, c + 1)
                pe.matmul(Wb[:, c * P:(c + 1) * P], bo_col[:, c:c + 1].to_broadcast([P, P]), ident[:],
                          start=True, stop=True).then_inc(bo_full, 1)

            def turn_router():
                pe.wait_ge(rw.loaded, rw.all_loaded)
                for c in range(C):
                    last = pe.transpose(Lg[:, c * E:(c + 1) * E], gw[:, c * P:(c + 1) * P], ident[0:E, 0:E])
                last.then_inc(wT_full, 1)

            def predict(k, s, st):
                pe.wait_ge(yT_ready, ST * k + st)
                src, prev = (yT[s], st - 1) if st else (yT[1 - s], ST - 1)
                for c in range(C):
                    for o in range(C):
                        last = pe.matmul(Pb[o * B:(o + 1) * B, 0:P], src[:, c, prev, :], WrT[:, c, o * P:(o + 1) * P],
                                         start=(c == 0), stop=(c == C - 1))
                last.then_inc(pred_full, 1)

            def logits(c0, c1):
                for c in range(c0, c1):
                    last = pe.matmul(Lg[:, 0:B], xn3T[:, c, :], gwT[:, c, None, :].to_broadcast([P, B // E, E]),
                                     start=(c == 0), stop=(c == C - 1))
                return last

            def body(k, s, scan, loads):
                for st in range(ST):
                    if scan and not (st == 0 and first(k)):
                        predict(k, s, st)
                    if first(k):
                        turn_weight(C + st)
                        bo_product(st)
                    if k1(k) and st == 0:
                        turn_router()
                    if has(k - 2):
                        if st == 0:
                            pe.wait_ge(yL_ready, k - 1)
                            if has(k - 3):
                                pe.wait_ge(x2_ready, k - 2)
                            if first(k - 2):
                                pe.wait_ge(woL_ready, C)
                        pe.matmul(Wb[:], yH[s][:, st, :], WoH[:, st, :], start=(st == 0), stop=False)
                        pe.matmul(Wb[:], yH[s][:, st, :], WoL[:, st, :], start=False, stop=False)
                        mm = pe.matmul(Wb[:], yL[s][:, st, :], WoH[:, st, :], start=False, stop=(st == C - 1))
                        if st == ST - 1:
                            mm.then_inc(wo_done, 1)
                    if st == 1 and has(k - 5):
                        pe.wait_ge(top_step, TOP_OPS * (k - 4))
                        if has(k - 6):
                            pe.wait_ge(places_ready, k - 5)
                        pe.matmul(Rk[:, 0:P], tri[:], oh[:, None, :].to_broadcast([P, P // E, E]), start=True, stop=False)
                        pe.matmul(Rk[:, 0:P], ones[:], rt.acc[:, None, :].to_broadcast([P, P // E, E]),
                                  start=False, stop=True).then_inc(pfx_done, 1)
                    if st == 0 and has(k - 1):
                        if has(k - 2):
                            pe.wait_ge(st2_done, k - 1)
                        if not scan:
                            pe.wait_ge(yT_ready, ST * k)
                        for c in range(C):
                            last = pe.transpose(Yb[:, c * P:(c + 1) * P], yT[1 - s][:, c].rearrange("p t b -> p (t b)"), ident[:])
                        last.then_inc(y_full, 1)
                    if st == 2 and has(k - 3):
                        pe.wait_ge(xn3_ready, k - 2)
                        if has(k - 4):
                            pe.wait_ge(xn3T_ready, k - 3)
                        for c in range(C):
                            last = pe.transpose(XT[:, c * P:(c + 1) * P], xn3[1 - s][:, c * P:(c + 1) * P], ident[:])
                        last.then_inc(xn3_full, 1)
                    if st == 3 and has(k - 3):
                        pe.wait_ge(xn3T_ready, k - 2)
                        if first(k - 3):
                            pe.wait_ge(gwT_ready, 1)
                        if has(k - 4):
                            pe.wait_ge(ex_ready, k - 3)
                        logits(0, C // 2)
                    if st == 1 and has(k - 4):
                        logits(C // 2, C).then_inc(lg_done, 1)

            walk(pe, body)
            pe.wait_ge(places_ready, TILES)
            pe.matmul(Rk[:, 0:P], ones[:], rt.acc[:, None, :].to_broadcast([P, P // E, E]), start=True, stop=True).then_inc(cnt_full, 1)

        @block.scalar
        def _(act):
            for n in range(C):
                act.wait_ge(wT_full, n + 1)
                act.copy(WrT[:, :, n * P:(n + 1) * P], (YT, XT)[n % 2][:].rearrange("p (c e) -> p c e", c=C)).then_inc(wT_ready, 1)
            act.wait_ge(rw.loaded, rw.all_loaded)
            act.activation(df_h[:], dec_h[:], ACT.Sigmoid).then_inc(df_ready, 1)

            def take_wo(k):
                act.wait_ge(wT_full, C + k + 1)
                act.copy(WoH[:, :, k * P:(k + 1) * P],
                         (YT, XT)[k % 2][:].rearrange("p (c e) -> p c e", c=C)).then_inc(woH_ready, 1)

            def take_router():
                act.wait_ge(wT_full, 2 * C + 1)
                act.copy(gwT[:], Lg[:, 0:C * E].rearrange("p (c e) -> p c e", c=C)).then_inc(gwT_ready, 1)

            def body(k, s, scan, loads):
                for st in range(ST):
                    if first(k):
                        take_wo(st)
                    if st == 0 and k1(k):
                        take_router()
                    if st == 0 and has(k - 1):
                        if has(k - 3):
                            act.wait_ge(wo_done, k - 2)
                        act.wait_ge(yT_ready, ST * k)
                        act.copy(yH[1 - s][:], yT[1 - s][:].rearrange("p c t b -> p c (t b)")).then_inc(yH_ready, 1)
                    if st == 1 and has(k - 3):
                        j = k - 3
                        tile = rt.x2[:, idx(act, j), :]
                        act.wait_ge(df_ready, 1)
                        act.wait_ge(rs3_ready, 2 * (j + 1))
                        if has(k - 5):
                            act.wait_ge(xs_ready, j - 1)
                        act.activation(xn3[1 - s][:], tile, ACT.Identity, scale=rs3[:, 0:1], bias=nr3[:, 0:1]).then_inc(xn3_ready, 1)
                    if st == 2 and has(k - 4):
                        tile = rt.ew[:, idx(act, k - 4), :]
                        act.wait_ge(df_ready, 1)
                        act.wait_ge(nmx_ready, k - 3)
                        act.activation(tile, Lg[:, 0:E], ACT.Exp, bias=nmx[:, 0:1]).then_inc(ex_ready, 1)
                    if st == 3 and has(k - 4):
                        if has(k - 6):
                            act.wait_ge(x_scattered[s], 32 * (loads - 3) if scan else 32 * ((k - 4) // 2))
                        act.copy(xs[s][:], xn3[s][:]).then_inc(xs_ready, 1)
                    if st == 2 and has(k - 3):
                        act.wait_ge(xn3_full, k - 2)
                        if has(k - 4):
                            act.wait_ge(lg_done, k - 3)
                        act.copy(xn3T[:], XT[:].rearrange("p (c i) -> p c i", c=C)).then_inc(xn3T_ready, 1)
            walk(act, body)

        @block.vector
        def _(dve):
            def permute(n, src):
                if n >= 2:
                    dve.wait_ge(wT_full, n - 1)
                return (w_perm[n % 2][:].rearrange("p q (c r) -> p q c r", r=B),
                        src.rearrange("p (c q r) -> p q c r", q=C, r=B))

            dve.wait_ge(rw.loaded, rw.all_loaded)
            for n in range(C):
                dst, src = permute(n, rw.Wr[:, n])
                dve.tensor_copy(dst, src).then_inc(w_permuted, 1)

            def prepare_wo(k):
                if k:
                    dve.wait_ge(w_permuted, C + k)
                dve.tensor_tensor_reduce(out=w_scaled[:], in0=rw.Wo[:, k], in1=lnb_b[:], scale=1.0, scalar=0.0,
                                         op0=ALU.mult, op1=ALU.add, accum_out=bo_col[:, k:k + 1]).then_inc(bo_step, 1)
                dve.wait_ge(bo_step, k + 1)
                dve.tensor_tensor_reduce(out=w_scaled[:], in0=rw.Wo[:, k], in1=lnw_b[:], scale=1.0, scalar=0.0,
                                         op0=ALU.mult, op1=ALU.add, accum_out=w_sum[:, k:k + 1]).then_inc(wo_step, 1)
                dve.wait_ge(wo_step, 2 * k + 1)
                dve.tensor_scalar(w_nmean[:, k:k + 1], w_sum[:, k:k + 1], -1.0 / D, None, ALU.mult).then_inc(wo_step, 1)
                dve.wait_ge(wo_step, 2 * k + 2)
                dst, src = permute(C + k, w_scaled[:])
                dve.tensor_scalar(dst, src, w_nmean[:, k:k + 1], None, ALU.add).then_inc(w_permuted, 1)

            def low_wo(k):
                part = slice(k * P, (k + 1) * P)
                dve.wait_ge(woH_ready, k + 1)
                dve.tensor_tensor(WoL[:, :, part], (YT, XT)[k % 2][:].rearrange("p (c e) -> p c e", c=C),
                                  WoH[:, :, part].bitcast(F32), ALU.subtract).then_inc(woL_ready, 1)

            def add_lnb():
                dve.wait_ge(bo_full, C)
                dve.tensor_tensor(bo_b[:], bo_b[:], Wb[:], ALU.add).then_inc(bo_ready, 1)

            prepare_wo(0)
            dve.wait_ge(consts, 7 + 2 * E)

            def norm_stats(src, st, mv, ve, nm, done, ready, j):
                dve.bn_stats(st[:], src)
                dve.drain()
                dve.bn_aggr(mv[:], st[:]).then_inc(done, 1)
                dve.wait_ge(done, j + 1)
                dve.tensor_scalar(ve[:], mv[:, 1:2], LN_EPS, None, ALU.add).then_inc(ready, 1)
                if nm is not None:
                    dve.tensor_scalar(nm[:], mv[:, 0:1], -1.0, None, ALU.mult).then_inc(ready, 1)

            def rank_experts(j, half):
                n = TOP_OPS * j
                ew = rt.ew[:, idx(dve, j), :]
                other, this = ew[:, None, :].to_broadcast([P, E, E]), ew[:, :, None].to_broadcast([P, E, E])
                if half == 0:
                    dve.wait_ge(ex_ready, j + 1)
                    if later(j, 1):
                        dve.wait_ge(places_ready, j)
                    dve.tensor_tensor(equal[:], other, this, ALU.is_equal).then_inc(top_step, 1)
                    dve.tensor_tensor(ahead[:], other, this, ALU.is_gt).then_inc(top_step, 1)
                    dve.wait_ge(top_step, n + 1)
                    dve.tensor_tensor(equal[:], equal[:], earlier[:], ALU.mult).then_inc(top_step, 1)
                    dve.wait_ge(top_step, n + 3)
                    dve.tensor_tensor(ahead[:], ahead[:], equal[:], ALU.add).then_inc(top_step, 1)
                else:
                    dve.wait_ge(top_step, n + 4)
                    dve.tensor_reduce(rank[:], ahead[:], axis=AX.X, op=ALU.add).then_inc(top_step, 1)
                    dve.wait_ge(top_step, n + 5)
                    dve.tensor_tensor(oh2[:], rank[:, None, :].to_broadcast([P, 2, E]),
                                      rt.second[:, :, None].to_broadcast([P, 2, E]), ALU.is_equal).then_inc(top_step, 1)
                    dve.tensor_scalar(oh[:], rank[:], 2.0, None, ALU.is_lt).then_inc(top_step, 1)
                    dve.tensor_copy(rt.rank[:, idx(dve, j), :], rank[:])

            def row_places(j):
                col = idx(dve, j)
                n = PLACE_OPS * j
                dve.wait_ge(pfx_done, j + 1)
                dve.tensor_tensor(row[:], Rk[:, 0:E], ebase[:], ALU.add).then_inc(place_step, 1)
                dve.tensor_tensor(rt.acc[:], rt.acc[:], oh[:], ALU.add).then_inc(place_step, 1)
                dve.wait_ge(place_step, n + 1)
                dve.tensor_tensor(row2[:], oh2[:], row[:, None, :].to_broadcast([P, 2, E]), ALU.mult).then_inc(place_step, 1)
                dve.wait_ge(place_step, n + 3)
                dve.tensor_reduce(pl[:], row2[:], axis=AX.X, op=ALU.add).then_inc(place_step, 1)
                dve.wait_ge(place_step, n + 4)
                dve.tensor_copy(rt.places[:, col, :], pl[:])
                dve.wait_ge(pli_ready, j)
                dve.tensor_copy(pl_i[:], pl[:]).then_inc(places_ready, 1)

            def body(k, s, scan, loads):
                for st in range(ST):
                    if scan:
                        t = ST * k + st
                        if st == 0:
                            dve.wait_ge(uc_in[s], 32 * loads)
                        if st == 0 and first(k):
                            dve.tensor_copy(H[:], ct[s][:, st, :]).then_inc(h_ready, 1)
                        else:
                            dve.wait_ge(pred_full, t)
                            dve.tensor_tensor(m[:], Pb[:, 0:P], ut[s][:, st, :], ALU.mult).then_inc(m_done, 1)
                            dve.wait_ge(m_done, t)
                            dve.wait_ge(g_ready, t)
                            dve.tensor_tensor(H[:], g[:], m[:], ALU.subtract).then_inc(h_ready, 1)
                        dve.wait_ge(h_ready, t + 1)
                        dve.transpose(yT[s][:, :, st, :], H[:]).then_inc(yT_ready, 1)
                    if first(k):
                        if st < C - 1:
                            prepare_wo(st + 1)
                        if st:
                            low_wo(st - 1)
                    if st == 0 and k1(k):
                        low_wo(C - 1)
                        add_lnb()
                    if st == 0 and has(k - 3):
                        j = k - 3
                        tile = rt.x2[:, idx(dve, j), :]
                        dve.wait_ge(bo_ready, 1)
                        dve.wait_ge(x2_ready, j + 1)
                        if has(k - 4):
                            dve.wait_ge(xn3_ready, j)
                        norm_stats(tile, st3, mv3, ve3, nm3, st3_done, ln3_ready, j)
                    if st == 0 and has(k - 5):
                        rank_experts(k - 5, 1)
                    if st == 1 and has(k - 1):
                        j = k - 1
                        dve.wait_ge(y_full, j + 1)
                        if has(k - 2):
                            dve.wait_ge(rs2_ready, j)
                        norm_stats(Yb[:], st2, mv2, ve2, None, st2_done, ln2_ready, j)
                    if st == 2 and has(k - 4):
                        dve.wait_ge(lg_done, k - 3)
                        if has(k - 5):
                            dve.wait_ge(ex_ready, k - 4)
                        dve.tensor_reduce(nmx[:], Lg[:, 0:E], axis=AX.X, op=ALU.max, negate=True).then_inc(nmx_ready, 1)
                    if st == 2 and has(k - 5):
                        row_places(k - 5)
                    if st == 2 and has(k - 1):
                        dve.wait_ge(yH_ready, k)
                        if has(k - 3):
                            dve.wait_ge(wo_done, k - 2)
                        dve.tensor_tensor(yL[1 - s][:], yT[1 - s][:].rearrange("p c t b -> p c (t b)"),
                                          yH[1 - s][:].bitcast(F32), ALU.subtract).then_inc(yL_ready, 1)
                    if st == 3 and has(k - 4):
                        rank_experts(k - 4, 0)
                    if st == 3 and has(k - 2):
                        j = k - 2
                        tile = rt.x2[:, idx(dve, j), :]
                        dve.wait_ge(wo_done, j + 1)
                        dve.wait_ge(xp_ready, 2 * (j + 1))
                        dve.scalar_tensor_tensor(tile, Wb[:], rs2[s][:, 0:1], xt[s][:], ALU.mult, ALU.add).then_inc(x2_ready, 1)

            walk(dve, body)

            n = 0

            def then(*ops):
                nonlocal n
                for op in ops:
                    op.then_inc(plan_step, 1)
                n += len(ops)
                dve.wait_ge(plan_step, n)

            dve.wait_ge(iotas, 2)
            dve.wait_ge(plan_consts, 1 + 2 * E)
            dve.wait_ge(cnt_full, 1)
            then(dve.tensor_copy(tile_no[:], tile_no_i[:]), dve.tensor_copy(step_no[:], step_no_i[:]),
                 dve.tensor_copy(cnt[:], Rk[:, 0:E]))
            then(dve.tensor_scalar(step_no[:], step_no[:], float(P), None, ALU.mult))
            then(dve.tensor_tensor(more[:], cnt[:, :, None].to_broadcast([P, E, TILES]),
                                   step_no[:, None, :].to_broadcast([P, E, TILES]), ALU.is_gt))
            then(dve.tensor_reduce(nt[:], more[:], axis=AX.X, op=ALU.add))
            then(dve.tensor_tensor(upto[:], low[:], nt[:, None, :].to_broadcast([P, E, E]), ALU.mult))
            then(dve.tensor_reduce(te[:], upto[:], axis=AX.X, op=ALU.add))
            then(dve.tensor_tensor(base[:], base[:], cnt[:], ALU.add),
                 dve.tensor_scalar(rt.te_i[:], te[:], 1.0, None, ALU.add),
                 dve.memset(rt.first_row[:, E:E + 1], float(E * rt.region - P * (rt.tiles - rt.spare))))
            then(dve.scalar_tensor_tensor(rt.first_row[:, 0:E], te[:], -float(P), base[:], ALU.mult, ALU.add))
            then(dve.tensor_tensor(jump[:], rt.first_row[:, 1:E + 1], rt.first_row[:, 0:E], ALU.subtract))
            then(dve.tensor_tensor(past[:], tile_no[:, :, None].to_broadcast([P, rt.tiles, E]),
                                   te[:, None, :].to_broadcast([P, rt.tiles, E]), ALU.is_ge))
            then(dve.tensor_tensor(hop[:], past[:], jump[:, None, :].to_broadcast([P, rt.tiles, E]), ALU.mult),
                 dve.tensor_reduce(ef[:], past[:], axis=AX.X, op=ALU.add))
            then(dve.tensor_reduce(rowf[:], hop[:], axis=AX.X, op=ALU.add),
                 dve.tensor_scalar(ef[:], ef[:], float(E - 1), None, ALU.min))
            then(dve.tensor_scalar(rowf[:], rowf[:], rt.first_row[:, 0:1], None, ALU.add),
                 dve.tensor_scalar(s3[:], ef[:], float(ex.SLOTS), -float(ex.SLOTS), ALU.is_ge, ALU.mult),
                 dve.tensor_scalar(s6[:], ef[:], float(2 * ex.SLOTS), -float(ex.SLOTS), ALU.is_ge, ALU.mult))
            then(dve.scalar_tensor_tensor(rowf[:], tile_no[:], float(P), rowf[:], ALU.mult, ALU.add),
                 dve.tensor_tensor(slotf[:], s3[:], s6[:], ALU.add))
            then(dve.tensor_tensor(slotf[:], slotf[:], ef[:], ALU.add),
                 dve.tensor_scalar(ef[:], ef[:], float(ex.PARTS), None, ALU.mult))
            then(dve.tensor_copy(rt.row_i[:], rowf[:]), dve.tensor_copy(rt.part_i[:], ef[:]), dve.tensor_copy(rt.slot_i[:], slotf[:]))


class Experts:
    SLOTS, PARTS = 3, 3

    def __init__(self, nc, sh, gate_up, down, stack):
        F = down.shape[1]
        assert F == sh.D
        self.F = F
        self.sources = gate_up[:, :, 0:F], gate_up[:, :, F:2 * F], down
        self.low = stack.enter_context(nc.sbuf_tensor("w_low", [P, self.SLOTS, self.PARTS, sh.C, F], F32R))
        self.w_in = [stack.enter_context(nc.semaphore(f"expert_w_in{s}")) for s in range(self.SLOTS)]
        self.w_next = [stack.enter_context(nc.semaphore(f"expert_w_next{s}")) for s in range(self.PARTS)]

    def load(self, eng, e, part):
        s = e % self.SLOTS
        eng.dma_start(self.low[:, s, part].bitcast(F32), self.sources[part][e].rearrange("(c p) f -> p c f", p=P)
                      ).then_inc(self.w_in[s] if e < self.SLOTS else self.w_next[part], 16)


def experts(nc, sh, ident, ex, rt, out):
    D, C, E, F, SLOTS, PARTS = sh.D, sh.C, sh.E, ex.F, ex.SLOTS, ex.PARTS
    TOKEN_TILES, ST = sh.N // P, P // sh.B
    GROUP = 4
    POOLS = GROUP
    EPS = 1e-9
    GATE, UP, DOWN = range(PARTS)
    TILES = rt.tiles
    assert TILES % 2 == 1
    with ExitStack() as stack:
        def sb(name, shape, dt=F32):
            return stack.enter_context(nc.sbuf_tensor(name, shape, dt))

        def sem(name):
            return stack.enter_context(nc.semaphore(name))

        def psum(name):
            return stack.enter_context(nc.psum_tensor(name, [P, 512], F32))

        xt = [sb(f"f_xt{s}", [P, D]) for s in range(2)]
        zero = sb("f_zero", [P, F])
        high = sb("w_high", [P, SLOTS, PARTS, C, F], F32R)
        xH = [sb(f"f_xH{s}", [P, C, P], F32R) for s in range(2)]
        xL = [sb(f"f_xL{s}", [P, C, P], F32R) for s in range(2)]
        sg = sb("sg", [P, F])
        h = sb("f_h", [P, F])
        hH, hL = sb("f_hH", [P, C, P], F32R), sb("f_hL", [P, C, P], F32R)
        yt = [sb(f"f_yt{s}", [P, D]) for s in range(2)]
        hot, prod = (sb(n, [P, 2 * TOKEN_TILES, E]) for n in ("c_hot", "c_prod"))
        rs, total = sb("c_rs", [P, TOKEN_TILES]), sb("c_total", [P, TOKEN_TILES])
        part_w, swapped, kept = (sb(n, [P, TOKEN_TILES, 2]) for n in ("c_part", "c_swapped", "c_kept"))
        begin, place_r = sb("c_begin", [P, TOKEN_TILES, 2]), sb("c_place_r", [P, TOKEN_TILES, 2])
        order, below = sb("c_order", [P, TOKEN_TILES]), sb("c_below", [P, TOKEN_TILES])
        place = [sb(f"c_place{i}", [P, TOKEN_TILES], I32) for i in range(2)]
        weight = [sb(f"c_weight{i}", [P, TOKEN_TILES]) for i in range(2)]
        stored = [sb(f"c_stored{s}", [P, 2], I32) for s in range(2)]
        y = [t[:, (E - 1 - i) % SLOTS, part, c].bitcast(F32) for t in (high, ex.low) for i in (2, 1)
             for part in range(PARTS) for c in range(C)][0:2 * TOKEN_TILES]

        G, U, Dn, TX, TH = (psum(n) for n in ("f_G", "f_U", "f_Dn", "f_TX", "f_TH"))

        w_parts, w_high, tile_done = sem("w_parts"), sem("w_high_ready"), sem("tile_done")
        zero_set = sem("f_zero_set")
        x_in = [sem(f"f_x_in{s}") for s in range(2)]
        y_out = [sem(f"f_y_out{s}") for s in range(2)]
        x_full, xH_ready, xL_ready = sem("f_x_full"), sem("f_xH_ready"), sem("f_xL_ready")
        g_full, sg_ready, u_full, h_ready = sem("f_g_full"), sem("sg_ready"), sem("f_u_full"), sem("f_h_ready")
        h_full, hH_ready, hL_ready, y_ready = sem("f_h_full"), sem("f_hH_ready"), sem("f_hL_ready"), sem("f_y_ready")
        place_step, w_step, places_made, weights_made = sem("c_place_step"), sem("c_w_step"), sem("c_places_made"), sem("c_weights_made")
        first_in = sem("c_first_in")
        second_in = [sem(f"c_second_in{i}") for i in range(TOKEN_TILES // GROUP)]
        weighted, first_added, pool_added, dve_added = sem("c_weighted"), sem("c_first_added"), sem("c_pool_added"), sem("c_dve_added")
        pool_out, dve_out = sem("c_pool_out"), sem("c_dve_out")
        block = stack.enter_context(nc.Block())
        out_tiles = out.rearrange("b (k t) d -> k t b d", t=ST)

        def entry(eng, tab, t, lo, hi):
            return eng.value_load(tab[0:1, bass.ds(t if isinstance(t, int) else eng.snap(t), 1)], min_val=lo, max_val=hi)

        @block.sync
        def _(sp):
            last_row = rt.rows - P

            def load(t, s):
                r = entry(sp, rt.row_i, t, 0, last_row)
                sp.dma_start(xt[s][:], rt.x_rows[bass.ds(r, P), :]).then_inc(x_in[s], 16)

            def store(t, s):
                rows = bass.ds(t * P if isinstance(t, int) else sp.snap(t * P), P)
                sp.wait_ge(y_ready, t + 1)
                sp.dma_start(rt.y_rows[rows, :], yt[s][:]).then_inc(y_out[s], 16)

            def body(t, s, more):
                if more:
                    sp.wait_ge(x_full, t + 1)
                    load(t + 2, s)
                if later(t, 1):
                    store(t - 1, 1 - s)

            load(0, 0)
            load(1, 1)
            body(0, 0, True)
            with sp.Fori(0, TILES // 2 - 1) as i:
                body(2 * i + 1, 1, True)
                body(2 * i + 2, 0, True)
            body(TILES - 2, 1, False)
            body(TILES - 1, 0, False)
            store(TILES - 1, 0)
            for s in range(2):
                sp.wait_ge(y_out[s], 16 * ((TILES + 1 - s) // 2))
            for k in range(POOLS, TOKEN_TILES):
                sp.wait_ge(dve_added, k - POOLS + 1)
                sp.dma_start(out_tiles[k], rt.x2[:, k, :]).then_inc(dve_out, 16)
            sp.wait_ge(dve_out, 16 * (TOKEN_TILES - POOLS))

        @block.gpsimd
        def _(pool):
            def split_low(e, part):
                low = ex.low[:, e % SLOTS, part]
                pool.wait_ge(w_high, PARTS * e + part + 1)
                pool.tensor_tensor(low, low.bitcast(F32), high[:, e % SLOTS, part].bitcast(F32), ALU.subtract).then_inc(w_parts, 1)

            pool.memset(zero[:], 0.0).then_inc(zero_set, 1)
            pool.wait_ge(zero_set, 1)
            pool.wait_ge(w_parts, PARTS)
            for e in range(1, E):
                if e < SLOTS:
                    pool.wait_ge(ex.w_in[e], 16 * PARTS)
                else:
                    n = pool.value_load(rt.te_i[0:1, e - SLOTS:e - SLOTS + 1], min_val=1, max_val=TILES + 1)
                    pool.wait_ge(zero_set, 1)
                    pool.wait_ge(tile_done, n)
                    for part in range(PARTS):
                        ex.load(pool, e, part)
                for part in range(PARTS):
                    if e >= SLOTS:
                        pool.wait_ge(ex.w_next[part], 16 * (e - SLOTS + 1))
                    pool.tensor_tensor(high[:, e % SLOTS, part], ex.low[:, e % SLOTS, part].bitcast(F32),
                                       zero[:, None, :].to_broadcast([P, C, F]), ALU.add).then_inc(w_high, 1)
                    split_low(e, part)

            pool.wait_ge(places_made, 4)
            for i in range(2):
                counts = [pool.value_load(stored[s][0:1, i:i + 1], min_val=16, max_val=16 * TILES) for s in range(2)]
                pool.wait_ge(places_made, 4)
                for s in range(2):
                    pool.wait_ge(y_out[s], counts[s])
                for k in range(TOKEN_TILES):
                    pool.indirect_dma_start(out=y[i * TOKEN_TILES + k], out_offset=None, in_=rt.y_rows,
                                            in_offset=bass.IndirectOffsetOnAxis(ap=place[i][:, k:k + 1], axis=0)
                                            ).then_inc(second_in[k // GROUP] if i else first_in, 16)
                pool.wait_ge(weights_made, 2)
                for k in range(POOLS if i else TOKEN_TILES):
                    n = i * TOKEN_TILES + k
                    if i == 0:
                        pool.wait_ge(first_in, 16 * TOKEN_TILES)
                    elif k % GROUP == 0:
                        pool.wait_ge(second_in[k // GROUP], 16 * GROUP)
                    pool.tensor_tensor(y[n], y[n], weight[i][:, k:k + 1].to_broadcast([P, D]), ALU.mult).then_inc(weighted, 1)
                    pool.wait_ge(weighted, n + 1)
                    if i:
                        pool.wait_ge(first_added, k + 1)
                    x2 = rt.x2[:, k, :]
                    pool.tensor_tensor(x2, x2, y[n], ALU.add).then_inc(pool_added if i else first_added, 1)

        @block.tensor
        def _(pe):
            def turn_x(t, s, n):
                pe.wait_ge(x_in[s], 16 * n)
                if later(t, 1):
                    pe.wait_ge(xL_ready, t)
                for c in range(C):
                    last = pe.transpose(TX[:, c * P:(c + 1) * P], xt[s][:, c * P:(c + 1) * P], ident[:])
                last.then_inc(x_full, 1)

            def turn_h(t):
                pe.wait_ge(h_ready, t + 1)
                if later(t, 1):
                    pe.wait_ge(hL_ready, t)
                for c in range(C):
                    last = pe.transpose(TH[:, c * P:(c + 1) * P], h[:, c * P:(c + 1) * P], ident[:])
                last.then_inc(h_full, 1)

            def product(bank, aH, aL, slot, part):
                for c in range(C):
                    pe.matmul(bank[:], aH[:, c, :], high[:, slot, part, c, :], start=(c == 0), stop=False)
                    pe.matmul(bank[:], aH[:, c, :], ex.low[:, slot, part, c, :], start=False, stop=False)
                    last = pe.matmul(bank[:], aL[:, c, :], high[:, slot, part, c, :], start=False, stop=(c == C - 1))
                return last

            def down(t):
                slot = entry(pe, rt.slot_i, t, 0, SLOTS - 1)
                parts = entry(pe, rt.part_i, t, 0, PARTS * (E - 1))
                pe.wait_ge(w_parts, pe.snap(parts + PARTS))
                pe.wait_ge(hL_ready, t + 1)
                if later(t, 1):
                    pe.wait_ge(y_ready, t)
                product(Dn, hH, hL, slot, DOWN).then_inc(tile_done, 1)

            def body(t, s, n):
                slot = entry(pe, rt.slot_i, t, 0, SLOTS - 1)
                parts = entry(pe, rt.part_i, t, 0, PARTS * (E - 1))
                pe.wait_ge(xL_ready, t + 1)
                pe.wait_ge(w_parts, pe.snap(parts + GATE + 1))
                if later(t, 1):
                    pe.wait_ge(sg_ready, t)
                product(G, xH[s], xL[s], slot, GATE).then_inc(g_full, 1)
                if later(t, 1):
                    turn_h(t - 1)
                if not later(t, 1):
                    turn_x(t + 1, 1 - s, n)
                pe.wait_ge(w_parts, pe.snap(parts + UP + 1))
                product(U, xH[s], xL[s], slot, UP).then_inc(u_full, 1)
                if later(t, 1) and n is not None:
                    turn_x(t + 1, 1 - s, n)
                if later(t, 1):
                    down(t - 1)

            pe.sem_inc(tile_done, 1)
            turn_x(0, 0, 1)
            body(0, 0, 1)
            with pe.Fori(0, TILES // 2 - 1) as i:
                body(2 * i + 1, 1, i + 2)
                body(2 * i + 2, 0, i + 2)
            body(TILES - 2, 1, (TILES + 1) // 2)
            body(TILES - 1, 0, None)
            turn_h(TILES - 1)
            down(TILES - 1)

        @block.scalar
        def _(act):
            def take_x(t, s):
                act.wait_ge(x_full, t + 1)
                if later(t, 2):
                    act.wait_ge(u_full, t - 1)
                act.copy(xH[s][:], TX[:].rearrange("p (c i) -> p c i", c=C)).then_inc(xH_ready, 1)

            def take_h(t):
                act.wait_ge(h_full, t + 1)
                act.wait_ge(tile_done, t + 1)
                act.copy(hH[:], TH[:].rearrange("p (c i) -> p c i", c=C)).then_inc(hH_ready, 1)

            def body(t, s, more):
                act.wait_ge(g_full, t + 1)
                act.wait_ge(h_ready, t)
                act.activation(sg[:], G[:], ACT.Silu).then_inc(sg_ready, 1)
                if later(t, 1):
                    take_h(t - 1)
                if more:
                    take_x(t + 1, 1 - s)

            def high_first(part):
                act.copy(high[:, 0, part], ex.low[:, 0, part].bitcast(F32)).then_inc(w_high, 1)

            act.wait_ge(ex.w_in[0], 16 * PARTS)
            high_first(GATE)
            take_x(0, 0)
            high_first(UP)
            high_first(DOWN)
            body(0, 0, True)
            with act.Fori(0, TILES // 2 - 1) as i:
                body(2 * i + 1, 1, True)
                body(2 * i + 2, 0, True)
            body(TILES - 2, 1, True)
            body(TILES - 1, 0, False)
            take_h(TILES - 1)
            for k in range(POOLS):
                act.wait_ge(pool_added, k + 1)
                act.dma_start(out_tiles[k], rt.x2[:, k, :]).then_inc(pool_out, 16)
            act.wait_ge(pool_out, 16 * POOLS)

        @block.vector
        def _(dve):
            def low_first(part):
                raw = ex.low[:, 0, part]
                dve.wait_ge(w_high, part + 1)
                dve.tensor_tensor(raw, raw.bitcast(F32), high[:, 0, part].bitcast(F32), ALU.subtract).then_inc(w_parts, 1)

            def low_x(t, s):
                dve.wait_ge(xH_ready, t + 1)
                if later(t, 2):
                    dve.wait_ge(u_full, t - 1)
                dve.tensor_tensor(xL[s][:], TX[:].rearrange("p (c i) -> p c i", c=C), xH[s][:].bitcast(F32),
                                  ALU.subtract).then_inc(xL_ready, 1)

            def low_h(t):
                dve.wait_ge(hH_ready, t + 1)
                dve.wait_ge(tile_done, t + 1)
                dve.tensor_tensor(hL[:], TH[:].rearrange("p (c i) -> p c i", c=C), hH[:].bitcast(F32),
                                  ALU.subtract).then_inc(hL_ready, 1)

            def gate(t):
                dve.wait_ge(u_full, t + 1)
                dve.wait_ge(sg_ready, t + 1)
                if later(t, 1):
                    dve.wait_ge(h_full, t)
                dve.tensor_tensor(h[:], U[:], sg[:], ALU.mult).then_inc(h_ready, 1)

            def take_y(t, s, stored):
                dve.wait_ge(tile_done, t + 2)
                if later(t, 2):
                    dve.wait_ge(y_out[s], 16 * stored)
                dve.tensor_copy(yt[s][:], Dn[:]).then_inc(y_ready, 1)

            def body(t, s, stored, more):
                if later(t, 1):
                    low_h(t - 1)
                else:
                    low_x(t + 1, 1 - s)
                gate(t)
                if later(t, 1) and more:
                    low_x(t + 1, 1 - s)
                if later(t, 1):
                    take_y(t - 1, 1 - s, stored)

            def token_places():
                dve.tensor_tensor(hot[:].rearrange("p (k w) e -> p k w e", w=2),
                                  rt.rank[:, :, None, :].to_broadcast([P, TOKEN_TILES, 2, E]),
                                  rt.second[:, None, :, None].to_broadcast([P, TOKEN_TILES, 2, E]), ALU.is_equal).then_inc(place_step, 1)
                dve.wait_ge(place_step, 1)
                dve.tensor_tensor(prod[:], hot[:], rt.first_row[:, None, 0:E].to_broadcast([P, 2 * TOKEN_TILES, E]),
                                  ALU.mult).then_inc(place_step, 1)
                dve.wait_ge(place_step, 2)
                dve.tensor_reduce(begin[:].rearrange("p k w -> p (k w)"), prod[:], axis=AX.X, op=ALU.add).then_inc(place_step, 1)
                dve.wait_ge(place_step, 3)
                dve.tensor_tensor(place_r[:], rt.places[:], begin[:], ALU.subtract).then_inc(place_step, 1)
                dve.wait_ge(place_step, 4)
                dve.tensor_reduce(order[:], place_r[:], axis=AX.X, op=ALU.min).then_inc(place_step, 1)
                dve.tensor_reduce(below[:], place_r[:], axis=AX.X, op=ALU.max).then_inc(place_step, 1)
                dve.wait_ge(place_step, 6)
                dve.tensor_copy(place[0][:], order[:]).then_inc(places_made, 1)
                dve.tensor_copy(place[1][:], below[:]).then_inc(places_made, 1)
                dve.tensor_tensor(kept[:], place_r[:], order[:, :, None].to_broadcast([P, TOKEN_TILES, 2]),
                                  ALU.is_equal).then_inc(w_step, 1)
                dve.tensor_tensor(swapped[:], place_r[:], below[:, :, None].to_broadcast([P, TOKEN_TILES, 2]),
                                  ALU.is_equal).then_inc(w_step, 1)

            def stored_counts():
                last_two = rt.te_i[:, E - 2:E]
                dve.tensor_scalar(stored[0][:], last_two, 1, 4, ALU.logical_shift_right, ALU.logical_shift_left).then_inc(places_made, 1)
                dve.tensor_scalar(stored[1][:], last_two, -1, None, ALU.add).then_inc(place_step, 1)
                dve.wait_ge(place_step, 7)
                dve.tensor_scalar(stored[1][:], stored[1][:], 1, 4, ALU.logical_shift_right, ALU.logical_shift_left).then_inc(places_made, 1)

            def rank_weights():
                dve.wait_ge(place_step, 7)
                dve.tensor_tensor(prod[:].rearrange("p (k w) e -> p k w e", w=2), hot[:].rearrange("p (k w) e -> p k w e", w=2),
                                  rt.ew[:, :, None, :].to_broadcast([P, TOKEN_TILES, 2, E]), ALU.mult).then_inc(w_step, 1)
                dve.tensor_reduce(total[:], rt.ew[:], axis=AX.X, op=ALU.add).then_inc(w_step, 1)
                dve.wait_ge(w_step, 4)
                dve.tensor_reduce(part_w[:].rearrange("p k w -> p (k w)"), prod[:], axis=AX.X, op=ALU.add).then_inc(w_step, 1)
                dve.reciprocal(rs[:], total[:]).then_inc(w_step, 1)
                dve.wait_ge(w_step, 6)
                dve.tensor_tensor(part_w[:], part_w[:], rs[:, :, None].to_broadcast([P, TOKEN_TILES, 2]), ALU.mult).then_inc(w_step, 1)

            def token_weights():
                n = 7
                dve.wait_ge(w_step, n)
                for _ in range(2):
                    dve.tensor_reduce(total[:], part_w[:], axis=AX.X, op=ALU.add).then_inc(w_step, 1)
                    dve.wait_ge(w_step, n + 1)
                    dve.tensor_scalar(total[:], total[:], EPS, None, ALU.add).then_inc(w_step, 1)
                    dve.wait_ge(w_step, n + 2)
                    dve.reciprocal(rs[:], total[:]).then_inc(w_step, 1)
                    dve.wait_ge(w_step, n + 3)
                    dve.tensor_tensor(part_w[:], part_w[:], rs[:, :, None].to_broadcast([P, TOKEN_TILES, 2]), ALU.mult).then_inc(w_step, 1)
                    n += 4
                    dve.wait_ge(w_step, n)
                dve.tensor_tensor(kept[:], kept[:], part_w[:], ALU.mult).then_inc(w_step, 1)
                dve.tensor_tensor(swapped[:], swapped[:], part_w[:], ALU.mult).then_inc(w_step, 1)
                dve.wait_ge(w_step, n + 2)
                dve.tensor_reduce(weight[0][:], kept[:], axis=AX.X, op=ALU.add).then_inc(weights_made, 1)
                dve.tensor_reduce(weight[1][:], swapped[:], axis=AX.X, op=ALU.add).then_inc(weights_made, 1)

            low_first(GATE)
            low_x(0, 0)
            low_first(UP)
            low_first(DOWN)
            body(0, 0, 0, True)
            body(1, 1, 0, True)
            token_places()
            body(2, 0, 0, True)
            stored_counts()
            rank_weights()
            body(3, 1, 1, True)
            token_weights()
            body(4, 0, 1, True)
            with dve.Fori(2, TILES // 2 - 1) as i:
                body(2 * i + 1, 1, i, True)
                body(2 * i + 2, 0, i, True)
            body(TILES - 2, 1, TILES // 2 - 1, True)
            body(TILES - 1, 0, TILES // 2 - 1, False)
            low_h(TILES - 1)
            take_y(TILES - 1, 0, TILES // 2)
            dve.wait_ge(weights_made, 2)
            for k in range(POOLS, TOKEN_TILES):
                x2 = rt.x2[:, k, :]
                if k % GROUP == 0:
                    dve.wait_ge(second_in[k // GROUP], 16 * GROUP)
                dve.wait_ge(first_added, k + 1)
                dve.scalar_tensor_tensor(x2, y[TOKEN_TILES + k], weight[1][:, k:k + 1], x2, ALU.mult, ALU.add).then_inc(dve_added, 1)


def program(nc, x, ctx, w_sim, b_sim, W_qv, b_qv, decay, Wr, br, Wg, bg, Wo, bo, ln_w, ln_b, gate_w, gate_up, down, out):
    sh = Shapes(x, ctx, gate_w)
    C = sh.C
    x1 = nc.dram_tensor("x1", (sh.PAIRS, P, sh.D), F32, kind="Internal").ap()
    u_d = nc.dram_tensor("u", (C * sh.B, sh.L, P), F32, kind="Internal").ap()
    c_d = nc.dram_tensor("c", (C * sh.B, sh.L, P), F32, kind="Internal").ap()
    with ExitStack() as stack:
        ident = stack.enter_context(nc.sbuf_tensor("ident", [P, P], F32))
        make_identity(nc, ident)
        x2 = stack.enter_context(nc.sbuf_tensor("x2", [P, sh.N // P, sh.D], F32))
        ahead = GatesAhead(nc, sh, x1, Wg, x2, stack)
        cross_attention(nc, sh, ident, x.rearrange("(p b) l d -> p (b l) d", b=2), ctx.rearrange("(p b) j d -> p b j d", b=2),
                        w_sim, b_sim, W_qv, b_qv, x1, x2, ahead)
        rt = Routing(nc, sh, x2, stack)
        ex = Experts(nc, sh, gate_up, down, stack)
        with ExitStack() as inner:
            rw = RecurrenceWeights(nc, sh, Wr, Wo, decay, ln_w, ln_b, bo, gate_w, inner)
            recurrence_gates(nc, sh, ident, x1, bg, br, decay, u_d, c_d, rw, rt, ahead)
            recurrence(nc, sh, ident, x1, u_d, c_d, rw, rt, ex)
        experts(nc, sh, ident, ex, rt, out)


_INS = ["x", "ctx_1024", "L0_xattn_w_sim", "L0_xattn_b_sim", "L0_xattn_W_qv", "L0_xattn_b_qv",
        "L0_attn_decay", "L0_attn_Wr", "L0_attn_br", "L0_attn_Wg", "L0_attn_bg", "L0_attn_Wo", "L0_attn_bo",
        "L0_attn_ln_w", "L0_attn_ln_b", "L0_ffn_gate_w", "L0_ffn_gate_up_proj", "L0_ffn_down_proj"]


def kernel(**inputs):
    import numpy as _np
    import concourse.bacc as _bacc
    from concourse.bass_utils import run_bass_kernel_spmd as _run

    nc = _bacc.Bacc("TRN2", target_bir_lowering=False, num_devices=1)
    arrays, args = {}, []
    for name in _INS:
        a = _np.ascontiguousarray(inputs[name])
        arrays[f"in_{name}_dram"] = a
        args.append(nc.dram_tensor(f"in_{name}_dram", a.shape, mybir.dt.from_np(a.dtype), kind="ExternalInput").ap())
    out = nc.dram_tensor("out_0_dram", inputs["x"].shape, F32, kind="ExternalOutput").ap()
    program(nc, *args, out)
    r = _run(nc, [arrays], core_ids=[0])
    return r.results[0]["out_0_dram"]
```
